# Optimizing a Trainium2 kernel written in Bass

```python
import numpy as np
import jax
import jax.numpy as jnp

def _softmax(x, axis=-1):
    return jax.nn.softmax(x, axis=axis)

def _gelu(x):
    return jax.nn.gelu(x, approximate=True)

def _silu(x):
    return jax.nn.silu(x)

def _sigmoid(x):
    return jax.nn.sigmoid(x)

def _layernorm(x, axis=-1, eps=1e-05):
    m = jnp.mean(x, axis=axis, keepdims=True)
    v = jnp.var(x, axis=axis, keepdims=True)
    return (x - m) / jnp.sqrt(v + eps)

def _scatter_add(tgt, idx, src, axis=0):
    return tgt.at[idx].add(src)

def _segment_sum(src, seg, n):
    return jax.ops.segment_sum(src, seg, n)
kernel_name = 'mk_flamingo_gated_d2_seqx_r4_b43724'

def setup_inputs(seed: int=0):
    np.random.seed(seed)
    _w = jnp.asarray

    def _rec_inputs():
        import jax
        import jax.numpy as jnp
        _rk = jax.random.key(seed)
        x = -0.0002928 + 1 * jax.random.normal(jax.random.fold_in(_rk, 1), (32, 256, 256), jnp.float32)
        _lenS = 256 - jax.random.randint(jax.random.fold_in(_rk, 7), (32,), 0, max(1, 256 // 4) + 1, jnp.int32)
        _lenS2 = 256 - jax.random.randint(jax.random.fold_in(_rk, 8), (32,), 0, max(1, 256 // 4) + 1, jnp.int32)
        _ctx_1024P = jax.random.normal(jax.random.fold_in(_rk, 11), (32, 16, 256), jnp.float32)
        _ctx_1024c = jax.random.dirichlet(jax.random.fold_in(_rk, 511), 0.3 * jnp.ones((16,), jnp.float32), (32, 256))
        _ctx_1024t = jnp.einsum('bsk,bkd->bsd', _ctx_1024c, _ctx_1024P)
        _ctx_1024t = _ctx_1024t * jax.lax.rsqrt(jnp.mean(jnp.square(_ctx_1024t)) + 1e-12) * 0.953939
        ctx_1024 = -1.39393e-06 + 0.999914 * (_ctx_1024t + 0.3 * jax.random.normal(jax.random.fold_in(_rk, 611), (32, 256, 256), jnp.float32))
        _g = jax.random.normal(jax.random.fold_in(_rk, 9001), (2, 2), jnp.float32)
        _g = jnp.sign(_g) * jnp.maximum(jnp.abs(_g), 1.0) + (_g == 0) * 1.0
        g_xattn = _g[0]
        g_ffn = _g[1]
        return (x, ctx_1024, g_xattn, g_ffn)
    x, ctx_1024, g_xattn, g_ffn = _rec_inputs()

    def _L0_xattn_setup():
        import jax, jax.numpy as jnp
        import numpy as np
        D_MODEL = 256
        HEADS = 16
        DK = D_MODEL // HEADS
        B, S = (1, 1024)
        key = jax.random.key(seed)
        ks = jax.random.split(key, 11)
        sd = 1.0 / np.sqrt(D_MODEL)
        return {'q': jax.random.normal(ks[0], (B, S, D_MODEL), jnp.float32), 'k': jax.random.normal(ks[1], (B, S, D_MODEL), jnp.float32), 'v': jax.random.normal(ks[2], (B, S, D_MODEL), jnp.float32), 'Wq': jax.random.uniform(ks[3], (D_MODEL, D_MODEL), jnp.float32, -sd, sd), 'bq': jax.random.uniform(ks[4], (D_MODEL,), jnp.float32, -sd, sd), 'Wk': jax.random.uniform(ks[5], (D_MODEL, DK), jnp.float32, -sd, sd), 'bk': jax.random.uniform(ks[6], (DK,), jnp.float32, -sd, sd), 'Wv': jax.random.uniform(ks[7], (D_MODEL, DK), jnp.float32, -sd, sd), 'bv': jax.random.uniform(ks[8], (DK,), jnp.float32, -sd, sd), 'Wo': jax.random.uniform(ks[9], (D_MODEL, D_MODEL), jnp.float32, -sd, sd), 'bo': jax.random.uniform(ks[10], (D_MODEL,), jnp.float32, -sd, sd)}
    _L0_xattn_all = _L0_xattn_setup()
    _L0_xattn_in = {k: v for k, v in _L0_xattn_all.items() if k in ('Wq', 'bq', 'Wk', 'bk', 'Wv', 'bv', 'Wo', 'bo')}
    del _L0_xattn_all

    def _L0_ffn_setup():
        import jax, jax.numpy as jnp
        import numpy as np
        EPS_NORM = 1e-08
        EPS_Q = 1e-05

        def rmsnorm(x, w):
            v = jnp.mean(jnp.square(x.astype(jnp.float32)), axis=-1, keepdims=True)
            x_hat = x * jax.lax.rsqrt(v + EPS_NORM)
            return (x_hat * w).astype(x.dtype)

        def activation_quant(x):
            scale = 127.0 / jnp.clip(jnp.max(jnp.abs(x), axis=-1, keepdims=True), EPS_Q, None)
            return jnp.clip(jnp.round(x * scale), -128, 127) / scale

        def weight_quant(w):
            scale = 1.0 / jnp.clip(jnp.mean(jnp.abs(w)), EPS_Q, None)
            return jnp.clip(jnp.round(w * scale), -1, 1) / scale

        def bitlinear(x, norm_w, w):
            x_norm = rmsnorm(x, norm_w)
            x_q = x_norm + jax.lax.stop_gradient(activation_quant(x_norm) - x_norm)
            w_q = w + jax.lax.stop_gradient(weight_quant(w) - w)
            return jnp.einsum('bsd,hd->bsh', x_q, w_q)
        key = jax.random.key(seed)
        k1, k2, k3 = jax.random.split(key, 3)
        dim, hidden = (256, 1024)
        return {'x': jax.random.normal(k1, (4, 512, dim), dtype=jnp.float32), 'norm1_w': jnp.ones((dim,), jnp.float32), 'w1': jax.random.normal(k2, (hidden, dim), jnp.float32) * 0.02, 'act_scale': jnp.ones((1,), jnp.float32), 'act_bias': jnp.zeros((1,), jnp.float32), 'norm2_w': jnp.ones((hidden,), jnp.float32), 'w2': jax.random.normal(k3, (dim, hidden), jnp.float32) * 0.02}
    _L0_ffn_all = _L0_ffn_setup()
    _L0_ffn_in = {k: v for k, v in _L0_ffn_all.items() if k in ('norm1_w', 'w1', 'act_scale', 'act_bias', 'norm2_w', 'w2')}
    del _L0_ffn_all

    def _L1_xattn_setup():
        import jax, jax.numpy as jnp
        import numpy as np
        N_HEAD = 16
        key = jax.random.key(seed)
        ks = jax.random.split(key, 5)
        b, l, d = (4, 512, 256)
        dh = d // N_HEAD
        return {'q': jax.random.normal(ks[0], (b, l, d), dtype=jnp.float32), 'kv': jax.random.normal(ks[1], (b, l, d), dtype=jnp.float32), 'Wq': jax.random.normal(ks[2], (d, d), dtype=jnp.float32) * 0.02, 'Wkv': jax.random.normal(ks[3], (2 * dh, d), dtype=jnp.float32) * 0.02, 'Wc': jax.random.normal(ks[4], (d, d), dtype=jnp.float32) * 0.02}
    _L1_xattn_all = _L1_xattn_setup()
    _L1_xattn_in = {k: v for k, v in _L1_xattn_all.items() if k in ('Wq', 'Wkv', 'Wc')}
    del _L1_xattn_all

    def _L1_ffn_setup():
        import jax, jax.numpy as jnp
        import numpy as np
        DIM = 256
        HEADS = 16
        HD = DIM // HEADS
        M = 64
        E = 4
        K = 2
        HID = 512
        MID = 512
        LB = 0.01
        EPS = 1.1920929e-07

        def _rms(x, w):
            return x * jax.lax.rsqrt(jnp.mean(x * x, axis=-1, keepdims=True) + EPS) * w

        def _gelu(x):
            return jax.nn.gelu(x, approximate=False)
        key = jax.random.key(seed)
        ks = jax.random.split(key, 20)
        d = DIM
        w = lambda k, s: jax.random.normal(k, s, jnp.float32) * 0.02
        return {'x': jax.random.normal(ks[0], (4, 256, d), jnp.float32), 'n1_w': jnp.ones((d,), jnp.float32), 'n2_w': jnp.ones((d,), jnp.float32), 'wq': w(ks[1], (d, d)), 'wk': w(ks[2], (d, d)), 'wv': w(ks[3], (d, d)), 'wo': w(ks[4], (d, d)), 'qn_w': jnp.ones((HD,), jnp.float32), 'kn_w': jnp.ones((HD,), jnp.float32), 'gate_w': w(ks[5], (E, d)), 'e0_up': w(ks[6], (HID, d)), 'e0_down': w(ks[7], (d, HID)), 'e1_w1': w(ks[8], (HID, d)), 'e1_w2': w(ks[9], (HID, d)), 'e1_down': w(ks[10], (d, HID)), 'e2_l1': w(ks[11], (MID, d)), 'e2_l2': w(ks[12], (HID, MID)), 'e2_l3': w(ks[13], (MID, HID)), 'e2_l4': w(ks[14], (d, MID)), 'e3_down': w(ks[15], (d, d)), 'e3_up': w(ks[16], (HID, d)), 'e3_out': w(ks[17], (d, HID))}
    _L1_ffn_all = _L1_ffn_setup()
    _L1_ffn_in = {k: v for k, v in _L1_ffn_all.items() if k in ('n1_w', 'n2_w', 'wq', 'wk', 'wv', 'wo', 'qn_w', 'kn_w', 'gate_w', 'e0_up', 'e0_down', 'e1_w1', 'e1_w2', 'e1_down', 'e2_l1', 'e2_l2', 'e2_l3', 'e2_l4', 'e3_down', 'e3_up', 'e3_out')}
    del _L1_ffn_all
    return {'x': x, 'ctx_1024': ctx_1024, 'g_xattn': g_xattn, 'g_ffn': g_ffn, 'L0_xattn_Wq': _L0_xattn_in['Wq'], 'L0_xattn_bq': _L0_xattn_in['bq'], 'L0_xattn_Wk': _L0_xattn_in['Wk'], 'L0_xattn_bk': _L0_xattn_in['bk'], 'L0_xattn_Wv': _L0_xattn_in['Wv'], 'L0_xattn_bv': _L0_xattn_in['bv'], 'L0_xattn_Wo': _L0_xattn_in['Wo'], 'L0_xattn_bo': _L0_xattn_in['bo'], 'L0_ffn_norm1_w': _L0_ffn_in['norm1_w'], 'L0_ffn_w1': _L0_ffn_in['w1'], 'L0_ffn_act_scale': _L0_ffn_in['act_scale'], 'L0_ffn_act_bias': _L0_ffn_in['act_bias'], 'L0_ffn_norm2_w': _L0_ffn_in['norm2_w'], 'L0_ffn_w2': _L0_ffn_in['w2'], 'L1_xattn_Wq': _L1_xattn_in['Wq'], 'L1_xattn_Wkv': _L1_xattn_in['Wkv'], 'L1_xattn_Wc': _L1_xattn_in['Wc'], 'L1_ffn_n1_w': _L1_ffn_in['n1_w'], 'L1_ffn_n2_w': _L1_ffn_in['n2_w'], 'L1_ffn_wq': _L1_ffn_in['wq'], 'L1_ffn_wk': _L1_ffn_in['wk'], 'L1_ffn_wv': _L1_ffn_in['wv'], 'L1_ffn_wo': _L1_ffn_in['wo'], 'L1_ffn_qn_w': _L1_ffn_in['qn_w'], 'L1_ffn_kn_w': _L1_ffn_in['kn_w'], 'L1_ffn_gate_w': _L1_ffn_in['gate_w'], 'L1_ffn_e0_up': _L1_ffn_in['e0_up'], 'L1_ffn_e0_down': _L1_ffn_in['e0_down'], 'L1_ffn_e1_w1': _L1_ffn_in['e1_w1'], 'L1_ffn_e1_w2': _L1_ffn_in['e1_w2'], 'L1_ffn_e1_down': _L1_ffn_in['e1_down'], 'L1_ffn_e2_l1': _L1_ffn_in['e2_l1'], 'L1_ffn_e2_l2': _L1_ffn_in['e2_l2'], 'L1_ffn_e2_l3': _L1_ffn_in['e2_l3'], 'L1_ffn_e2_l4': _L1_ffn_in['e2_l4'], 'L1_ffn_e3_down': _L1_ffn_in['e3_down'], 'L1_ffn_e3_up': _L1_ffn_in['e3_up'], 'L1_ffn_e3_out': _L1_ffn_in['e3_out']}

def reference(x, ctx_1024, g_xattn, g_ffn, L0_xattn_Wq, L0_xattn_bq, L0_xattn_Wk, L0_xattn_bk, L0_xattn_Wv, L0_xattn_bv, L0_xattn_Wo, L0_xattn_bo, L0_ffn_norm1_w, L0_ffn_w1, L0_ffn_act_scale, L0_ffn_act_bias, L0_ffn_norm2_w, L0_ffn_w2, L1_xattn_Wq, L1_xattn_Wkv, L1_xattn_Wc, L1_ffn_n1_w, L1_ffn_n2_w, L1_ffn_wq, L1_ffn_wk, L1_ffn_wv, L1_ffn_wo, L1_ffn_qn_w, L1_ffn_kn_w, L1_ffn_gate_w, L1_ffn_e0_up, L1_ffn_e0_down, L1_ffn_e1_w1, L1_ffn_e1_w2, L1_ffn_e1_down, L1_ffn_e2_l1, L1_ffn_e2_l2, L1_ffn_e2_l3, L1_ffn_e2_l4, L1_ffn_e3_down, L1_ffn_e3_up, L1_ffn_e3_out):
    import jax
    import jax.numpy as jnp

    def _L0_xattn_ref(q, k, v, Wq, bq, Wk, bk, Wv, bv, Wo, bo):
        import jax, jax.numpy as jnp
        import numpy as np
        D_MODEL = 256
        HEADS = 16
        DK = D_MODEL // HEADS
        B, S = (1, 1024)
        b, s, d = q.shape
        qp = (q @ Wq + bq).reshape(b, s, HEADS, DK).transpose(0, 2, 1, 3)
        kp = k @ Wk + bk
        vp = v @ Wv + bv
        scores = jnp.einsum('bhqd,bkd->bhqk', qp, kp)
        attn = jax.nn.softmax(scores, axis=-1)
        out = jnp.einsum('bhqk,bkd->bhqd', attn, vp)
        out = out.transpose(0, 2, 1, 3).reshape(b, s, d)
        return out @ Wo + bo

    def _L0_ffn_ref(x, norm1_w, w1, act_scale, act_bias, norm2_w, w2):
        import jax, jax.numpy as jnp
        import numpy as np
        EPS_NORM = 1e-08
        EPS_Q = 1e-05

        def rmsnorm(x, w):
            v = jnp.mean(jnp.square(x.astype(jnp.float32)), axis=-1, keepdims=True)
            x_hat = x * jax.lax.rsqrt(v + EPS_NORM)
            return (x_hat * w).astype(x.dtype)

        def activation_quant(x):
            scale = 127.0 / jnp.clip(jnp.max(jnp.abs(x), axis=-1, keepdims=True), EPS_Q, None)
            return jnp.clip(jnp.round(x * scale), -128, 127) / scale

        def weight_quant(w):
            scale = 1.0 / jnp.clip(jnp.mean(jnp.abs(w)), EPS_Q, None)
            return jnp.clip(jnp.round(w * scale), -1, 1) / scale

        def bitlinear(x, norm_w, w):
            x_norm = rmsnorm(x, norm_w)
            x_q = x_norm + jax.lax.stop_gradient(activation_quant(x_norm) - x_norm)
            w_q = w + jax.lax.stop_gradient(weight_quant(w) - w)
            return jnp.einsum('bsd,hd->bsh', x_q, w_q)
        h = bitlinear(x, norm1_w, w1)
        h = act_scale * jnp.square(jax.nn.relu(h)) + act_bias
        y = bitlinear(h, norm2_w, w2)
        return y

    def _L1_xattn_ref(q, kv, Wq, Wkv, Wc):
        import jax, jax.numpy as jnp
        import numpy as np
        N_HEAD = 16
        b, l, d = q.shape
        h = N_HEAD
        dh = d // h
        qp = jnp.einsum('bld,ed->ble', q, Wq)
        scores = jnp.einsum('bld,bmd->blm', qp, kv)
        idx = jnp.argmax(scores, axis=-1)
        mem = jnp.take_along_axis(kv, idx[..., None], axis=1)
        mkv = jnp.einsum('bld,ed->ble', mem, Wkv)
        mk, mv = jnp.split(mkv, 2, axis=-1)
        qh = qp.reshape(b, l, h, dh).transpose(0, 2, 1, 3)
        scale = 1.0 / np.sqrt(dh).astype(np.float32)
        logits = jnp.einsum('bhld,bmd->bhlm', qh, mk) * scale
        attn = jax.nn.softmax(logits, axis=-1)
        out = jnp.einsum('bhlm,bmd->bhld', attn, mv)
        out = out.transpose(0, 2, 1, 3).reshape(b, l, d)
        return jnp.einsum('bld,ed->ble', out, Wc)

    def _L1_ffn_ref(x, n1_w, n2_w, wq, wk, wv, wo, qn_w, kn_w, gate_w, e0_up, e0_down, e1_w1, e1_w2, e1_down, e2_l1, e2_l2, e2_l3, e2_l4, e3_down, e3_up, e3_out):
        import jax, jax.numpy as jnp
        import numpy as np
        DIM = 256
        HEADS = 16
        HD = DIM // HEADS
        M = 64
        E = 4
        K = 2
        HID = 512
        MID = 512
        LB = 0.01
        EPS = 1.1920929e-07

        def _rms(x, w):
            return x * jax.lax.rsqrt(jnp.mean(x * x, axis=-1, keepdims=True) + EPS) * w

        def _gelu(x):
            return jax.nn.gelu(x, approximate=False)
        B, T, C = x.shape
        h = _rms(x, n1_w)
        heads = lambda w_: (h @ w_.T).reshape(B, T, HEADS, HD).transpose(0, 2, 1, 3)
        q = _rms(heads(wq), qn_w)
        k = _rms(heads(wk), kn_w)
        v = heads(wv)
        scores = jnp.einsum('bhqd,bhkd->bhqk', q, k) * HD ** (-0.5)
        causal = jnp.tril(jnp.ones((T, T), bool))
        scores = jnp.where(causal[None, None], scores, -jnp.inf)
        attn = jax.nn.softmax(scores, axis=-1)
        ao = jnp.einsum('bhqk,bhkd->bhqd', attn, v).transpose(0, 2, 1, 3).reshape(B, T, C) @ wo.T
        ao = ao.at[:, :, :M].set(0.0)
        x = x + ao
        xf = _rms(x, n2_w).reshape(-1, C)
        N = xf.shape[0]
        logits = jnp.nan_to_num(xf @ gate_w.T)
        probs = jax.nn.softmax(logits, axis=-1)
        topv, topi = jax.lax.top_k(probs, K)
        topv = topv / (topv.sum(-1, keepdims=True) + 1e-08)
        wts = jnp.zeros((N, E), x.dtype).at[jnp.arange(N)[:, None], topi].add(topv)
        o0 = _gelu(xf @ e0_up.T) @ e0_down.T
        o1 = jax.nn.silu(xf @ e1_w1.T) * (xf @ e1_w2.T) @ e1_down.T
        o2 = _gelu(_gelu(_gelu(xf @ e2_l1.T) @ e2_l2.T) @ e2_l3.T) @ e2_l4.T
        o3 = _gelu(_gelu(xf @ e3_down.T) @ e3_up.T) @ e3_out.T
        moe = wts[:, 0:1] * o0 + wts[:, 1:2] * o1 + wts[:, 2:3] * o2 + wts[:, 3:4] * o3
        moe = moe.reshape(B, T, C).at[:, :, :M].set(0.0)
        return x + moe
    x = x + jnp.tanh(g_xattn[0]) * _L0_xattn_ref(_layernorm(x, axis=-1), ctx_1024, ctx_1024, L0_xattn_Wq, L0_xattn_bq, L0_xattn_Wk, L0_xattn_bk, L0_xattn_Wv, L0_xattn_bv, L0_xattn_Wo, L0_xattn_bo)
    x = x + jnp.tanh(g_ffn[0]) * _L0_ffn_ref(_layernorm(x, axis=-1), L0_ffn_norm1_w, L0_ffn_w1, L0_ffn_act_scale, L0_ffn_act_bias, L0_ffn_norm2_w, L0_ffn_w2)
    x = x + jnp.tanh(g_xattn[1]) * _L1_xattn_ref(_layernorm(x, axis=-1), ctx_1024, L1_xattn_Wq, L1_xattn_Wkv, L1_xattn_Wc)
    x = x + jnp.tanh(g_ffn[1]) * _L1_ffn_ref(_layernorm(x, axis=-1), L1_ffn_n1_w, L1_ffn_n2_w, L1_ffn_wq, L1_ffn_wk, L1_ffn_wv, L1_ffn_wo, L1_ffn_qn_w, L1_ffn_kn_w, L1_ffn_gate_w, L1_ffn_e0_up, L1_ffn_e0_down, L1_ffn_e1_w1, L1_ffn_e1_w2, L1_ffn_e1_down, L1_ffn_e2_l1, L1_ffn_e2_l2, L1_ffn_e2_l3, L1_ffn_e2_l4, L1_ffn_e3_down, L1_ffn_e3_up, L1_ffn_e3_out)
    return x

_drawn_inputs = setup_inputs


def setup_inputs(seed=0):
    import zlib

    import numpy as np

    out = dict(_drawn_inputs(seed))
    spreads = {'g_ffn': (-1.0, 0.2),
     'L0_ffn_norm1_w': (1.0, 0.2),
     'L0_ffn_norm2_w': (1.0, 0.2),
     'L1_ffn_n1_w': (1.0, 0.6),
     'L1_ffn_n2_w': (1.0, 0.549),
     'L1_ffn_qn_w': (1.0, 0.6),
     'L1_ffn_kn_w': (1.0, 0.6)}
    factors = {'L0_xattn_bq': 6.92,
     'L0_xattn_bk': 64.0,
     'L0_xattn_bv': 3.731,
     'L1_xattn_Wq': 3.489,
     'L1_ffn_e2_l1': 8.0,
     'L1_ffn_e2_l2': 8.0,
     'L1_ffn_e2_l3': 8.0,
     'L1_ffn_e2_l4': 8.0,
     'L1_ffn_e3_down': 4.792,
     'L1_ffn_e3_up': 4.661,
     'L1_ffn_e3_out': 4.743,
     'L1_ffn_e0_up': 8.0,
     'L1_ffn_e0_down': 8.0,
     'L1_ffn_e1_w1': 8.0,
     'L1_ffn_e1_w2': 8.0,
     'L1_ffn_e1_down': 8.0}
    for name, (base, spread) in spreads.items():
        noise = np.random.default_rng([zlib.crc32(name.encode()), seed]).standard_normal(out[name].shape)
        drawn = base * np.exp(spread * noise) if base else spread * noise
        out[name] = jnp.asarray(drawn.astype(out[name].dtype))
    for name, factor in factors.items():
        out[name] = (out[name] * factor).astype(out[name].dtype)
    return out
```

```python
import concourse.bass as bass
from concourse import mybir
from contextlib import ExitStack

F32 = mybir.dt.float32
BF16 = mybir.dt.bfloat16
U32 = mybir.dt.uint32
ALU = mybir.AluOpType
ACT = mybir.ActivationFunctionType
AX = mybir.AxisListType

P = 128
B, S, D = 32, 256, 256
NT = B * S // P
H, DK = 16, 16
DC = D // P
HID1 = 1024
M0 = 64
MW = D - M0
E = 4
LN_EPS, EPS_NORM, EPS_Q, EPS_RMS = 1e-5, 1e-8, 1e-5, 1.1920929e-07
RND = 12582912.0
NEG = -1e30
Q_PART = (0, 0, 1, 1, 0, 2)
K_PART = (0, 1, 0, 1, 2, 0)
KR = 16 * len(Q_PART)
STACK_READS = len(Q_PART)


def sl(i, n):
    return bass.ds(i, n)


class Kernel:

    def __init__(self, nc, a, out):
        self.nc, self.a, self.out = nc, a, out
        self.x_rows = a["x"].rearrange("b (t p) d -> p (b t) d", p=P)
        self.out_rows = out.rearrange("b (t p) d -> p (b t) d", p=P)

    def build(self):
        nc = self.nc
        with ExitStack() as c:
            def sb(name, shape, dt=F32):
                return c.enter_context(nc.sbuf_tensor(name, shape, dt))
            self.X = sb("x_all", [P, NT, D])
            self.ST = sb("row_stats", [P, NT, 6])
            self.MEAN = sb("mean", [P, NT])
            self.RSTD = sb("rstd", [P, NT])
            self.RRMS = sb("rrms", [P, NT])
            self.WTS = sb("wts", [P, NT, E])
            self.TG = sb("tanh_gates", [P, 4])
            self.IDF = sb("ident_f", [P, P])
            self.IDB = sb("ident_b", [P, P], BF16)
            self.PS = c.enter_context(nc.psum_tensor("psum", [P, 8, 512], F32))
            self.q_dram = nc.dram_tensor("q_parts", (2, 3, H, DK, S), BF16, kind="Internal").ap()
            self.k_dram = nc.dram_tensor("k_parts", (2, 3, H, DK, S), BF16, kind="Internal").ap()
            self.nm_dram = nc.dram_tensor("max_parts", (2, 3, 32, P), BF16, kind="Internal").ap()
            self.load_phase()
            self.norm_params("a", LN_EPS, None)
            self.attention("A")
            self.norm_params("b", LN_EPS, EPS_NORM)
            self.bit_ffn()
            self.norm_params("c", LN_EPS, None)
            self.attention("C")
            self.norm_params("d", LN_EPS, EPS_RMS)
            self.attention("D")
            self.norm_params("e", EPS_RMS, None, raw=True)
            self.router()
            self.experts()

    def load_phase(self):
        nc, a = self.nc, self.a
        with ExitStack() as c:
            def sem(name):
                return c.enter_context(nc.semaphore("ld_" + name))
            x_in = [sem(f"x_in{n}") for n in range(4)]
            gates_in, ident, stats, gates = sem("gates_in"), sem("ident"), sem("stats"), sem("gates")
            G = c.enter_context(nc.sbuf_tensor("gates_raw", [P, 4], F32))
            block = c.enter_context(nc.Block())
            n4 = NT // 4

            @block.sync
            def _(sp):
                for n in range(4):
                    sp.dma_start(self.X[:, n * n4:(n + 1) * n4, :], self.x_rows[:, n * n4:(n + 1) * n4, :]).then_inc(x_in[n], 16)
                sp.dma_start(G[:, 0:2], a["g_xattn"][None, :].broadcast_to((P, 2))).then_inc(gates_in, 16)
                sp.dma_start(G[:, 2:4], a["g_ffn"][None, :].broadcast_to((P, 2))).then_inc(gates_in, 16)

            @block.gpsimd
            def _(pool):
                nc.gpsimd.memset(self.IDF[:], 0.0).then_inc(ident, 1)
                nc.gpsimd.memset(self.IDB[:], 0.0).then_inc(ident, 1)
                pool.wait_ge(ident, 2)
                for m in (self.IDF, self.IDB):
                    nc.gpsimd.affine_select(out=m[:], in_=m[:], compare_op=ALU.not_equal, fill=1.0, base=0,
                                            pattern=[[-1, P]], channel_multiplier=1).then_inc(ident, 1)
                pool.wait_ge(ident, 4)

            @block.scalar
            def _(act):
                act.wait_ge(gates_in, 32)
                nc.scalar.activation(self.TG[:], G[:], ACT.Tanh).then_inc(gates, 1)
                act.wait_ge(gates, 1)

            @block.vector
            def _(dve):
                for n in range(4):
                    dve.wait_ge(x_in[n], 16)
                    with dve.Fori(n * n4, (n + 1) * n4) as t:
                        nc.vector.bn_stats(self.ST[:, sl(t, 1), :].rearrange("p o s -> p (o s)"),
                                           self.X[:, sl(t, 1), :].rearrange("p o d -> p (o d)")).then_inc(stats, 1)
                dve.wait_ge(stats, NT)

    def norm_params(self, tag, eps, rms_eps, raw=False):
        nc = self.nc
        with ExitStack() as c:
            def sem(name):
                return c.enter_context(nc.semaphore(f"np{tag}_{name}"))
            step, sq_in, sq_out = sem("step"), sem("var_ready"), sem("root_ready")
            V = c.enter_context(nc.sbuf_tensor(f"np{tag}_v", [P, NT], F32))
            T = c.enter_context(nc.sbuf_tensor(f"np{tag}_t", [P, NT], F32))
            R = c.enter_context(nc.sbuf_tensor(f"np{tag}_r", [P, NT], F32))
            U = c.enter_context(nc.sbuf_tensor(f"np{tag}_u", [P, NT], F32))
            block = c.enter_context(nc.Block())
            st, n_roots = self.ST, 1 if rms_eps is None else 2
            v = nc.vector

            @block.vector
            def _(dve):
                n = [0]

                def link(ins):
                    n[0] += 1
                    ins.then_inc(step, 1)
                    dve.wait_ge(step, n[0])

                def rsqrt(out, root, k):
                    v.tensor_scalar(U[:], R[:], 0.0, None, ALU.add).then_inc(sq_in, 1)
                    dve.wait_ge(sq_out, k)
                    link(v.reciprocal(out[:], root[:]))
                    link(v.tensor_tensor(U[:], out[:], out[:], ALU.mult))
                    link(v.tensor_tensor(U[:], U[:], R[:], ALU.mult))
                    link(v.tensor_scalar(U[:], U[:], -0.5, 1.5, ALU.mult, ALU.add))
                    link(v.tensor_tensor(out[:], out[:], U[:], ALU.mult))

                link(v.tensor_tensor(self.MEAN[:], st[:, :, 1], st[:, :, 4], ALU.add))
                link(v.tensor_scalar(self.MEAN[:], self.MEAN[:], 0.5, None, ALU.mult))
                link(v.tensor_tensor(T[:], st[:, :, 1], st[:, :, 4], ALU.subtract))
                link(v.tensor_tensor(T[:], T[:], T[:], ALU.mult))
                link(v.tensor_tensor(V[:], st[:, :, 2], st[:, :, 5], ALU.add))
                link(v.tensor_scalar(V[:], V[:], 1.0 / D, None, ALU.mult))
                link(v.tensor_scalar(T[:], T[:], 0.25, None, ALU.mult))
                link(v.tensor_tensor(V[:], V[:], T[:], ALU.add))
                if raw:
                    link(v.tensor_tensor(T[:], self.MEAN[:], self.MEAN[:], ALU.mult))
                    link(v.tensor_tensor(V[:], V[:], T[:], ALU.add))
                link(v.tensor_scalar(R[:], V[:], eps, None, ALU.add))
                rsqrt(self.RSTD, T, 1)
                if rms_eps is not None:
                    link(v.tensor_tensor(R[:], V[:], self.RSTD[:], ALU.mult))
                    link(v.tensor_tensor(R[:], R[:], self.RSTD[:], ALU.mult))
                    link(v.tensor_scalar(R[:], R[:], rms_eps, None, ALU.add))
                    rsqrt(self.RRMS, T, 2)
                    link(v.tensor_tensor(self.RRMS[:], self.RRMS[:], self.RSTD[:], ALU.mult))

            @block.scalar
            def _(act):
                for k in range(n_roots):
                    act.wait_ge(sq_in, k + 1)
                    nc.scalar.activation(T[:], R[:], ACT.Sqrt).then_inc(sq_out, 1)

    def attention(self, kind):
        nc, a = self.nc, self.a
        mha, gathered = kind == "D", kind == "C"
        L = kind.lower()
        with ExitStack() as c:
            def sb(name, shape, dt=F32):
                return c.enter_context(nc.sbuf_tensor(f"{L}_{name}", shape, dt))

            def sem(name):
                return c.enter_context(nc.semaphore(f"{L}_{name}"))

            OW = MW if mha else D
            QW = 3 * D if mha else D
            Wq = sb("wq", [P, DC, QW])
            Wo = sb("wo", [P, DC, OW])
            KVW = P + DK
            Wkv = None if mha else sb("wkv", [P, DC, KVW])
            CTX = None if mha else sb("ctx", [P, 2, DC, S])
            PB = sb("part_bias", [P, 3])
            FB = sb("free_bias", [P, D + DK])
            XN = sb("xn", [P, 2, D])
            XNT = sb("xnt", [P, DC, S])
            nk = 4 if mha else 3
            QF = sb("qf", [P, nk, S])
            QR = sb("q_rest", [P, nk, S])
            QP = sb("q_parts", [P, 2, 3, nk, S], BF16)
            QS = sb("q_stack", [KR + 3, 2, H, S], BF16)
            KH = H if mha else 1
            KS = sb("k_stack", [KR + 3, 2, KH, S], BF16)
            VH = H if mha else 1
            VP = sb("v_ones", [P, 2, 2, VH, DK + 1])
            NM = sb("neg_max", [P, 2 * H])
            NMR = sb("neg_max_rest", [P, 2 * H])
            NMS = sb("neg_max_parts", [P, 3, 2 * H], BF16)
            NMT = sb("neg_max_t", [3 * 2 * H, 2, P], BF16)
            EX = sb("exps", [P, 2, 2, 512])
            REC = sb("rec", [P, 16])
            HOLD = sb("hold", [P, 1])
            POOL_HOLD = sb("pool_hold", [P, 1])
            O = sb("o", [P, 2, D])
            OT = sb("o_t", [P, DC, S])
            if gathered:
                MX = sb("mx8", [P, 2, 8])
                IX = sb("ix8", [P, 2, 8], U32)
                IXF = sb("ixf", [P, 2])
                IOTA = sb("iota", [P, S])
                OH = sb("onehot", [P, 2, S], BF16)
                OHT = sb("onehot_t", [P, 2, S])
                KVP = sb("kvp", [P, 2, KVW])
            if mha:
                QK = sb("qk", [P, 2, 2 * D])
                SQ = sb("qk_sq", [P, 2 * D])
                MS = sb("qk_ms", [P, 2, 32])
                RT = sb("qk_root", [P, 2, 32])
                HALF = sb("minus_half", [P, 64])
                MASKQ = sb("mask_q", [P, 2, S], BF16)
                MASKK = sb("mask_k", [P, 2, 2, S], BF16)
                XR = sb("x1", [P, 2, D])
                YB = sb("y", [P, 2, D])

            W_, PVB = self.PS[:, 0, :], self.PS[:, 1, :]
            WB = self.PS[:, 0, :].bitcast(BF16)
            sc_slot = [self.PS[:, 2 + n, :] for n in range(2)]
            st_slot = [self.PS[:, 4 + 2 * n:6 + 2 * n, :] for n in range(2)]

            w_in, consts = sem("weights_in"), sem("consts")
            ctx_in = [] if mha else [sem(f"ctx_in{n}") for n in range(2)]
            xn_ready = sem("xn_ready")
            work_full, work_free = sem("work_full"), sem("work_free")
            kf_ready, qp_ready, pool_step = sem("kf_ready"), sem("parts_ready"), sem("pool_step")
            parts_out = [sem(f"parts_out{n}") for n in range(2)]
            stack_in = [sem(f"stack_in{n}") for n in range(2)]
            scores_ready, scores_used = sem("scores_ready"), sem("scores_used")
            nms_ready = sem("neg_max_parts_ready")
            nm_out = [sem(f"neg_max_out{n}") for n in range(2)]
            nm_in = [sem(f"neg_max_in{n}") for n in range(2)]
            st_ready, exp_ready, pv_done, o_ready = sem("scores_t_ready"), sem("exp_ready"), sem("pv_done"), sem("o_ready")
            x_step, dve_step = sem("x_step"), sem("dve_step")
            if kind == "A":
                x_biased = sem("x_plus_bias")
            if mha:
                y_ready, y_out, ms_ready = sem("y_ready"), sem("y_out"), sem("ms_ready")
                xr_ready, rt_ready = sem("xr_ready"), sem("rt_ready")

            NPREP = 3 if kind == "A" else 6
            NBODY = NPREP + 3
            W0 = 2 * NPREP + 1

            def w_prep(b):
                return b * NPREP if isinstance(b, int) and b < 2 else W0 + (b - 2) * NBODY + 2

            def w_nm(b):
                return 2 * NPREP if isinstance(b, int) and b == 0 else W0 + (b - 1) * NBODY

            def w_ot(b):
                return W0 + b * NBODY + 1

            def w_pr(b):
                return W0 + b * NBODY + 2 + NPREP

            def w_last(b, use):
                base = W0 + (B - 2) * NBODY
                return base + {(B - 2, "nm"): 0, (B - 2, "ot"): 1, (B - 2, "pr"): 2,
                               (B - 1, "ot"): 3, (B - 1, "pr"): 4}[(b, use)]

            n0 = 3 if mha else 0
            NS_PREP, NS_NM, NS_PV = {"A": 0, "C": 3, "D": 6}[kind], 3, 2
            NS_BODY = NS_PREP + NS_NM + NS_PV
            s_start = n0 + 2 * NS_PREP + NS_NM

            def s_prep(b):
                return n0 + b * NS_PREP if isinstance(b, int) and b < 2 else s_start + (b - 2) * NS_BODY + NS_PV + NS_NM

            H_AT = {1: (0, 1), 2: (2, 3), 3: (4, 5), 4: (6, 7), 5: (8, 9), 6: (10, 11, 12), 7: (13, 14, 15)}
            N_CONST = {"A": 3, "C": 4, "D": 8}[kind]
            NPO = 4 if mha else 3
            NW = (5 if kind == "A" else 4 if kind == "C" else 7)
            block = c.enter_context(nc.Block())

            def steps(loop, prologue, step):
                prologue()
                with loop(0, B // 2 - 1) as j:
                    for n in range(2):
                        step(2 * j + n, j, n, "full")
                step(B - 2, B // 2 - 1, 0, "no_prep")
                step(B - 1, B // 2 - 1, 1, "only_exps")

            def at(i, d, j, n):
                m = n + d
                return i + d, j + m // 2, m % 2

            @block.sync
            def _(sp):
                if kind == "A":
                    sp.dma_start(Wq[:], a["L0_xattn_Wq"].rearrange("(c p) e -> p c e", p=P)).then_inc(w_in, 16)
                    sp.dma_start(Wo[:], a["L0_xattn_Wo"].rearrange("(c p) e -> p c e", p=P)).then_inc(w_in, 16)
                    sp.dma_start(Wkv[:], a["A_wkv"].rearrange("(c p) e -> p c e", p=P)).then_inc(w_in, 16)
                    sp.dma_start(PB[:], a["A_part_bias"]).then_inc(w_in, 16)
                    sp.dma_start(FB[:], a["A_free_bias"][None, :].broadcast_to((P, D + DK))).then_inc(w_in, 16)
                elif kind == "C":
                    sp.dma_start(Wq[:], a["C_wq"].rearrange("(c p) e -> p c e", p=P)).then_inc(w_in, 16)
                    sp.dma_start(Wo[:], a["C_wc"].rearrange("(c p) e -> p c e", p=P)).then_inc(w_in, 16)
                    sp.dma_start(Wkv[:], a["C_wkv"].rearrange("(c p) e -> p c e", p=P)).then_inc(w_in, 16)
                    sp.dma_start(PB[:], a["A_part_bias"]).then_inc(w_in, 16)
                else:
                    for n in range(3):
                        sp.dma_start(Wq[:, :, n * D:(n + 1) * D],
                                     a[f"D_w{'qkv'[n]}"].rearrange("(c p) e -> p c e", p=P)).then_inc(w_in, 16)
                    sp.dma_start(Wo[:], a["D_wo"][:, M0:].rearrange("(c p) e -> p c e", p=P)).then_inc(w_in, 16)
                    sp.dma_start(PB[:, 0:2], a["D_part_w"]).then_inc(w_in, 16)
                    sp.dma_start(PB[:, 2:3], a["L1_ffn_n1_w"][0:P][:, None]).then_inc(w_in, 16)
                    sp.dma_start(FB[:, 0:1], a["L1_ffn_n1_w"][P:D][:, None]).then_inc(w_in, 16)

                def ctx(b, j, n):
                    if mha:
                        return
                    if not (isinstance(b, int) and b < 2):
                        sp.wait_ge(qp_ready, b - 1)
                    sp.dma_start(CTX[:, n, :, :], a["ctx_t"][sl(b, 1)].rearrange("o (c p) s -> p (o c) s", p=P)).then_inc(ctx_in[n], 16)

                def restack(b, j, n):
                    sp.wait_ge(qp_ready, b + 1)
                    for m in range(2):
                        heads = slice(m * H // 2, (m + 1) * H // 2)
                        sp.dma_start(self.q_dram[n, :, heads].rearrange("t h d s -> (h d) t s"), QP[:, n, :, m, :]).then_inc(parts_out[n], 16)
                        if mha:
                            sp.dma_start(self.k_dram[n, :, heads].rearrange("t h d s -> (h d) t s"), QP[:, n, :, 2 + m, :]).then_inc(parts_out[n], 16)
                    if not mha:
                        sp.dma_start(self.k_dram[n, :, 0].rearrange("t d s -> d t s"), QP[0:DK, n, :, 2, :]).then_inc(parts_out[n], 16)
                    sp.wait_ge(parts_out[n], 16 * NPO * (j + 1))
                    if not (isinstance(b, int) and b < 2):
                        sp.wait_ge(pv_done, 8 * (b - 1) + 1)
                    for blk in range(STACK_READS):
                        rows = slice(16 * blk, 16 * blk + 16)
                        sp.dma_start(QS[rows, n, :, :], self.q_dram[n, Q_PART[blk]].rearrange("h d s -> d h s")).then_inc(stack_in[n], 16)
                        if mha:
                            sp.dma_start(KS[rows, n, :, :], self.k_dram[n, K_PART[blk]].rearrange("h d s -> d h s")).then_inc(stack_in[n], 16)
                        else:
                            sp.dma_start(KS[rows, n, 0, :], self.k_dram[n, K_PART[blk], 0]).then_inc(stack_in[n], 16)

                def neg_max(b, j, n, w):
                    sp.wait_ge(work_free, w + 1)
                    sp.dma_start(self.nm_dram[n].rearrange("t u q -> (t u) q"), NMT[:, n, :]).then_inc(nm_out[n], 16)
                    sp.wait_ge(nm_out[n], 16 * (j + 1))
                    sp.dma_start(QS[KR:KR + 3, n, :, :].rearrange("t h s -> t (h s)"),
                                 self.nm_dram[n].rearrange("t u q -> t (u q)")).then_inc(nm_in[n], 16)

                def y_store(b):
                    sp.wait_ge(y_ready, b + 1)
                    sp.dma_start(self.out_rows[:, sl(2 * b, 2), :], YB[:]).then_inc(y_out, 16)

                def prologue():
                    ctx(0, 0, 0)
                    ctx(1, 0, 1)
                    restack(0, 0, 0)
                    restack(1, 0, 1)
                    neg_max(0, 0, 0, w_nm(0))

                def step(i, j, n, part):
                    if part == "full":
                        ctx(*at(i, 2, j, n))
                    if part != "only_exps":
                        neg_max(*at(i, 1, j, n), w_nm(i + 1) if part == "full" else w_last(i, "nm"))
                    if part == "full":
                        restack(*at(i, 2, j, n))
                    if mha:
                        y_store(i)

                steps(sp.Fori, prologue, step)
                if mha:
                    sp.wait_ge(y_out, 16 * B)

            @block.gpsimd
            def _(pool):
                cn = [0]

                def const(ins):
                    cn[0] += 1
                    ins.then_inc(consts, 1)
                    pool.wait_ge(consts, cn[0])

                const(nc.gpsimd.memset(VP[:, :, :, :, DK:DK + 1], 1.0))
                const(nc.gpsimd.memset(POOL_HOLD[:], 0.0))
                const(nc.gpsimd.memset(KS[KR:KR + 3, :, :, :], 1.0))
                if gathered:
                    const(nc.gpsimd.iota(IOTA[:], [[1, S]], base=0, channel_multiplier=0, allow_small_or_imprecise_dtypes=True))
                if mha:
                    const(nc.gpsimd.memset(HALF[:], -0.5))
                    const(nc.gpsimd.memset(MASKQ[:], 0.0))
                    const(nc.gpsimd.memset(MASKK[:], 0.0))
                    const(nc.gpsimd.affine_select(out=MASKQ[:], in_=MASKQ[:], compare_op=ALU.is_ge, fill=NEG, base=0,
                                                  pattern=[[P, 2], [-1, S]], channel_multiplier=1))
                    const(nc.gpsimd.affine_select(out=MASKK[:].rearrange("p c h q -> p (c h) q"),
                                                  in_=MASKK[:].rearrange("p c h q -> p (c h) q"),
                                                  compare_op=ALU.is_ge, fill=NEG, base=0,
                                                  pattern=[[0, 4], [1, S]], channel_multiplier=-1))
                if kind == "A":
                    pool.wait_ge(w_in, 16 * NW)
                    nc.gpsimd.tensor_scalar(FB[:, 0:D], FB[:, 0:D], self.TG[:, 0:1], None, ALU.mult).then_inc(pool_step, 1)
                    pool.wait_ge(pool_step, 1)
                base = 1 if kind == "A" else 0

                def prep(b, j, n, w):
                    if mha:
                        pool.wait_ge(ms_ready, b + 1)
                        if not (isinstance(b, int) and b == 0):
                            pool.wait_ge(work_free, w)
                        nc.gpsimd.tensor_tensor(RT[:].rearrange("p t h -> p (t h)"), MS[:].rearrange("p t h -> p (t h)"), HALF[:], ALU.pow).then_inc(rt_ready, 1)
                    if kind == "A":
                        pool.wait_ge(xn_ready, b + 1)
                        nc.gpsimd.tensor_tensor(self.X[:, sl(2 * b, 2), :], self.X[:, sl(2 * b, 2), :],
                                                FB[:, None, 0:D].broadcast_to((P, 2, D)), ALU.add).then_inc(x_biased, 1)
                    if mha:
                        pool.wait_ge(work_free, w + 6)
                    else:
                        pool.wait_ge(kf_ready, b + 1)
                    if not (isinstance(b, int) and b < 2):
                        pool.wait_ge(parts_out[n], 16 * NPO * j)
                    g, s = nc.gpsimd, base + 3 * b

                    def hold():
                        g.tensor_tensor(POOL_HOLD[:], POOL_HOLD[:], POOL_HOLD[:], ALU.add)
                    hold()
                    g.tensor_copy(QP[:, n, 0], QF[:]).then_inc(pool_step, 1)
                    pool.wait_ge(pool_step, s + 1)
                    g.tensor_tensor(QR[:], QF[:], QP[:, n, 0], ALU.subtract).then_inc(pool_step, 1)
                    pool.wait_ge(pool_step, s + 2)
                    hold()
                    g.tensor_copy(QP[:, n, 1], QR[:]).then_inc(pool_step, 1)
                    pool.wait_ge(pool_step, s + 3)
                    g.tensor_tensor(QP[:, n, 2], QR[:], QP[:, n, 1], ALU.subtract).then_inc(qp_ready, 1)

                def prologue():
                    prep(0, 0, 0, 0)
                    prep(1, 0, 1, NPREP)

                def step(i, j, n, part):
                    if part == "full":
                        prep(*at(i, 2, j, n), w_prep(i + 2))

                steps(pool.Fori, prologue, step)

            @block.scalar
            def _(act):
                s_ = nc.scalar
                s_.preload_act_table(ACT.Exp)
                act.wait_ge(w_in, 16 * NW)
                if mha:
                    act.wait_ge(dve_step, n0)

                act.sem_inc(exp_ready, 1)

                def evac(w, out, in_):
                    act.wait_ge(work_full, w + 1)
                    s_.activation(out, in_, ACT.Copy).then_inc(work_free, 1)

                def prep(b, j, n, w):
                    first = isinstance(b, int) and b == 0
                    W2 = W_.rearrange("p (m s) -> p m s", m=2)
                    evac(w, XNT[:], W2)
                    if not mha:
                        act.wait_ge(work_full, w + 2)
                        if not first:
                            act.wait_ge(qp_ready, b)
                        if kind == "A":
                            s_.activation(QF[:, 0], W2[:, 0], ACT.Identity, bias=PB[:, 0:1])
                            s_.activation(QF[:, 1], W2[:, 1], ACT.Identity, bias=PB[:, 1:2]).then_inc(work_free, 1)
                        else:
                            s_.activation(QF[:, 0:2], W2, ACT.Copy, scale=DK ** -0.5).then_inc(work_free, 1)
                    if kind == "A":
                        act.wait_ge(work_full, w + 3)
                        s_.activation(QF[:, 2], W_[:, 0:S], ACT.Identity, bias=PB[:, 2:3]).then_inc(kf_ready, 1)
                    if gathered:
                        evac(w + 3, OHT[:], WB[:, 0:2 * S].rearrange("p (m s) -> p m s", m=2))
                        evac(w + 4, KVP[:], W_[:, 0:2 * KVW].rearrange("p (m s) -> p m s", m=2))
                        act.wait_ge(work_full, w + 6)
                        s_.activation(QF[:, 2], W_[:, 0:S], ACT.Copy).then_inc(kf_ready, 1)
                    if mha:
                        evac(w + 1, QK[:, 0], W_)
                        evac(w + 2, QK[:, 1], W_)
                        evac(w + 3, VP[:, n, :, :, 0:DK], W_.rearrange("p (c h d) -> p c h d", c=2, h=H))
                        act.wait_ge(work_full, w + 5)
                        if not first:
                            act.wait_ge(qp_ready, b)
                        s_.activation(QF[:, 0:2], W2, ACT.Copy, scale=PB[:, 0:1]).then_inc(work_free, 1)
                        act.wait_ge(work_full, w + 6)
                        s_.activation(QF[:, 2:4], W2, ACT.Copy, scale=PB[:, 1:2]).then_inc(work_free, 1)

                def exps(b, g):
                    act.wait_ge(st_ready, 8 * b + g + 1)
                    if not (isinstance(b, int) and b == 0 and g < 2):
                        act.wait_ge(pv_done, 8 * b + g)
                    if mha:
                        s_.activation(EX[:, g % 2].rearrange("p c f -> p (c f)")[:, 0:768],
                                      st_slot[g % 2].rearrange("p c f -> p (c f)")[:, 0:768], ACT.Exp).then_inc(exp_ready, 1)
                    else:
                        s_.activation(EX[:, g % 2], st_slot[g % 2], ACT.Exp).then_inc(exp_ready, 1)

                def prologue():
                    prep(0, 0, 0, 0)
                    prep(1, 0, 1, NPREP)

                def step(i, j, n, part):
                    for g in range(8):
                        exps(i, g)
                    evac(w_ot(i) if part == "full" else w_last(i, "ot"), OT[:], W_.rearrange("p (m s) -> p m s", m=2))
                    if part == "full":
                        prep(*at(i, 2, j, n), w_prep(i + 2))

                steps(act.Fori, prologue, step)

            @block.vector
            def _(dve):
                v = nc.vector
                dve.wait_ge(w_in, 16 * NW)
                dve.wait_ge(consts, N_CONST)
                if mha:
                    v.tensor_scalar(Wq[:, 0], Wq[:, 0], PB[:, 2:3], None, ALU.mult).then_inc(dve_step, 1)
                    v.tensor_scalar(Wq[:, 1], Wq[:, 1], FB[:, 0:1], None, ALU.mult).then_inc(dve_step, 1)
                    v.tensor_scalar(PB[:, 0:1], PB[:, 0:1], DK ** -0.5, None, ALU.mult).then_inc(dve_step, 1)
                    dve.wait_ge(dve_step, n0)
                def norm(b, w_before):
                    if w_before is not None:
                        dve.wait_ge(work_free, w_before + 1)
                    r = self.RRMS if mha else self.RSTD
                    for t in range(2):
                        i = v.tensor_scalar(XN[:, t, :], self.X[:, sl(2 * b + t, 1), :].rearrange("p o d -> p (o d)"),
                                            self.MEAN[:, sl(2 * b + t, 1)], r[:, sl(2 * b + t, 1)], ALU.subtract, ALU.mult)
                    i.then_inc(xn_ready, 1)

                def prep(b, j, n, w, w_before, s):
                    first = isinstance(b, int) and b == 0
                    norm(b, w_before)
                    if kind == "A":
                        dve.wait_ge(kf_ready, b + 1)
                        v.tensor_tensor(VP[:, n, :, 0, 0:DK], W_[:, S:S + 2 * DK].rearrange("p (c d) -> p c d", c=2),
                                        FB[:, None, D:D + DK].broadcast_to((P, 2, DK)), ALU.add).then_inc(work_free, 1)
                    if gathered:
                        dve.wait_ge(work_full, w + 3)
                        v.tensor_copy(HOLD[:], W_[:, 0:1])
                        for t in range(2):
                            i = v.max(MX[:, t], W_[:, t * S:(t + 1) * S])
                        i.then_inc(dve_step, 1)
                        dve.wait_ge(dve_step, s + 1)
                        v.tensor_copy(HOLD[:], MX[:, 0, 0:1])
                        for t in range(2):
                            i = v.max_index(IX[:, t], MX[:, t], W_[:, t * S:(t + 1) * S])
                        i.then_inc(work_free, 1)
                        dve.wait_ge(work_free, w + 3)
                        v.tensor_copy(IXF[:], IX[:, :, 0]).then_inc(dve_step, 1)
                        dve.wait_ge(dve_step, s + 2)
                        for t in range(2):
                            i = v.tensor_scalar(OH[:, t], IOTA[:], IXF[:, t:t + 1], None, ALU.is_equal)
                        i.then_inc(dve_step, 1)
                        dve.wait_ge(kf_ready, b + 1)
                        v.tensor_copy(VP[:, n, :, 0, 0:DK], W_[:, S:S + 2 * DK].rearrange("p (c d) -> p c d", c=2)).then_inc(work_free, 1)
                    if mha:
                        k = [0]

                        def link(ins):
                            k[0] += 1
                            ins.then_inc(dve_step, 1)
                            dve.wait_ge(dve_step, s + k[0])
                        for t in range(2):
                            dve.wait_ge(work_free, w + 2 + t)
                            link(v.tensor_tensor(SQ[:], QK[:, t], QK[:, t], ALU.mult))
                            link(v.tensor_reduce(MS[:, t], SQ[:].rearrange("p (h d) -> p h d", d=DK), AX.X, ALU.add))
                        v.tensor_scalar(MS[:], MS[:], 1.0 / DK, EPS_RMS, ALU.mult, ALU.add).then_inc(ms_ready, 1)
                        dve.wait_ge(rt_ready, b + 1)
                        for t in range(2):
                            link(v.tensor_tensor(QK[:, t].rearrange("p (h d) -> p h d", d=DK),
                                                 QK[:, t].rearrange("p (h d) -> p h d", d=DK),
                                                 RT[:, t, :, None].broadcast_to((P, 32, DK)), ALU.mult))

                def row_max(b, h):
                    dve.wait_ge(scores_ready, H * b + h + 1)
                    v.tensor_reduce(NM[:, 2 * h:2 * h + 2], sc_slot[h % 2].rearrange("p (t k) -> p t k", t=2),
                                    AX.X, ALU.max, negate=True).then_inc(scores_used, 1)

                def neg_max(b, j, n, w, s):
                    dve.wait_ge(scores_used, H * (b + 1))
                    v.tensor_copy(NMS[:, 0], NM[:]).then_inc(dve_step, 1)
                    dve.wait_ge(dve_step, s + 1)
                    v.tensor_tensor(NMR[:], NM[:], NMS[:, 0], ALU.subtract).then_inc(dve_step, 1)
                    dve.wait_ge(dve_step, s + 2)
                    v.tensor_copy(NMS[:, 1], NMR[:]).then_inc(dve_step, 1)
                    dve.wait_ge(dve_step, s + 3)
                    v.tensor_tensor(NMS[:, 2], NMR[:], NMS[:, 1], ALU.subtract).then_inc(nms_ready, 1)
                    dve.wait_ge(work_full, w + 1)
                    if not (isinstance(b, int) and b < 2):
                        dve.wait_ge(nm_out[n], 16 * j)
                    v.tensor_copy(NMT[:, n, :], WB[0:3 * 2 * H, 0:P]).then_inc(work_free, 1)

                def half(b, k, w_before, s):
                    dve.wait_ge(pv_done, 8 * b + 4 * k + 5)
                    if w_before is not None:
                        dve.wait_ge(work_free, w_before + 1)
                    pv = PVB[:, 0:16 * (DK + 1)].rearrange("p (u e) -> p u e", e=DK + 1)
                    v.reciprocal(REC[:], pv[:, :, DK]).then_inc(dve_step, 1)
                    dve.wait_ge(dve_step, s + 1)
                    v.tensor_tensor(O[:, :, k * P:(k + 1) * P].rearrange("p t (h d) -> p h t d", d=DK),
                                    pv[:, :, 0:DK].rearrange("p (h t) d -> p h t d", t=2),
                                    REC[:].rearrange("p (h t) -> p h t", t=2)[:, :, :, None].broadcast_to((P, 8, 2, DK)),
                                    ALU.mult).then_inc(o_ready, 1)

                def post(b, w):
                    xs = self.X[:, sl(2 * b, 2), :]
                    if not mha:
                        dve.wait_ge(work_full, w + 1)
                        if kind == "A":
                            dve.wait_ge(x_biased, b + 1)
                        gate = self.TG[:, 0:1] if kind == "A" else self.TG[:, 1:2]
                        v.scalar_tensor_tensor(xs, W_.rearrange("p (t d) -> p t d", t=2), gate, xs, ALU.mult, ALU.add).then_inc(work_free, 1)
                        dve.wait_ge(work_free, w + 1)
                        src = [self.X[:, sl(2 * b + t, 1), :].rearrange("p o d -> p (o d)") for t in range(2)]
                    else:
                        if not (isinstance(b, int) and b == 0):
                            dve.wait_ge(x_step, 2 * b)
                        for t in range(2):
                            i = v.tensor_scalar(XR[:, t, :], self.X[:, sl(2 * b + t, 1), :].rearrange("p o d -> p (o d)"),
                                                self.MEAN[:, sl(2 * b + t, 1)], self.RSTD[:, sl(2 * b + t, 1)], ALU.subtract, ALU.mult)
                        i.then_inc(xr_ready, 1)
                        dve.wait_ge(xr_ready, b + 1)
                        dve.wait_ge(work_full, w + 1)
                        v.tensor_tensor(XR[:, :, M0:D], XR[:, :, M0:D], W_[:, 0:2 * MW].rearrange("p (t d) -> p t d", t=2), ALU.add).then_inc(work_free, 1)
                        dve.wait_ge(work_free, w + 1)
                        if not (isinstance(b, int) and b == 0):
                            dve.wait_ge(y_out, 16 * b)
                        v.scalar_tensor_tensor(YB[:], XR[:], self.TG[:, 3:4], xs, ALU.mult, ALU.add).then_inc(y_ready, 1)
                        dve.wait_ge(y_ready, b + 1)
                        v.tensor_scalar(xs, XR[:], 1.0, None, ALU.mult)
                        src = [XR[:, t, :] for t in range(2)]
                    for t in range(2):
                        v.bn_stats(self.ST[:, sl(2 * b + t, 1), :].rearrange("p o s -> p (o s)"), src[t]).then_inc(x_step, 1)

                def prologue():
                    prep(0, 0, 0, 0, None, n0)
                    prep(1, 0, 1, NPREP, 0, n0 + NS_PREP)
                    for h in range(H):
                        row_max(0, h)
                    neg_max(0, 0, 0, w_nm(0), n0 + 2 * NS_PREP)

                def step(i, j, n, part):
                    s = s_start + NS_BODY * i
                    if part == "only_exps":
                        s = s_start + NS_BODY * (B - 2) + NS_NM + NS_PV
                    w_o_before = (None if isinstance(i, int) and i == 0 else
                                  w_last(B - 2, "ot") if part == "only_exps" else w_ot(i - 1))
                    for g in range(8):
                        if part != "only_exps":
                            if g >= 1:
                                for h in H_AT[g]:
                                    row_max(i + 1, h)
                        if g == 4:
                            half(i, 0, w_o_before, s)
                    half(i, 1, w_o_before, s + 1)
                    s = s + 2
                    if part != "only_exps":
                        neg_max(*at(i, 1, j, n), w_nm(i + 1) if part == "full" else w_last(i, "nm"), s)
                    if part == "full":
                        prep(*at(i, 2, j, n), w_prep(i + 2), w_prep(i + 1) if not isinstance(i, int) else None, s + NS_NM)
                    post(i, w_pr(i) if part == "full" else w_last(i, "pr"))

                steps(dve.Fori, prologue, step)
                dve.wait_ge(x_step, 2 * B)

            @block.tensor
            def _(pe):
                mm, tr = nc.tensor.matmul, nc.tensor.transpose
                pe.wait_ge(w_in, 16 * NW)
                pe.wait_ge(consts, N_CONST)
                if mha:
                    pe.wait_ge(dve_step, 3)

                pe.sem_inc(pv_done, 1)

                def use(w):
                    if not (isinstance(w, int) and w == 0):
                        pe.wait_ge(work_free, w)

                def transpose_rows(src):
                    for cc in range(DC):
                        for t in range(2):
                            i = tr(W_[:, cc * S + t * P:cc * S + (t + 1) * P], src[:, t, cc * P:(cc + 1) * P], self.IDF[:])
                    i.then_inc(work_full, 1)

                def prep(b, j, n, w):
                    pe.wait_ge(xn_ready, b + 1)
                    use(w)
                    transpose_rows(XN)
                    use(w + 1)
                    if not mha:
                        for m in range(2):
                            for cc in range(DC):
                                i = mm(W_[:, m * S:(m + 1) * S], Wq[:, cc, m * P:(m + 1) * P], XNT[:, cc], start=cc == 0, stop=cc == DC - 1)
                        i.then_inc(work_full, 1)
                        pe.wait_ge(ctx_in[n], 16 * (j + 1))
                    if kind == "A":
                        use(w + 2)
                        for cc in range(DC):
                            mm(W_[:, 0:S], Wkv[:, cc, 0:P], CTX[:, n, cc], start=cc == 0, stop=cc == DC - 1)
                        for k in range(2):
                            for cc in range(DC):
                                i = mm(W_[:, S + k * DK:S + (k + 1) * DK], CTX[:, n, cc, k * P:(k + 1) * P], Wkv[:, cc, P:P + DK], start=cc == 0, stop=cc == DC - 1)
                        i.then_inc(work_full, 1)
                    if gathered:
                        use(w + 2)
                        for t in range(2):
                            for cc in range(DC):
                                i = mm(W_[:, t * S:(t + 1) * S], QF[:, cc, t * P:(t + 1) * P], CTX[:, n, cc], start=cc == 0, stop=cc == DC - 1)
                        i.then_inc(work_full, 1)
                        use(w + 3)
                        pe.wait_ge(dve_step, s_prep(b) + 3)
                        for k in range(2):
                            for t in range(2):
                                i = tr(WB[:, k * S + t * P:k * S + (t + 1) * P], OH[:, t, k * P:(k + 1) * P], self.IDB[:])
                        i.then_inc(work_full, 1)
                        use(w + 4)
                        for k in range(2):
                            for cc in range(DC):
                                i = mm(W_[:, k * KVW:(k + 1) * KVW], CTX[:, n, cc, k * P:(k + 1) * P], Wkv[:, cc], start=cc == 0, stop=cc == DC - 1)
                        i.then_inc(work_full, 1)
                        use(w + 5)
                        for k in range(2):
                            mm(W_[:, 0:S], KVP[:, k, 0:P], OHT[:, k], start=k == 0, stop=k == 1)
                        for t in range(2):
                            for k in range(2):
                                i = mm(W_[:, S + t * DK:S + (t + 1) * DK], OHT[:, k, t * P:(t + 1) * P], KVP[:, k, P:P + DK], start=k == 0, stop=k == 1)
                        i.then_inc(work_full, 1)
                    if mha:
                        for t in range(2):
                            use(w + 1 + t)
                            for cc in range(DC):
                                i = mm(W_[:, :], XNT[:, cc, t * P:(t + 1) * P], Wq[:, cc, 0:2 * D], start=cc == 0, stop=cc == DC - 1)
                            i.then_inc(work_full, 1)
                        use(w + 3)
                        for t in range(2):
                            for cc in range(DC):
                                i = mm(W_[:, t * S:(t + 1) * S], XNT[:, cc, t * P:(t + 1) * P], Wq[:, cc, 2 * D:3 * D], start=cc == 0, stop=cc == DC - 1)
                        i.then_inc(work_full, 1)
                        use(w + 4)
                        pe.wait_ge(dve_step, s_prep(b) + 6)
                        transpose_rows(QK)
                        use(w + 5)
                        for cc in range(DC):
                            for t in range(2):
                                i = tr(W_[:, cc * S + t * P:cc * S + (t + 1) * P], QK[:, t, D + cc * P:D + (cc + 1) * P], self.IDF[:])
                        i.then_inc(work_full, 1)

                def scores(b, j, n, h):
                    if h == 0:
                        pe.wait_ge(stack_in[n], 16 * 2 * STACK_READS * (j + 1))
                    if not (isinstance(b, int) and b == 0 and h < 2):
                        pe.wait_ge(scores_used, H * b + h - 1)
                    if mha:
                        mm(sc_slot[h % 2], self.IDB[:], MASKQ[:].rearrange("p t k -> p (t k)"), start=True, stop=True, skip_group_check=True)
                    for t in range(2):
                        i = mm(sc_slot[h % 2][:, t * S:(t + 1) * S], QS[0:KR, n, h, t * P:(t + 1) * P], KS[0:KR, n, h if mha else 0, :],
                               start=not mha, stop=True, skip_group_check=mha)
                    i.then_inc(scores_ready, 1)

                def neg_max(b, w):
                    pe.wait_ge(nms_ready, b + 1)
                    use(w)
                    tr(WB[0:3 * 2 * H, 0:P], NMS[:].rearrange("p t u -> p (t u)"), self.IDB[:]).then_inc(work_full, 1)

                def scores_t(b, j, n, g):
                    if g == 0:
                        pe.wait_ge(nm_in[n], 16 * (j + 1))
                    if not (isinstance(b, int) and b == 0 and g < 2):
                        pe.wait_ge(exp_ready, 8 * b + g)
                    slot = st_slot[g % 2]
                    if not mha:
                        for k in range(2):
                            i = mm(slot[:, k, :], KS[:, n, 0, k * P:(k + 1) * P], QS[:, n, 2 * g:2 * g + 2, :], start=True, stop=True)
                    else:
                        mm(slot[:, 0, :], self.IDB[:], MASKK[:, 0].rearrange("p h q -> p (h q)"), start=True, stop=True, skip_group_check=True)
                        for h in range(2):
                            mm(slot[:, 0, h * S:(h + 1) * S], KS[:, n, 2 * g + h, 0:P], QS[:, n, 2 * g + h, :], start=False, stop=True, skip_group_check=True)
                        mm(slot[:, 1, 0:S].rearrange("p (h q) -> p h q", h=2), self.IDB[:], MASKK[:, 1, :, 0:P], start=True, stop=True, skip_group_check=True)
                        for h in range(2):
                            i = mm(slot[:, 1, h * P:(h + 1) * P], KS[:, n, 2 * g + h, P:S], QS[:, n, 2 * g + h, P:S], start=False, stop=True, skip_group_check=True)
                    i.then_inc(st_ready, 1)

                def values(b, n, g):
                    pe.wait_ge(exp_ready, 8 * b + g + 2)
                    if g % 4 == 0 and not (isinstance(b, int) and b == 0 and g == 0):
                        pe.wait_ge(o_ready, 2 * b + g // 4)
                    for h in range(2):
                        for t in range(2):
                            u = 2 * (2 * (g % 4) + h) + t
                            chunks = range(t + 1) if mha else range(2)
                            for k in chunks:
                                if mha:
                                    e = EX[:, g % 2, 0, h * S + t * P:h * S + (t + 1) * P] if k == 0 else EX[:, g % 2, 1, h * P:(h + 1) * P]
                                else:
                                    e = EX[:, g % 2, k, h * S + t * P:h * S + (t + 1) * P]
                                i = mm(PVB[:, u * (DK + 1):(u + 1) * (DK + 1)], e, VP[:, n, k, (2 * g + h) if mha else 0, :],
                                       start=k == 0, stop=k == chunks[-1])
                    i.then_inc(pv_done, 1)

                def out_t(b, w):
                    pe.wait_ge(o_ready, 2 * b + 2)
                    use(w)
                    transpose_rows(O)

                def project(b, w):
                    use(w)
                    for t in range(2):
                        for cc in range(DC):
                            i = mm(W_[:, t * OW:(t + 1) * OW], OT[:, cc, t * P:(t + 1) * P], Wo[:, cc], start=cc == 0, stop=cc == DC - 1)
                    i.then_inc(work_full, 1)

                def prologue():
                    prep(0, 0, 0, 0)
                    prep(1, 0, 1, NPREP)
                    for h in range(H):
                        scores(0, 0, 0, h)
                    neg_max(0, w_nm(0))

                def step(i, j, n, part):
                    for g in range(8):
                        scores_t(i, j, n, g)
                        if part != "only_exps" and g >= 1:
                            for h in H_AT[g]:
                                scores(*at(i, 1, j, n), h)
                        if g >= 1:
                            values(i, n, g - 1)
                    values(i, n, 7)
                    if part != "only_exps":
                        neg_max(i + 1, w_nm(i + 1) if part == "full" else w_last(i, "nm"))
                    out_t(i, w_ot(i) if part == "full" else w_last(i, "ot"))
                    if part == "full":
                        prep(*at(i, 2, j, n), w_prep(i + 2))
                    project(i, w_pr(i) if part == "full" else w_last(i, "pr"))

                steps(pe.Fori, prologue, step)

    def bit_ffn(self):
        nc, a = self.nc, self.a
        KH1, KH2 = DC, HID1 // P
        with ExitStack() as c:
            def sb(name, shape, dt=F32):
                return c.enter_context(nc.sbuf_tensor(f"b_{name}", shape, dt))

            def sem(name):
                return c.enter_context(nc.semaphore(f"b_{name}"))
            WF = sb("w_float", [P, 2, KH1 * HID1])
            W1 = sb("w1", [P, KH1, HID1], BF16)
            W2 = sb("w2", [P, KH2, D], BF16)
            N1 = sb("n1", [P, D])
            N2 = sb("n2", [P, HID1])
            AB = sb("act_scale_bias", [P, 2])
            ONES = sb("ones", [P, P])
            WS = sb("w_sum", [P, 1])
            WM = sb("w_mean", [P, 2])
            WI = sb("w_scale", [P, 2])
            WG = sb("w2_mean_gate", [P, 1])
            XB = sb("xb", [P, D])
            QA = sb("qa", [P, D])
            QB = sb("qb", [P, D], BF16)
            QT = sb("qt", [P, KH1, P], BF16)
            S1 = sb("s1", [P, 4])
            C1 = sb("c1", [P, 2])
            R = sb("r", [P, 2, HID1])
            G = sb("g", [P, HID1])
            SQ = sb("sq", [P, HID1])
            S2 = sb("s2", [P, 12])
            MSQ = sb("msq", [P, 1])
            Y2 = sb("y2", [P, HID1])
            Q2 = sb("q2", [P, HID1])
            Q2B = sb("q2b", [P, HID1], BF16)
            Q2T = sb("q2t", [P, KH2, P], BF16)
            C2 = sb("c2", [P, 1])
            PS = self.PS
            TB = PS[:, 0, 0:P].bitcast(BF16)
            HB = [PS[:, 1 + 2 * n:3 + 2 * n, :] for n in range(2)]
            T2B = PS[:, 5, :].bitcast(BF16)
            YB = PS[:, 6, 0:D]
            SB = PS[:, 7, 0:1]
            W2_COLS = PS[:, 1:5, :].rearrange("p k f -> p (k f)")

            w_in, ones, sums, w_sum, w_ready = sem("w_in"), sem("ones"), sem("sums"), sem("w_sum"), sem("w_ready")
            q_ready, qt_ready, qt_evac = sem("q_ready"), sem("qt_psum"), sem("qt_sbuf")
            h_ready, r_ready, g_ready, sq_ready = sem("h_ready"), sem("relu_ready"), sem("g_ready"), sem("sum_sq_ready")
            ms_ready, root_ready = sem("ms_ready"), sem("root_ready")
            q2_ready, q2t_ready, q2t_evac, y_ready, y_used = sem("q2_ready"), sem("q2t_psum"), sem("q2t_sbuf"), sem("y_ready"), sem("y_used")
            c1_ready, r_used, setup, front_step, back_step, stats = sem("c1_ready"), sem("relu_used"), sem("setup"), sem("front_step"), sem("back_step"), sem("stats")
            block = c.enter_context(nc.Block())

            def steps(loop, prologue, step):
                prologue()
                with loop(0, NT // 2 - 1) as j:
                    for n in range(2):
                        step(2 * j + n, n, True)
                step(NT - 2, 0, True)
                step(NT - 1, 1, False)

            @block.sync
            def _(sp):
                sp.dma_start(WF[:, 0, :].rearrange("p (c h) -> p c h", c=KH1), a["B_w1"].rearrange("(c p) h -> p c h", p=P)).then_inc(w_in, 16)
                sp.dma_start(WF[:, 1, :].rearrange("p (c h) -> p c h", c=KH2), a["B_w2"].rearrange("(c p) h -> p c h", p=P)).then_inc(w_in, 16)
                sp.dma_start(N1[:], a["L0_ffn_norm1_w"][None, :].broadcast_to((P, D))).then_inc(w_in, 16)
                sp.dma_start(N2[:], a["L0_ffn_norm2_w"][None, :].broadcast_to((P, HID1))).then_inc(w_in, 16)
                sp.dma_start(AB[:, 0:1], a["L0_ffn_act_scale"][None, :].broadcast_to((P, 1))).then_inc(w_in, 16)
                sp.dma_start(AB[:, 1:2], a["L0_ffn_act_bias"][None, :].broadcast_to((P, 1))).then_inc(w_in, 16)

            @block.gpsimd
            def _(pool):
                nc.gpsimd.memset(ONES[:], 1.0).then_inc(ones, 1)

            @block.scalar
            def _(act):
                s_ = nc.scalar
                act.wait_ge(w_in, 16 * 6)
                s_.activation(R[:].rearrange("p n h -> p (n h)"), WF[:, 1, :], ACT.Abs).then_inc(sums, 1)

                def front(t, n):
                    act.wait_ge(qt_ready, t + 1)
                    s_.activation(QT[:], TB.rearrange("p (c q) -> p c q", c=KH1), ACT.Copy).then_inc(qt_evac, 1)
                    act.wait_ge(c1_ready, t + 1)
                    act.wait_ge(h_ready, t + 1)
                    if not (isinstance(t, int) and t < 2):
                        act.wait_ge(g_ready, t - 1)
                    s_.activation(R[:, n].rearrange("p (k f) -> p k f", k=2), HB[n], ACT.Relu, scale=C1[:, n:n + 1]).then_inc(r_ready, 1)

                def back(t, n):
                    act.wait_ge(g_ready, t + 1)
                    s_.activation(SQ[:], G[:], ACT.Square, bias=AB[:, 1:2], accum_out=MSQ[:]).then_inc(sq_ready, 1)
                    act.wait_ge(ms_ready, t + 1)
                    s_.activation(S2[:, 1:2], S2[:, 0:1], ACT.Sqrt).then_inc(root_ready, 1)
                    act.wait_ge(q2t_ready, t + 1)
                    s_.activation(Q2T[:], T2B.rearrange("p (c q) -> p c q", c=KH2), ACT.Copy).then_inc(q2t_evac, 1)

                def step(t, n, more):
                    if more:
                        front(t + 1, 1 - n)
                    back(t, n)

                steps(act.Fori, lambda: front(0, 0), step)

            @block.vector
            def _(dve):
                v = nc.vector
                k0 = [0]

                def setup_link(ins):
                    k0[0] += 1
                    ins.then_inc(setup, 1)
                    dve.wait_ge(setup, k0[0])

                dve.wait_ge(w_in, 16 * 6)
                v.tensor_reduce(WS[:], WF[:, 0, :], AX.X, ALU.add, apply_absolute_value=True).then_inc(sums, 1)
                dve.wait_ge(w_sum, 1)
                setup_link(v.tensor_reduce(WM[:, 1:2], W2_COLS, AX.X, ALU.add))
                setup_link(v.tensor_copy(WM[:, 0:1], SB))
                setup_link(v.tensor_scalar(WM[:], WM[:], 1.0 / (D * HID1), EPS_Q, ALU.mult, ALU.max))
                setup_link(v.reciprocal(WI[:], WM[:]))
                setup_link(v.tensor_scalar(WG[:], WM[:, 1:2], self.TG[:, 2:3], None, ALU.mult))
                for w, wq in ((0, W1), (1, W2)):
                    setup_link(v.tensor_scalar(WF[:, w, :], WF[:, w, :], WI[:, w:w + 1], RND, ALU.mult, ALU.add))
                    setup_link(v.tensor_scalar(WF[:, w, :], WF[:, w, :], RND, 1.0, ALU.subtract, ALU.min))
                    v.tensor_scalar(wq[:].rearrange("p c h -> p (c h)"), WF[:, w, :], -1.0, None, ALU.max).then_inc(w_ready, 1)

                NF, NB = 7, 9
                k = [0]

                def flink(t, ins):
                    k[0] += 1
                    ins.then_inc(front_step, 1)
                    dve.wait_ge(front_step, NF * t + k[0])

                def blink(t, ins):
                    k[0] += 1
                    ins.then_inc(back_step, 1)
                    dve.wait_ge(back_step, NB * t + k[0])

                def front(t, n):
                    k[0] = 0
                    flink(t, v.tensor_scalar(XB[:], self.X[:, sl(t, 1), :].rearrange("p o d -> p (o d)"),
                                             self.MEAN[:, sl(t, 1)], self.RRMS[:, sl(t, 1)], ALU.subtract, ALU.mult))
                    flink(t, v.tensor_tensor(XB[:], XB[:], N1[:], ALU.mult))
                    flink(t, v.tensor_reduce(S1[:, 0:1], XB[:], AX.X, ALU.max, apply_absolute_value=True))
                    flink(t, v.tensor_scalar(S1[:, 1:2], S1[:, 0:1], EPS_Q, None, ALU.max))
                    flink(t, v.reciprocal(S1[:, 3:4], S1[:, 1:2]))
                    flink(t, v.tensor_scalar(S1[:, 2:3], S1[:, 3:4], 127.0, None, ALU.mult))
                    flink(t, v.tensor_scalar(QA[:], XB[:], S1[:, 2:3], RND, ALU.mult, ALU.add))
                    if not (isinstance(t, int) and t == 0):
                        dve.wait_ge(qt_ready, t)
                    v.tensor_scalar(QB[:], QA[:], RND, None, ALU.subtract).then_inc(q_ready, 1)
                    if not (isinstance(t, int) and t < 2):
                        dve.wait_ge(r_ready, t - 1)
                    v.tensor_scalar(C1[:, n:n + 1], S1[:, 1:2], 1.0 / 127.0, WM[:, 0:1], ALU.mult, ALU.mult).then_inc(c1_ready, 1)

                def back(t, n):
                    k[0] = 0
                    dve.wait_ge(r_ready, t + 1)
                    if not (isinstance(t, int) and t == 0):
                        dve.wait_ge(sq_ready, t)
                    v.scalar_tensor_tensor(G[:], R[:, n], AB[:, 0:1], R[:, n], ALU.mult, ALU.mult).then_inc(g_ready, 1)
                    dve.wait_ge(g_ready, t + 1)
                    blink(t, v.scalar_tensor_tensor(Y2[:], G[:], AB[:, 1:2], N2[:], ALU.add, ALU.mult))
                    blink(t, v.tensor_reduce(S2[:, 2:3], Y2[:], AX.X, ALU.max, apply_absolute_value=True))
                    dve.wait_ge(sq_ready, t + 1)
                    v.tensor_scalar(S2[:, 0:1], MSQ[:], 1.0 / HID1, EPS_NORM, ALU.mult, ALU.add).then_inc(ms_ready, 1)
                    dve.wait_ge(root_ready, t + 1)
                    blink(t, v.reciprocal(S2[:, 3:4], S2[:, 1:2]))
                    blink(t, v.tensor_scalar(S2[:, 4:5], S2[:, 3:4], S2[:, 3:4], S2[:, 0:1], ALU.mult, ALU.mult))
                    blink(t, v.tensor_scalar(S2[:, 4:5], S2[:, 4:5], -0.5, 1.5, ALU.mult, ALU.add))
                    blink(t, v.tensor_scalar(S2[:, 5:6], S2[:, 4:5], S2[:, 3:4], None, ALU.mult))
                    blink(t, v.tensor_scalar(S2[:, 6:7], S2[:, 2:3], S2[:, 5:6], EPS_Q, ALU.mult, ALU.max))
                    blink(t, v.reciprocal(S2[:, 7:8], S2[:, 6:7]))
                    blink(t, v.tensor_scalar(S2[:, 8:9], S2[:, 7:8], 127.0, S2[:, 5:6], ALU.mult, ALU.mult))
                    v.tensor_scalar(Q2[:], Y2[:], S2[:, 8:9], RND, ALU.mult, ALU.add).then_inc(stats, 1)
                    dve.wait_ge(stats, 3 * t + 1)
                    if not (isinstance(t, int) and t == 0):
                        dve.wait_ge(q2t_ready, t)
                    v.tensor_scalar(Q2B[:], Q2[:], RND, None, ALU.subtract).then_inc(q2_ready, 1)
                    v.tensor_scalar(C2[:], S2[:, 6:7], 1.0 / 127.0, WG[:, 0:1], ALU.mult, ALU.mult).then_inc(stats, 1)
                    dve.wait_ge(stats, 3 * t + 2)
                    dve.wait_ge(y_ready, t + 1)
                    xs = self.X[:, sl(t, 1), :].rearrange("p o d -> p (o d)")
                    v.scalar_tensor_tensor(xs, YB, C2[:], xs, ALU.mult, ALU.add).then_inc(y_used, 1)
                    dve.wait_ge(y_used, t + 1)
                    v.bn_stats(self.ST[:, sl(t, 1), :].rearrange("p o s -> p (o s)"), xs).then_inc(stats, 1)

                def step(t, n, more):
                    if more:
                        front(t + 1, 1 - n)
                    back(t, n)

                steps(dve.Fori, lambda: front(0, 0), step)
                dve.wait_ge(stats, 3 * NT)

            @block.tensor
            def _(pe):
                mm, tr = nc.tensor.matmul, nc.tensor.transpose
                pe.wait_ge(ones, 1)
                pe.wait_ge(sums, 2)
                mm(SB, ONES[:], WS[:], start=True, stop=True)
                w2_abs = R[:].rearrange("p n (k f) -> p (n k) f", f=512)
                for k in range(4):
                    i = mm(PS[:, 1 + k, :], ONES[:], w2_abs[:, k], start=True, stop=True)
                i.then_inc(w_sum, 1)
                pe.wait_ge(w_ready, 2)

                def front(t, n):
                    pe.wait_ge(q_ready, t + 1)
                    if not (isinstance(t, int) and t == 0):
                        pe.wait_ge(qt_evac, t)
                    for cc in range(KH1):
                        i = tr(TB[:, cc * P:(cc + 1) * P], QB[:, cc * P:(cc + 1) * P], self.IDB[:])
                    i.then_inc(qt_ready, 1)
                    pe.wait_ge(qt_evac, t + 1)
                    if not (isinstance(t, int) and t < 2):
                        pe.wait_ge(r_ready, t - 1)
                    for k in range(2):
                        for cc in range(KH1):
                            i = mm(HB[n][:, k, :], QT[:, cc], W1[:, cc, k * 512:(k + 1) * 512], start=cc == 0, stop=cc == KH1 - 1)
                    i.then_inc(h_ready, 1)

                def back(t, n):
                    pe.wait_ge(q2_ready, t + 1)
                    if not (isinstance(t, int) and t == 0):
                        pe.wait_ge(q2t_evac, t)
                    for cc in range(KH2):
                        i = tr(T2B[:, cc * P:(cc + 1) * P], Q2B[:, cc * P:(cc + 1) * P], self.IDB[:])
                    i.then_inc(q2t_ready, 1)
                    pe.wait_ge(q2t_evac, t + 1)
                    if not (isinstance(t, int) and t == 0):
                        pe.wait_ge(y_used, t)
                    for cc in range(KH2):
                        i = mm(YB, Q2T[:, cc], W2[:, cc], start=cc == 0, stop=cc == KH2 - 1)
                    i.then_inc(y_ready, 1)

                def step(t, n, more):
                    if more:
                        front(t + 1, 1 - n)
                    back(t, n)

                steps(pe.Fori, lambda: front(0, 0), step)

    def router(self):
        nc, a = self.nc, self.a
        with ExitStack() as c:
            def sb(name, shape, dt=F32):
                return c.enter_context(nc.sbuf_tensor(f"r_{name}", shape, dt))

            def sem(name):
                return c.enter_context(nc.semaphore(f"r_{name}"))
            GW = sb("gate", [P, DC, E])
            N2 = sb("n2", [P, DC])
            XF = sb("xf", [P, 2, D])
            XT = sb("xt", [P, 2, DC, P])
            LG = sb("logits", [P, NT, E])
            RK = sb("rank", [P, NT, E])
            M = sb("m", [P, NT])
            w_in, gate_ready, xf_ready = sem("w_in"), sem("gate_ready"), sem("xf_ready")
            t_ready, t_evac, l_ready, l_used = sem("xt_psum"), sem("xt_sbuf"), sem("logits_psum"), sem("logits_used")
            e_in, e_out, step = sem("exp_in"), sem("exp_out"), sem("step")
            block = c.enter_context(nc.Block())
            tb = [self.PS[:, n, 0:DC * P] for n in range(2)]
            lb = [self.PS[:, 2 + n, 0:E] for n in range(2)]

            @block.sync
            def _(sp):
                sp.dma_start(GW[:], a["E_gate"].rearrange("(c p) e -> p c e", p=P)).then_inc(w_in, 16)
                sp.dma_start(N2[:], a["E_n2"]).then_inc(w_in, 16)

            @block.tensor
            def _(pe):
                pe.wait_ge(gate_ready, DC)
                with pe.Fori(0, NT // 2) as j:
                    for n in range(2):
                        t = 2 * j + n
                        pe.wait_ge(xf_ready, t + 1)
                        pe.wait_ge(t_evac, 2 * j)
                        for cc in range(DC):
                            i = nc.tensor.transpose(tb[n][:, cc * P:(cc + 1) * P], XF[:, n, cc * P:(cc + 1) * P], self.IDF[:])
                        i.then_inc(t_ready, 1)
                        pe.wait_ge(t_evac, t + 1)
                        pe.wait_ge(l_used, 2 * j)
                        for cc in range(DC):
                            i = nc.tensor.matmul(lb[n], XT[:, n, cc], GW[:, cc], start=cc == 0, stop=cc == DC - 1)
                        i.then_inc(l_ready, 1)

            @block.scalar
            def _(act):
                with act.Fori(0, NT // 2) as j:
                    for n in range(2):
                        t = 2 * j + n
                        act.wait_ge(t_ready, t + 1)
                        act.wait_ge(l_ready, 2 * j)
                        nc.scalar.activation(XT[:, n], tb[n].rearrange("p (c q) -> p c q", c=DC), ACT.Copy).then_inc(t_evac, 1)
                act.wait_ge(e_in, 1)
                nc.scalar.activation(LG[:], LG[:], ACT.Exp).then_inc(e_out, 1)

            @block.vector
            def _(dve):
                v = nc.vector
                dve.wait_ge(w_in, 32)
                for cc in range(DC):
                    v.tensor_scalar(GW[:, cc], GW[:, cc], N2[:, cc:cc + 1], None, ALU.mult).then_inc(gate_ready, 1)
                with dve.Fori(0, NT // 2) as j:
                    for n in range(2):
                        t = 2 * j + n
                        dve.wait_ge(t_ready, 2 * j)
                        v.tensor_scalar(XF[:, n, :], self.X[:, sl(t, 1), :].rearrange("p o d -> p (o d)"),
                                        self.RSTD[:, sl(t, 1)], None, ALU.mult).then_inc(xf_ready, 1)
                    for n in range(2):
                        t = 2 * j + n
                        dve.wait_ge(l_ready, t + 1)
                        v.tensor_scalar(LG[:, sl(t, 1), :].rearrange("p o e -> p (o e)"), lb[n], 1.0, None, ALU.mult).then_inc(l_used, 1)
                dve.wait_ge(l_used, NT)
                k = [0]

                def link(ins):
                    k[0] += 1
                    ins.then_inc(step, 1)
                    dve.wait_ge(step, k[0])

                def wide(col):
                    return col[:, :, None].broadcast_to((P, NT, E))
                big = 3.4028234663852886e38
                link(v.tensor_scalar(LG[:], LG[:], big, -big, ALU.min, ALU.max))
                link(v.tensor_reduce(M[:], LG[:], AX.X, ALU.max))
                v.tensor_tensor(LG[:], LG[:], wide(M), ALU.subtract).then_inc(e_in, 1)
                dve.wait_ge(e_out, 1)
                link(v.tensor_reduce(M[:], LG[:], AX.X, ALU.add))
                link(v.reciprocal(M[:], M[:]))
                link(v.tensor_tensor(LG[:], LG[:], wide(M), ALU.mult))
                link(v.memset(RK[:], 0.0))
                for lo in range(E):
                    for hi in range(lo + 1, E):
                        link(v.tensor_tensor(M[:], LG[:, :, lo], LG[:, :, hi], ALU.is_ge))
                        link(v.tensor_tensor(RK[:, :, hi], RK[:, :, hi], M[:], ALU.add))
                        link(v.tensor_scalar(M[:], M[:], -1.0, 1.0, ALU.mult, ALU.add))
                        link(v.tensor_tensor(RK[:, :, lo], RK[:, :, lo], M[:], ALU.add))
                link(v.tensor_scalar(RK[:], RK[:], 2.0, None, ALU.is_lt))
                link(v.tensor_tensor(LG[:], LG[:], RK[:], ALU.mult))
                link(v.tensor_reduce(M[:], LG[:], AX.X, ALU.add))
                link(v.tensor_scalar(M[:], M[:], 1e-8, None, ALU.add))
                link(v.reciprocal(M[:], M[:]))
                link(v.tensor_tensor(LG[:], LG[:], wide(M), ALU.mult))
                link(v.tensor_scalar(self.WTS[:], LG[:], self.TG[:, 3:4], None, ALU.mult))

    def experts(self):
        nc, a = self.nc, self.a
        NG, TG_ = NT // 4, 4
        first = {"e2_l1", "e3_down", "e0_up", "e1_w1", "e1_w2"}
        layers = [("e2_l1", None, 0), ("e3_down", None, 1), ("e2_l2", 0, 2), ("e3_up", 1, 3), ("e2_l3", 2, 0),
                  ("e0_up", None, 1), ("e1_w1", None, 2), ("e1_w2", None, 2)]
        blocks = {"e2_l1": 4, "e3_down": 2, "e2_l2": 4, "e3_up": 4, "e2_l3": 4, "e0_up": 4, "e1_w1": 4, "e1_w2": 4}
        chunks = {n: DC if n in first else 4 for n in blocks}
        chunks["e3_up"] = 2
        outs = [("e2_l4", 0, 2), ("e3_out", 3, 3), ("e0_down", 1, 0), ("e1_down", 2, 1)]
        NBLK = sum(blocks.values())
        RING = 5
        with ExitStack() as c:
            def sb(name, shape, dt=F32):
                return c.enter_context(nc.sbuf_tensor(f"e_{name}", shape, dt))

            def sem(name):
                return c.enter_context(nc.semaphore(f"e_{name}"))
            W = {n: sb(n, [P, chunks[n], blocks[n] * P]) for n in blocks}
            WO = {n: sb(n, [P, 4, MW]) for n, _, _ in outs}
            N2 = sb("n2", [P, DC])
            XF = sb("xf", [P, TG_, D])
            XT = sb("xt", [P, 2, DC, 512])
            HB = [sb(f"hidden{n}", [P, 4, 512]) for n in range(4)]
            Y = sb("y", [P, 2, TG_, D])
            w_in, w_ready, xf_ready = sem("w_in"), sem("w_ready"), sem("xf_ready")
            t_ready, t_evac = sem("xt_psum"), sem("xt_sbuf")
            blk_ready, blk_used = sem("block_psum"), sem("block_used")
            o_ready, o_used = sem("out_psum"), sem("out_used")
            y_in = [sem(f"y_in{n}") for n in range(2)]
            y_out = [sem(f"y_out{n}") for n in range(2)]
            block = c.enter_context(nc.Block())
            ring = [self.PS[:, n, :] for n in range(RING)]
            ob = [self.PS[:, RING + n, 0:MW] for n in range(2)]
            tb = self.PS[:, 7, :]
            assert NBLK % RING == 0
            N_W = len(blocks) + len(outs) + 1

            def steps(loop, step):
                with loop(0, NG // 2) as j:
                    for n in range(2):
                        step(2 * j + n, j, n)

            @block.sync
            def _(sp):
                sp.dma_start(N2[:], a["E_n2"]).then_inc(w_in, 16)
                for n in blocks:
                    sp.dma_start(W[n][:], a["E_" + n].rearrange("(c p) h -> p c h", p=P)).then_inc(w_in, 16)
                for n, _, _ in outs:
                    sp.dma_start(WO[n][:], a["E_" + n][:, M0:].rearrange("(c p) h -> p c h", p=P)).then_inc(w_in, 16)

                def load(g, j, n):
                    sp.dma_start(Y[:, n], self.out_rows[:, sl(4 * g, 4), :]).then_inc(y_in[n], 16)

                def step(g, j, n):
                    sp.wait_ge(y_out[n], 16 * j)
                    load(g, j, n)
                    sp.wait_ge(o_used, 16 * g + 16)
                    sp.dma_start(self.out_rows[:, sl(4 * g, 4), :], Y[:, n]).then_inc(y_out[n], 16)

                steps(sp.Fori, step)
                for n in range(2):
                    sp.wait_ge(y_out[n], 16 * (NG // 2))

            @block.vector
            def _(dve):
                v = nc.vector
                dve.wait_ge(w_in, 16 * N_W)
                for n in ("e2_l1", "e3_down", "e0_up", "e1_w1", "e1_w2"):
                    for cc in range(DC):
                        v.tensor_scalar(W[n][:, cc], W[n][:, cc], N2[:, cc:cc + 1], None, ALU.mult).then_inc(w_ready, 1)

                def norm(g):
                    dve.wait_ge(t_evac, DC * g)
                    for t in range(TG_):
                        i = v.tensor_scalar(XF[:, t], self.X[:, sl(4 * g + t, 1), :].rearrange("p o d -> p (o d)"),
                                            self.RSTD[:, sl(4 * g + t, 1)], None, ALU.mult)
                    i.then_inc(xf_ready, 1)

                def step(g, j, n):
                    norm(g)
                    for b in range(blocks["e1_w2"]):
                        at = NBLK - 4 + b
                        dve.wait_ge(blk_ready, NBLK * g + at + 1)
                        dve.wait_ge(blk_used, NBLK * g + NBLK - 4 + b)
                        v.tensor_tensor(HB[2][:, b], HB[2][:, b], ring[at % RING], ALU.mult).then_inc(blk_used, 1)
                    dve.wait_ge(y_in[n], 16 * (j + 1))
                    m = 0
                    for name, buf, e in outs:
                        for t in range(TG_):
                            dve.wait_ge(o_ready, 16 * g + m + 1)
                            if m >= TG_:
                                dve.wait_ge(o_used, 16 * g + m - TG_ + 1)
                            v.scalar_tensor_tensor(Y[:, n, t, M0:D], ob[m % 2], self.WTS[:, sl(4 * g + t, 1), e],
                                                   Y[:, n, t, M0:D], ALU.mult, ALU.add).then_inc(o_used, 1)
                            m += 1

                steps(dve.Fori, step)

            @block.scalar
            def _(act):
                s_ = nc.scalar

                def step(g, j, n):
                    for cc in range(DC):
                        act.wait_ge(t_ready, DC * g + cc + 1)
                        s_.activation(XT[:, n, cc], tb, ACT.Copy).then_inc(t_evac, 1)
                    at = 0
                    for name, _, buf in layers[:-1]:
                        for b in range(blocks[name]):
                            act.wait_ge(blk_ready, NBLK * g + at + 1)
                            s_.activation(HB[buf][:, b], ring[at % RING], ACT.Silu if name == "e1_w1" else ACT.Gelu).then_inc(blk_used, 1)
                            at += 1
                    act.wait_ge(blk_used, NBLK * g + NBLK)

                steps(act.Fori, step)

            @block.tensor
            def _(pe):
                mm = nc.tensor.matmul
                pe.wait_ge(w_ready, 10)

                def step(g, j, n):
                    pe.wait_ge(xf_ready, g + 1)
                    for cc in range(DC):
                        pe.wait_ge(t_evac, DC * g + cc)
                        for t in range(TG_):
                            i = nc.tensor.transpose(tb[:, t * P:(t + 1) * P], XF[:, t, cc * P:(cc + 1) * P], self.IDF[:])
                        i.then_inc(t_ready, 1)
                    pe.wait_ge(t_evac, DC * g + DC)
                    at = 0
                    done_at = {}
                    for name, src, buf in layers:
                        if src is not None:
                            pe.wait_ge(blk_used, NBLK * g + done_at[src])
                        for b in range(blocks[name]):
                            if at >= RING:
                                pe.wait_ge(blk_used, NBLK * g + at - RING + 1)
                            for cc in range(chunks[name]):
                                rhs = XT[:, n, cc] if src is None else HB[src][:, cc]
                                i = mm(ring[at % RING], W[name][:, cc, b * P:(b + 1) * P], rhs, start=cc == 0, stop=cc == chunks[name] - 1)
                            i.then_inc(blk_ready, 1)
                            at += 1
                        done_at[buf] = at
                    m = 0
                    for name, buf, e in outs:
                        pe.wait_ge(blk_used, NBLK * g + done_at[buf])
                        for t in range(TG_):
                            pe.wait_ge(o_used, 16 * g + max(m - 1, 0))
                            for cc in range(4):
                                i = mm(ob[m % 2], HB[buf][:, cc, t * P:(t + 1) * P], WO[name][:, cc], start=cc == 0, stop=cc == 3)
                            i.then_inc(o_ready, 1)
                            m += 1

                steps(pe.Fori, step)


def kernel(**inputs):
    import numpy as _np
    import concourse.bacc as _bacc
    from concourse import mybir as _mybir
    from concourse.bass_utils import run_bass_kernel_spmd as _run

    g = {k: _np.asarray(v) for k, v in inputs.items()}
    rep = P // DK

    def t(name):
        return _np.ascontiguousarray(g[name].T)

    lay = {
        "x": g["x"],
        "ctx_t": _np.ascontiguousarray(g["ctx_1024"].transpose(0, 2, 1)),
        "g_xattn": g["g_xattn"], "g_ffn": g["g_ffn"],
        "L0_xattn_Wq": g["L0_xattn_Wq"], "L0_xattn_Wo": g["L0_xattn_Wo"],
        "A_wkv": _np.concatenate([_np.tile(g["L0_xattn_Wk"], (1, rep)), g["L0_xattn_Wv"]], axis=1),
        "A_part_bias": _np.stack([g["L0_xattn_bq"][:P], g["L0_xattn_bq"][P:], _np.tile(g["L0_xattn_bk"], rep)], axis=1),
        "A_free_bias": _np.concatenate([g["L0_xattn_bo"], g["L0_xattn_bv"]]),
        "B_w1": t("L0_ffn_w1"), "B_w2": t("L0_ffn_w2"),
        "L0_ffn_norm1_w": g["L0_ffn_norm1_w"], "L0_ffn_norm2_w": g["L0_ffn_norm2_w"],
        "L0_ffn_act_scale": g["L0_ffn_act_scale"], "L0_ffn_act_bias": g["L0_ffn_act_bias"],
        "C_wq": t("L1_xattn_Wq"), "C_wc": t("L1_xattn_Wc"),
        "C_wkv": _np.concatenate([_np.tile(g["L1_xattn_Wkv"][:DK].T, (1, rep)), g["L1_xattn_Wkv"][DK:].T], axis=1),
        "D_wq": t("L1_ffn_wq"), "D_wk": t("L1_ffn_wk"), "D_wv": t("L1_ffn_wv"), "D_wo": t("L1_ffn_wo"),
        "D_part_w": _np.stack([_np.tile(g["L1_ffn_qn_w"], rep), _np.tile(g["L1_ffn_kn_w"], rep)], axis=1),
        "L1_ffn_n1_w": g["L1_ffn_n1_w"],
        "E_gate": t("L1_ffn_gate_w"),
        "E_n2": _np.ascontiguousarray(g["L1_ffn_n2_w"].reshape(DC, P).T),
    }
    for n in ("e0_up", "e0_down", "e1_w1", "e1_w2", "e1_down", "e2_l1", "e2_l2", "e2_l3", "e2_l4", "e3_down", "e3_up", "e3_out"):
        lay["E_" + n] = t("L1_ffn_" + n)

    nc = _bacc.Bacc("TRN2", target_bir_lowering=False, num_devices=1)
    arrays, args = {}, {}
    for name, v in lay.items():
        v = _np.ascontiguousarray(v)
        arrays[f"in_{name}_dram"] = v
        args[name] = nc.dram_tensor(f"in_{name}_dram", v.shape, _mybir.dt.from_np(v.dtype), kind="ExternalInput").ap()
    out = nc.dram_tensor("out_0_dram", (B, S, D), _mybir.dt.float32, kind="ExternalOutput").ap()
    Kernel(nc, args, out).build()
    r = _run(nc, [arrays], core_ids=[0])
    return r.results[0]["out_0_dram"]
```

```python
import concourse.bass as bass
from concourse import mybir
from contextlib import ExitStack

F32 = mybir.dt.float32
BF16 = mybir.dt.bfloat16
U32 = mybir.dt.uint32
ALU = mybir.AluOpType
ACT = mybir.ActivationFunctionType
AX = mybir.AxisListType

P = 128
B, S, D = 32, 256, 256
NT = B * S // P
H, DK = 16, 16
DC = D // P
HID1 = 1024
M0 = 64
MW = D - M0
E = 4
LN_EPS, EPS_NORM, EPS_Q, EPS_RMS = 1e-5, 1e-8, 1e-5, 1.1920929e-07
RND = 12582912.0
NEG = -1e30
Q_PART = (0, 0, 0, 1, 1, 2)
K_PART = (0, 1, 2, 0, 1, 0)
KR = 16 * len(Q_PART)


def sl(i, n):
    return bass.ds(i, n)


class Kernel:

    def __init__(self, nc, a, out):
        self.nc, self.a, self.out = nc, a, out
        self.x_rows = a["x"].rearrange("b (t p) d -> p (b t) d", p=P)
        self.out_rows = out.rearrange("b (t p) d -> p (b t) d", p=P)

    def build(self):
        nc = self.nc
        with ExitStack() as c:
            def sb(name, shape, dt=F32):
                return c.enter_context(nc.sbuf_tensor(name, shape, dt))
            self.X = sb("x_all", [P, NT, D])
            self.ST = sb("row_stats", [P, NT, 6])
            self.MEAN = sb("mean", [P, NT])
            self.RSTD = sb("rstd", [P, NT])
            self.RRMS = sb("rrms", [P, NT])
            self.WTS = sb("wts", [P, NT, E])
            self.TG = sb("tanh_gates", [P, 4])
            self.IDF = sb("ident_f", [P, P])
            self.IDB = sb("ident_b", [P, P], BF16)
            self.PS = c.enter_context(nc.psum_tensor("psum", [P, 8, 512], F32))
            self.q_dram = nc.dram_tensor("q_parts", (2, 3, DK, H, S), BF16, kind="Internal").ap()
            self.k_dram = nc.dram_tensor("k_parts", (2, 3, DK, H, S), BF16, kind="Internal").ap()
            self.k1_dram = nc.dram_tensor("k1_parts", (2, 3, DK, S), BF16, kind="Internal").ap()
            self.nm_dram = nc.dram_tensor("max_parts", (2, 3, 32, P), BF16, kind="Internal").ap()
            self.np_step, self.np_var, self.np_root = [c.enter_context(nc.semaphore(f"np_{name}"))
                                                       for name in ("step", "var_ready", "root_ready")]
            self.np_steps, self.np_roots = 0, 0
            self.load_phase()
            self.norm_params("a", LN_EPS, None)
            self.attention("A")
            self.norm_params("b", LN_EPS, EPS_NORM)
            self.bit_ffn()
            self.norm_params("c", LN_EPS, None)
            self.attention("C")
            self.norm_params("d", LN_EPS, EPS_RMS)
            self.attention("D")
            self.norm_params("e", EPS_RMS, None, raw=True)
            self.router()
            self.experts()

    def load_phase(self):
        nc, a = self.nc, self.a
        with ExitStack() as c:
            def sem(name):
                return c.enter_context(nc.semaphore("ld_" + name))
            x_in = [sem(f"x_in{n}") for n in range(4)]
            gates_in, ident, stats, gates = sem("gates_in"), sem("ident"), sem("stats"), sem("gates")
            G = c.enter_context(nc.sbuf_tensor("gates_raw", [P, 4], F32))
            block = c.enter_context(nc.Block())
            n4 = NT // 4

            @block.sync
            def _(sp):
                for n in range(4):
                    sp.dma_start(self.X[:, n * n4:(n + 1) * n4, :], self.x_rows[:, n * n4:(n + 1) * n4, :]).then_inc(x_in[n], 16)
                sp.dma_start(G[:, 0:2], a["g_xattn"][None, :].broadcast_to((P, 2))).then_inc(gates_in, 16)
                sp.dma_start(G[:, 2:4], a["g_ffn"][None, :].broadcast_to((P, 2))).then_inc(gates_in, 16)

            @block.gpsimd
            def _(pool):
                nc.gpsimd.memset(self.IDF[:], 0.0).then_inc(ident, 1)
                nc.gpsimd.memset(self.IDB[:], 0.0).then_inc(ident, 1)
                pool.wait_ge(ident, 2)
                for m in (self.IDF, self.IDB):
                    nc.gpsimd.affine_select(out=m[:], in_=m[:], compare_op=ALU.not_equal, fill=1.0, base=0,
                                            pattern=[[-1, P]], channel_multiplier=1).then_inc(ident, 1)
                pool.wait_ge(ident, 4)

            @block.scalar
            def _(act):
                act.wait_ge(gates_in, 32)
                nc.scalar.activation(self.TG[:], G[:], ACT.Tanh).then_inc(gates, 1)
                act.wait_ge(gates, 1)

            @block.vector
            def _(dve):
                for n in range(4):
                    dve.wait_ge(x_in[n], 16)
                    with dve.Fori(n * n4, (n + 1) * n4) as t:
                        nc.vector.bn_stats(self.ST[:, sl(t, 1), :].rearrange("p o s -> p (o s)"),
                                           self.X[:, sl(t, 1), :].rearrange("p o d -> p (o d)")).then_inc(stats, 1)
                dve.wait_ge(stats, NT)

    def norm_params(self, tag, eps, rms_eps, raw=False):
        nc = self.nc
        with ExitStack() as c:
            step, sq_in, sq_out = self.np_step, self.np_var, self.np_root
            n, roots_before = [self.np_steps], self.np_roots
            V = c.enter_context(nc.sbuf_tensor(f"np{tag}_v", [P, NT], F32))
            T = c.enter_context(nc.sbuf_tensor(f"np{tag}_t", [P, NT], F32))
            R = c.enter_context(nc.sbuf_tensor(f"np{tag}_r", [P, NT], F32))
            U = c.enter_context(nc.sbuf_tensor(f"np{tag}_u", [P, NT], F32))
            block = c.enter_context(nc.Block())
            st, n_roots = self.ST, 1 if rms_eps is None else 2
            v = nc.vector

            @block.vector
            def _(dve):
                def link(ins):
                    n[0] += 1
                    ins.then_inc(step, 1)
                    dve.wait_ge(step, n[0])

                def rsqrt(out, root, k):
                    v.tensor_scalar(U[:], R[:], 0.0, None, ALU.add).then_inc(sq_in, 1)
                    dve.wait_ge(sq_out, roots_before + k)
                    link(v.reciprocal(out[:], root[:]))
                    link(v.tensor_tensor(U[:], out[:], out[:], ALU.mult))
                    link(v.tensor_tensor(U[:], U[:], R[:], ALU.mult))
                    link(v.tensor_scalar(U[:], U[:], -0.5, 1.5, ALU.mult, ALU.add))
                    link(v.tensor_tensor(out[:], out[:], U[:], ALU.mult))

                link(v.tensor_tensor(self.MEAN[:], st[:, :, 1], st[:, :, 4], ALU.add))
                link(v.tensor_scalar(self.MEAN[:], self.MEAN[:], 0.5, None, ALU.mult))
                link(v.tensor_tensor(T[:], st[:, :, 1], st[:, :, 4], ALU.subtract))
                link(v.tensor_tensor(T[:], T[:], T[:], ALU.mult))
                link(v.tensor_tensor(V[:], st[:, :, 2], st[:, :, 5], ALU.add))
                link(v.tensor_scalar(V[:], V[:], 1.0 / D, None, ALU.mult))
                link(v.tensor_scalar(T[:], T[:], 0.25, None, ALU.mult))
                link(v.tensor_tensor(V[:], V[:], T[:], ALU.add))
                if raw:
                    link(v.tensor_tensor(T[:], self.MEAN[:], self.MEAN[:], ALU.mult))
                    link(v.tensor_tensor(V[:], V[:], T[:], ALU.add))
                link(v.tensor_scalar(R[:], V[:], eps, None, ALU.add))
                rsqrt(self.RSTD, T, 1)
                if rms_eps is not None:
                    link(v.tensor_tensor(R[:], V[:], self.RSTD[:], ALU.mult))
                    link(v.tensor_tensor(R[:], R[:], self.RSTD[:], ALU.mult))
                    link(v.tensor_scalar(R[:], R[:], rms_eps, None, ALU.add))
                    rsqrt(self.RRMS, T, 2)
                    link(v.tensor_tensor(self.RRMS[:], self.RRMS[:], self.RSTD[:], ALU.mult))

            @block.scalar
            def _(act):
                for k in range(n_roots):
                    act.wait_ge(sq_in, roots_before + k + 1)
                    nc.scalar.activation(T[:], R[:], ACT.Sqrt).then_inc(sq_out, 1)

            self.np_steps, self.np_roots = n[0], roots_before + n_roots

    def attention(self, kind):
        nc, a = self.nc, self.a
        mha, gathered = kind == "D", kind == "C"
        L = kind.lower()
        with ExitStack() as c:
            def sb(name, shape, dt=F32):
                return c.enter_context(nc.sbuf_tensor(f"{L}_{name}", shape, dt))

            def sem(name):
                return c.enter_context(nc.semaphore(f"{L}_{name}"))

            OW = MW if mha else D
            QW = 3 * D if mha else D
            Wq = sb("wq", [P, DC, QW])
            Wo = sb("wo", [P, DC, OW])
            KVW = P + DK
            Wkv = None if mha else sb("wkv", [P, DC, KVW])
            CTX = None if mha else sb("ctx", [P, 2, DC, S])
            PB = sb("part_bias", [P, 3])
            FB = sb("free_bias", [P, D + DK])
            XN = sb("xn", [P, 2, D])
            XNT = sb("xnt", [P, DC, S])
            nk = 4 if mha else 3
            QF = sb("qf", [P, nk, S])
            QR = sb("q_rest", [P, nk, S])
            QP = sb("q_parts", [P, 2, 3, nk, S], BF16)
            QS = sb("q_stack", [KR + 3, 2, H, S], BF16)
            KS = sb("k_stack", [KR + 3, 2, H if mha else 1, S], BF16)
            VH = H if mha else 1
            VW = 32
            VS = sb("v_staged", [P, 2, VH, DK])
            VP = sb("v_ones", [P, 2, 2, VH, VW])
            NM = sb("neg_max", [P, 2 * H])
            NMR = sb("neg_max_rest", [P, 2 * H])
            NMS = sb("neg_max_parts", [P, 3, 2 * H], BF16)
            NMT = sb("neg_max_t", [3 * 2 * H, 2, P], BF16)
            EX = sb("exps", [P, 8, 2, 512])
            OV = sb("o_raw", [P, 2, 512])
            REC = sb("rec", [P, 16])
            HOLD = sb("hold", [P, 1])
            POOL_HOLD = sb("pool_hold", [P, 1])
            O = sb("o", [P, 2, D])
            OT = sb("o_t", [P, DC, S])
            if gathered:
                MX = sb("mx8", [P, 2, 8])
                IX = sb("ix8", [P, 2, 8], U32)
                IXF = sb("ixf", [P, 2])
                IOTA = sb("iota", [P, S])
                OH = sb("onehot", [P, 2, S], BF16)
                OHT = sb("onehot_t", [P, 2, S])
                KVP = sb("kvp", [P, 2, KVW])
            if mha:
                QK = sb("qk", [P, 2, 2 * D])
                SQ = sb("qk_sq", [P, 2 * D])
                MS = sb("qk_ms", [P, 2, 32])
                RT = sb("qk_root", [P, 2, 32])
                HALF = sb("minus_half", [P, 64])
                MASKQ = sb("mask_q", [P, 2, S], BF16)
                MASKK = sb("mask_k", [P, 2, 2, S], BF16)
                XR = sb("x1", [P, 2, D])
                YB = sb("y", [P, 2, D])

            W_, PVB = self.PS[:, 0, :], self.PS[:, 1, :]
            WB = self.PS[:, 0, :].bitcast(BF16)
            W2 = W_.rearrange("p (m s) -> p m s", m=2)
            sc_slot = [self.PS[:, 2 + n, :] for n in range(2)]
            st_slot = [self.PS[:, 4 + 2 * n:6 + 2 * n, :] for n in range(2)]

            w_in, consts = sem("weights_in"), sem("consts")
            ctx_in = [] if mha else [sem(f"ctx_in{n}") for n in range(2)]
            xn_ready = sem("xn_ready")
            work_full, work_free = sem("work_full"), sem("work_free")
            rounded, rest_ready, parts_ready = sem("parts_rounded"), sem("rest_ready"), sem("parts_ready")
            v_ready = sem("v_ready")
            parts_out = [sem(f"parts_out{n}") for n in range(2)]
            stack_in = [sem(f"stack_in{n}") for n in range(2)]
            scores_ready, scores_used = sem("scores_ready"), sem("scores_used")
            nms_ready, nm_step = sem("neg_max_parts_ready"), sem("neg_max_step")
            nm_out = [sem(f"neg_max_out{n}") for n in range(2)]
            nm_in = [sem(f"neg_max_in{n}") for n in range(2)]
            st_ready, exp_ready, pv_done, ov_ready = sem("scores_t_ready"), sem("exp_ready"), sem("pv_done"), sem("o_raw_ready")
            rec_ready, stats = sem("rec_ready"), sem("stats")
            if not mha:
                kf_ready = sem("kf_ready")
            if kind != "A":
                prep_step = sem("prep_step")
            if kind == "A":
                x_biased = sem("x_plus_bias")
            if mha:
                w_scaled, y_ready, y_out = sem("w_scaled"), sem("y_ready"), sem("y_out")
                ms_ready, xr_ready, rt_ready = sem("ms_ready"), sem("xr_ready"), sem("rt_ready")

            NPREP = 3 if kind == "A" else 6
            ITEMS = {0: ["T1-", "p0"], 1: ["OT-", "p1"], 2: ["PR-", "p2"], 3: ["p3"], 4: ["p4"], 5: ["p5", "T0"], 6: [], 7: ["NM"]}
            if kind == "A":
                ITEMS = {g: [x for x in v if x not in ("p3", "p4", "p5")] for g, v in ITEMS.items()}
            SPLIT_AT = {"A": 2, "C": 5, "D": 5}[kind]
            V_ITEM = {"A": "p2", "C": "p5", "D": "p3"}[kind]
            H_AT = {2: (0, 1, 2), 3: (3, 4, 5), 4: (6, 7, 8), 5: (9, 10, 11), 6: (12, 13, 14, 15)}
            FIRST, LAST = 2, B - 2

            def items(i, g):
                out = []
                for x in ITEMS[g]:
                    if isinstance(i, int):
                        if x[-1] == "-" and i == 0 or x[0] == "p" and i + 2 >= B or x == "NM" and i + 1 >= B:
                            continue
                    out.append(x)
                return out

            number = {}
            for b in range(2):
                for k in range(NPREP):
                    number[b - 2, f"p{k}"] = len(number)
            number[-1, "NM"] = len(number)
            for i in range(B):
                for g in range(8):
                    for x in items(i, g):
                        number[i, x] = len(number)
            for x in ("T1-", "OT-", "PR-"):
                number[B, x] = len(number)
            NBODY = sum(len(v) for v in ITEMS.values())
            for x in sum(ITEMS.values(), []):
                assert number[LAST - 1, x] == number[FIRST, x] + (LAST - 1 - FIRST) * NBODY

            def nth(i, x):
                return number[i, x] if isinstance(i, int) else number[FIRST, x] + (i - FIRST) * NBODY

            N_CONST = {"A": 5, "C": 6, "D": 10}[kind]
            NPO = 12 if mha else 7
            NSI = 6
            NW = {"A": 5, "C": 3, "D": 7}[kind]
            block = c.enter_context(nc.Block())

            def at(i, d, j, n):
                m = n + d
                return i + d, j + m // 2, m % 2

            def steps(loop, prologue, step, tail):
                prologue()
                for i in range(FIRST):
                    step(i, i // 2, i % 2)
                with loop(FIRST // 2, LAST // 2) as j:
                    for n in range(2):
                        step(2 * j + n, j, n)
                for i in range(LAST, B):
                    step(i, i // 2, i % 2)
                tail()

            def known(b, least):
                return not (isinstance(b, int) and b < least)

            @block.sync
            def _(sp):
                if kind == "A":
                    sp.dma_start(Wq[:], a["L0_xattn_Wq"].rearrange("(c p) e -> p c e", p=P)).then_inc(w_in, 16)
                    sp.dma_start(Wo[:], a["L0_xattn_Wo"].rearrange("(c p) e -> p c e", p=P)).then_inc(w_in, 16)
                    sp.dma_start(Wkv[:], a["A_wkv"].rearrange("(c p) e -> p c e", p=P)).then_inc(w_in, 16)
                    sp.dma_start(PB[:], a["A_part_bias"]).then_inc(w_in, 16)
                    sp.dma_start(FB[:], a["A_free_bias"][None, :].broadcast_to((P, D + DK))).then_inc(w_in, 16)
                elif kind == "C":
                    sp.dma_start(Wq[:], a["C_wq"].rearrange("(c p) e -> p c e", p=P)).then_inc(w_in, 16)
                    sp.dma_start(Wo[:], a["C_wc"].rearrange("(c p) e -> p c e", p=P)).then_inc(w_in, 16)
                    sp.dma_start(Wkv[:], a["C_wkv"].rearrange("(c p) e -> p c e", p=P)).then_inc(w_in, 16)
                else:
                    for n in range(3):
                        sp.dma_start(Wq[:, :, n * D:(n + 1) * D],
                                     a[f"D_w{'qkv'[n]}"].rearrange("(c p) e -> p c e", p=P)).then_inc(w_in, 16)
                    sp.dma_start(Wo[:], a["D_wo"][:, M0:].rearrange("(c p) e -> p c e", p=P)).then_inc(w_in, 16)
                    sp.dma_start(PB[:, 0:2], a["D_part_w"]).then_inc(w_in, 16)
                    sp.dma_start(PB[:, 2:3], a["L1_ffn_n1_w"][0:P][:, None]).then_inc(w_in, 16)
                    sp.dma_start(FB[:, 0:1], a["L1_ffn_n1_w"][P:D][:, None]).then_inc(w_in, 16)

                def ctx(b, j, n):
                    if mha:
                        return
                    if known(b, 2):
                        sp.wait_ge(parts_ready, b - 1)
                    sp.dma_start(CTX[:, n, :, :], a["ctx_t"][sl(b, 1)].rearrange("o (c p) s -> p (o c) s", p=P)).then_inc(ctx_in[n], 16)

                def parts(b, j, n):
                    sp.wait_ge(parts_ready, b + 1)
                    for m in range(2):
                        heads = slice(m * H // 2, (m + 1) * H // 2)
                        for t in range(3):
                            sp.dma_start(self.q_dram[n, t, :, heads].rearrange("d h s -> h d s"), QP[:, n, t, m, :]).then_inc(parts_out[n], 16)
                            if mha:
                                sp.dma_start(self.k_dram[n, t, :, heads].rearrange("d h s -> h d s"), QP[:, n, t, 2 + m, :]).then_inc(parts_out[n], 16)
                    if not mha:
                        sp.dma_start(self.k1_dram[n].rearrange("t d s -> d t s"), QP[0:DK, n, :, 2, :]).then_inc(parts_out[n], 16)

                def stack(b, j, n, pieces):
                    if 0 in pieces:
                        sp.wait_ge(parts_out[n], 16 * NPO * (j + 1))
                    qd = self.q_dram[n].rearrange("t d h s -> t d (h s)")
                    qs = QS[:, n, :, :].rearrange("r h s -> r (h s)")
                    for k in pieces:
                        copies, row = (3, 2, 1)[k], (0, 48, 80)[k]
                        sp.dma_start(qs[row:row + 16 * copies, :], qd[k][None].broadcast_to((copies, DK, H * S))).then_inc(stack_in[n], 16)
                        if mha:
                            kd = self.k_dram[n].rearrange("t d h s -> (t d) (h s)")
                            sp.dma_start(KS[row:row + 16 * copies, n, :, :].rearrange("r h s -> r (h s)"), kd[0:16 * copies]).then_inc(stack_in[n], 16)
                        else:
                            kd = self.k1_dram[n].rearrange("t d s -> (t d) s")
                            sp.dma_start(KS[row:row + 16 * copies, n, 0, :], kd[0:16 * copies]).then_inc(stack_in[n], 16)

                def neg_max_out(b, j, n, w):
                    sp.wait_ge(work_free, w + 1)
                    sp.dma_start(self.nm_dram[n].rearrange("t u q -> (t u) q"), NMT[:, n, :]).then_inc(nm_out[n], 16)

                def neg_max_in(b, j, n):
                    sp.wait_ge(nm_out[n], 16 * (j + 1))
                    sp.dma_start(QS[KR:KR + 3, n, :, :].rearrange("t h s -> t (h s)"),
                                 self.nm_dram[n].rearrange("t u q -> t (u q)")).then_inc(nm_in[n], 16)

                def y_store(b):
                    sp.wait_ge(y_ready, b + 1)
                    sp.dma_start(self.out_rows[:, sl(2 * b, 2), :], YB[:]).then_inc(y_out, 16)

                def prologue():
                    ctx(0, 0, 0)
                    ctx(1, 0, 1)
                    for b in range(2):
                        parts(b, 0, b)
                        stack(b, 0, b, (0, 1, 2))
                    neg_max_out(0, 0, 0, nth(-1, "NM"))
                    neg_max_in(0, 0, 0)

                def step(i, j, n):
                    prep, maxes = known(i, 0) and not (isinstance(i, int) and i + 2 >= B), not (isinstance(i, int) and i + 1 >= B)
                    nxt, nxt2 = at(i, 1, j, n), at(i, 2, j, n)
                    if prep:
                        ctx(*nxt2)
                    if mha and known(i, 1):
                        y_store(i - 1)
                    if prep and not mha:
                        parts(*nxt2)
                    if maxes:
                        neg_max_out(*nxt, nth(i, "NM"))
                    if prep and not mha:
                        stack(*nxt2, (0,))
                    if maxes:
                        neg_max_in(*nxt)
                    if prep and not mha:
                        stack(*nxt2, (1, 2))
                    if prep and mha:
                        parts(*nxt2)
                        stack(*nxt2, (0, 1, 2))

                def tail():
                    if mha:
                        y_store(B - 1)
                        sp.wait_ge(y_out, 16 * B)

                steps(sp.Fori, prologue, step, tail)

            @block.gpsimd
            def _(pool):
                cn = [0]

                def const(ins):
                    cn[0] += 1
                    ins.then_inc(consts, 1)
                    pool.wait_ge(consts, cn[0])

                const(nc.gpsimd.memset(VP[:], 0.0))
                const(nc.gpsimd.memset(VP[:, :, :, :, DK:DK + 1], 1.0))
                const(nc.gpsimd.memset(POOL_HOLD[:], 0.0))
                const(nc.gpsimd.memset(QR[:], 0.0))
                const(nc.gpsimd.memset(KS[KR:KR + 3, :, :, :], 1.0))
                if gathered:
                    const(nc.gpsimd.iota(IOTA[:], [[1, S]], base=0, channel_multiplier=0, allow_small_or_imprecise_dtypes=True))
                if mha:
                    const(nc.gpsimd.memset(HALF[:], -0.5))
                    const(nc.gpsimd.memset(MASKQ[:], 0.0))
                    const(nc.gpsimd.memset(MASKK[:], 0.0))
                    const(nc.gpsimd.affine_select(out=MASKQ[:], in_=MASKQ[:], compare_op=ALU.is_ge, fill=NEG, base=0,
                                                  pattern=[[P, 2], [-1, S]], channel_multiplier=1))
                    const(nc.gpsimd.affine_select(out=MASKK[:].rearrange("p c h q -> p (c h) q"),
                                                  in_=MASKK[:].rearrange("p c h q -> p (c h) q"),
                                                  compare_op=ALU.is_ge, fill=NEG, base=0,
                                                  pattern=[[0, 4], [1, S]], channel_multiplier=-1))
                if kind == "A":
                    pool.wait_ge(w_in, 16 * NW)
                    const(nc.gpsimd.tensor_scalar(FB[:, 0:D], FB[:, 0:D], self.TG[:, 0:1], None, ALU.mult))
                g = nc.gpsimd

                def prep(b, j, n, w):
                    if mha:
                        pool.wait_ge(ms_ready, b + 1)
                        g.tensor_tensor(RT[:].rearrange("p t h -> p (t h)"), MS[:].rearrange("p t h -> p (t h)"), HALF[:], ALU.pow).then_inc(rt_ready, 1)
                    if kind == "A":
                        pool.wait_ge(xn_ready, b + 1)
                        g.tensor_tensor(self.X[:, sl(2 * b, 2), :], self.X[:, sl(2 * b, 2), :],
                                        FB[:, None, 0:D].broadcast_to((P, 2, D)), ALU.add).then_inc(x_biased, 1)
                    pool.wait_ge(rounded, 2 * b + 1)
                    g.tensor_tensor(QR[:], QF[:], QP[:, n, 0], ALU.subtract).then_inc(rest_ready, 1)
                    pool.wait_ge(rounded, 2 * b + 2)
                    g.tensor_tensor(QP[:, n, 2], QR[:], QP[:, n, 1], ALU.subtract).then_inc(parts_ready, 1)
                    pool.wait_ge(work_free, w + 1)
                    if known(b, 2):
                        pool.wait_ge(pv_done, 2 * (b - 1))
                    g.tensor_tensor(POOL_HOLD[:], POOL_HOLD[:], POOL_HOLD[:], ALU.add)
                    g.tensor_copy(VP[:, n, :, :, 0:DK], VS[:]).then_inc(v_ready, 1)

                def prologue():
                    for b in range(2):
                        prep(b, 0, b, nth(b - 2, V_ITEM))

                def step(i, j, n):
                    if not (isinstance(i, int) and i + 2 >= B):
                        prep(*at(i, 2, j, n), nth(i, V_ITEM))

                steps(pool.Fori, prologue, step, lambda: None)

            @block.scalar
            def _(act):
                s_ = nc.scalar
                s_.preload_act_table(ACT.Exp)
                act.wait_ge(w_in, 16 * NW)
                if mha:
                    act.wait_ge(w_scaled, 3)

                def evac(w, out, in_):
                    act.wait_ge(work_full, w + 1)
                    s_.activation(out, in_, ACT.Copy).then_inc(work_free, 1)

                def prep(k, b, w):
                    if k == 0:
                        evac(w, XNT[:], W2)
                    elif not mha and k == 1:
                        act.wait_ge(work_full, w + 1)
                        if known(b, 1):
                            act.wait_ge(parts_ready, b)
                        if kind == "A":
                            s_.activation(QF[:, 0], W2[:, 0], ACT.Identity, bias=PB[:, 0:1])
                            s_.activation(QF[:, 1], W2[:, 1], ACT.Identity, bias=PB[:, 1:2]).then_inc(work_free, 1)
                        else:
                            s_.activation(QF[:, 0:2], W2, ACT.Copy, scale=DK ** -0.5).then_inc(work_free, 1)
                    elif kind == "A":
                        act.wait_ge(work_full, w + 1)
                        s_.activation(QF[:, 2], W_[:, 0:S], ACT.Identity, bias=PB[:, 2:3]).then_inc(kf_ready, 1)
                    elif gathered and k == 3:
                        evac(w, OHT[:], WB[:, 0:2 * S].rearrange("p (m s) -> p m s", m=2))
                    elif gathered and k == 4:
                        evac(w, KVP[:], W_[:, 0:2 * KVW].rearrange("p (m s) -> p m s", m=2))
                    elif gathered and k == 5:
                        act.wait_ge(work_full, w + 1)
                        s_.activation(QF[:, 2], W_[:, 0:S], ACT.Copy).then_inc(kf_ready, 1)
                    elif mha and k in (1, 2):
                        evac(w, QK[:, k - 1], W_)
                    elif mha and k == 3:
                        act.wait_ge(work_full, w + 1)
                        if known(b, 1):
                            act.wait_ge(v_ready, b)
                        s_.activation(VS[:], W_.rearrange("p (c h d) -> p c h d", c=2, h=H), ACT.Copy).then_inc(work_free, 1)
                    elif mha and k in (4, 5):
                        act.wait_ge(work_full, w + 1)
                        if known(b, 1):
                            act.wait_ge(parts_ready, b)
                        s_.activation(QF[:, 2 * (k - 4):2 * (k - 4) + 2], W2, ACT.Copy, scale=PB[:, k - 4:k - 3]).then_inc(work_free, 1)

                def split_high(b, j, n, w):
                    if mha:
                        act.wait_ge(work_free, w + 1)
                    else:
                        act.wait_ge(kf_ready, b + 1)
                    if known(b, 2):
                        act.wait_ge(parts_out[n], 16 * NPO * j)
                    s_.activation(QP[:, n, 0], QF[:], ACT.Copy).then_inc(rounded, 1)

                def split_mid(b, n):
                    act.wait_ge(rest_ready, b + 1)
                    s_.activation(QP[:, n, 1], QR[:], ACT.Copy).then_inc(rounded, 1)

                def exps(b, g):
                    act.wait_ge(st_ready, 8 * b + g + 1)
                    if g % 4 == 0 and known(b, 1):
                        act.wait_ge(pv_done, 2 * b - 1 + g // 4)
                    if mha:
                        s_.activation(EX[:, g].rearrange("p c f -> p (c f)")[:, 0:768],
                                      st_slot[g % 2].rearrange("p c f -> p (c f)")[:, 0:768], ACT.Exp).then_inc(exp_ready, 1)
                    else:
                        s_.activation(EX[:, g], st_slot[g % 2], ACT.Exp).then_inc(exp_ready, 1)

                def raw_half(b, k):
                    act.wait_ge(pv_done, 2 * b + k + 1)
                    s_.activation(OV[:, k], PVB, ACT.Copy).then_inc(ov_ready, 1)

                def item(x, i):
                    if x[0] == "p":
                        prep(int(x[1]), i + 2, nth(i, x))
                    elif x == "OT-":
                        evac(nth(i, x), OT[:], W2)

                def prologue():
                    for b in range(2):
                        for k in range(NPREP):
                            prep(k, b, nth(b - 2, f"p{k}"))
                        split_high(b, 0, b, nth(b - 2, f"p{NPREP - 1}"))
                        split_mid(b, b)

                def step(i, j, n):
                    b, jj, nn = at(i, 2, j, n)
                    more = not (isinstance(i, int) and i + 2 >= B)
                    for g in range(8):
                        exps(i, g)
                        if g == 4:
                            raw_half(i, 0)
                        for x in items(i, g):
                            item(x, i)
                        if more and g == SPLIT_AT:
                            split_high(b, jj, nn, nth(i, f"p{NPREP - 1}"))
                        if more and g == SPLIT_AT + 1:
                            split_mid(b, nn)
                    raw_half(i, 1)

                steps(act.Fori, prologue, step, lambda: item("OT-", B))

            @block.vector
            def _(dve):
                v = nc.vector
                dve.wait_ge(w_in, 16 * NW)
                dve.wait_ge(consts, N_CONST)
                if mha:
                    v.tensor_scalar(Wq[:, 0], Wq[:, 0], PB[:, 2:3], None, ALU.mult).then_inc(w_scaled, 1)
                    v.tensor_scalar(Wq[:, 1], Wq[:, 1], FB[:, 0:1], None, ALU.mult).then_inc(w_scaled, 1)
                    v.tensor_scalar(PB[:, 0:1], PB[:, 0:1], DK ** -0.5, None, ALU.mult).then_inc(w_scaled, 1)
                    dve.wait_ge(w_scaled, 3)
                v_part = W_[:, S:S + 2 * DK].rearrange("p (c d) -> p c d", c=2)

                def norm(b, w_before):
                    if w_before is not None:
                        dve.wait_ge(work_free, w_before + 1)
                    r = self.RRMS if mha else self.RSTD
                    for t in range(2):
                        i = v.tensor_scalar(XN[:, t, :], self.X[:, sl(2 * b + t, 1), :].rearrange("p o d -> p (o d)"),
                                            self.MEAN[:, sl(2 * b + t, 1)], r[:, sl(2 * b + t, 1)], ALU.subtract, ALU.mult)
                    i.then_inc(xn_ready, 1)

                def prep(k, b, w):
                    if kind == "A" and k == 2 or gathered and k == 5:
                        dve.wait_ge(kf_ready, b + 1)
                        if known(b, 1):
                            dve.wait_ge(v_ready, b)
                        if kind == "A":
                            v.tensor_tensor(VS[:, :, 0, :], v_part, FB[:, None, D:D + DK].broadcast_to((P, 2, DK)), ALU.add).then_inc(work_free, 1)
                        else:
                            v.tensor_copy(VS[:, :, 0, :], v_part).then_inc(work_free, 1)
                    if gathered and k == 2:
                        dve.wait_ge(work_full, w + 1)
                        v.tensor_copy(HOLD[:], W_[:, 0:1])
                        for t in range(2):
                            i = v.max(MX[:, t], W_[:, t * S:(t + 1) * S])
                        i.then_inc(prep_step, 1)
                        dve.wait_ge(prep_step, 3 * b + 1)
                        v.tensor_copy(HOLD[:], MX[:, 0, 0:1])
                        for t in range(2):
                            i = v.max_index(IX[:, t], MX[:, t], W_[:, t * S:(t + 1) * S])
                        i.then_inc(work_free, 1)
                        dve.wait_ge(work_free, w + 1)
                        v.tensor_copy(IXF[:], IX[:, :, 0]).then_inc(prep_step, 1)
                        dve.wait_ge(prep_step, 3 * b + 2)
                        for t in range(2):
                            i = v.tensor_scalar(OH[:, t], IOTA[:], IXF[:, t:t + 1], None, ALU.is_equal)
                        i.then_inc(prep_step, 1)
                    if mha and k in (1, 2):
                        t = k - 1
                        dve.wait_ge(work_free, w + 1)
                        v.tensor_tensor(SQ[:], QK[:, t], QK[:, t], ALU.mult).then_inc(prep_step, 1)
                        dve.wait_ge(prep_step, 6 * b + 2 * t + 1)
                        v.tensor_reduce(MS[:, t], SQ[:].rearrange("p (h d) -> p h d", d=DK), AX.X, ALU.add).then_inc(prep_step, 1)
                        dve.wait_ge(prep_step, 6 * b + 2 * t + 2)
                        if t == 1:
                            v.tensor_scalar(MS[:], MS[:], 1.0 / DK, EPS_RMS, ALU.mult, ALU.add).then_inc(ms_ready, 1)
                    if mha and k == 3:
                        dve.wait_ge(rt_ready, b + 1)
                        for t in range(2):
                            v.tensor_tensor(QK[:, t].rearrange("p (h d) -> p h d", d=DK),
                                            QK[:, t].rearrange("p (h d) -> p h d", d=DK),
                                            RT[:, t, :, None].broadcast_to((P, 32, DK)), ALU.mult).then_inc(prep_step, 1)

                def row_max(b, h):
                    dve.wait_ge(scores_ready, H * b + h + 1)
                    v.tensor_reduce(NM[:, 2 * h:2 * h + 2], sc_slot[h % 2].rearrange("p (t k) -> p t k", t=2),
                                    AX.X, ALU.max, negate=True).then_inc(scores_used, 1)

                def neg_max(b, j, n, w):
                    dve.wait_ge(scores_used, H * (b + 1))
                    v.tensor_copy(NMS[:, 0], NM[:]).then_inc(nm_step, 1)
                    dve.wait_ge(nm_step, 3 * b + 1)
                    v.tensor_tensor(NMR[:], NM[:], NMS[:, 0], ALU.subtract).then_inc(nm_step, 1)
                    dve.wait_ge(nm_step, 3 * b + 2)
                    v.tensor_copy(NMS[:, 1], NMR[:]).then_inc(nm_step, 1)
                    dve.wait_ge(nm_step, 3 * b + 3)
                    v.tensor_tensor(NMS[:, 2], NMR[:], NMS[:, 1], ALU.subtract).then_inc(nms_ready, 1)
                    dve.wait_ge(work_full, w + 1)
                    if known(b, 2):
                        dve.wait_ge(nm_out[n], 16 * j)
                    v.tensor_copy(NMT[:, n, :], WB[0:3 * 2 * H, 0:P]).then_inc(work_free, 1)

                def half(b, k, w):
                    dve.wait_ge(work_full, w + 1)
                    pv = W_.rearrange("p (h t j e) -> p h t j e", h=2, t=2, j=4)
                    rec = REC[:].rearrange("p (h t j) -> p h t j", h=2, t=2)
                    v.reciprocal(rec.rearrange("p h t j -> p (h t) j"), pv.rearrange("p h t j e -> p (h t) j e")[:, :, :, DK]).then_inc(rec_ready, 1)
                    dve.wait_ge(rec_ready, 2 * b + k + 1)
                    for t in range(2):
                        i = v.tensor_tensor(O[:, t, k * P:(k + 1) * P].rearrange("p (h j d) -> p h j d", h=2, j=4), pv[:, :, t, :, 0:DK],
                                            rec[:, :, t, :, None].broadcast_to((P, 2, 4, DK)), ALU.mult)
                    i.then_inc(work_free, 1)

                def post(b, w):
                    xs = self.X[:, sl(2 * b, 2), :]
                    if not mha:
                        dve.wait_ge(work_full, w + 1)
                        if kind == "A":
                            dve.wait_ge(x_biased, b + 1)
                        gate = self.TG[:, 0:1] if kind == "A" else self.TG[:, 1:2]
                        v.scalar_tensor_tensor(xs, W2, gate, xs, ALU.mult, ALU.add).then_inc(work_free, 1)
                        dve.wait_ge(work_free, w + 1)
                        src = [self.X[:, sl(2 * b + t, 1), :].rearrange("p o d -> p (o d)") for t in range(2)]
                    else:
                        for t in range(2):
                            i = v.tensor_scalar(XR[:, t, :], self.X[:, sl(2 * b + t, 1), :].rearrange("p o d -> p (o d)"),
                                                self.MEAN[:, sl(2 * b + t, 1)], self.RSTD[:, sl(2 * b + t, 1)], ALU.subtract, ALU.mult)
                        i.then_inc(xr_ready, 1)
                        dve.wait_ge(xr_ready, b + 1)
                        dve.wait_ge(work_full, w + 1)
                        v.tensor_tensor(XR[:, :, M0:D], XR[:, :, M0:D], W_[:, 0:2 * MW].rearrange("p (t d) -> p t d", t=2), ALU.add).then_inc(work_free, 1)
                        dve.wait_ge(work_free, w + 1)
                        if known(b, 1):
                            dve.wait_ge(y_out, 16 * b)
                        v.scalar_tensor_tensor(YB[:], XR[:], self.TG[:, 3:4], xs, ALU.mult, ALU.add).then_inc(y_ready, 1)
                        dve.wait_ge(y_ready, b + 1)
                        v.tensor_scalar(xs, XR[:], 1.0, None, ALU.mult)
                        src = [XR[:, t, :] for t in range(2)]
                    for t in range(2):
                        v.bn_stats(self.ST[:, sl(2 * b + t, 1), :].rearrange("p o s -> p (o s)"), src[t]).then_inc(stats, 1)

                def item(x, i, j, n):
                    w = nth(i, x)
                    if x[0] == "p":
                        prep(int(x[1]), i + 2, w)
                    elif x in ("T0", "T1-"):
                        half(i - 1 if x == "T1-" else i, int(x[1]), w)
                    elif x == "NM":
                        neg_max(*at(i, 1, j, n), w)
                    elif x == "PR-":
                        post(i - 1, w)

                def prologue():
                    for b in range(2):
                        norm(b, None if b == 0 else nth(-2, "p0"))
                        for k in range(NPREP):
                            prep(k, b, nth(b - 2, f"p{k}"))
                    for h in range(H):
                        row_max(0, h)
                    neg_max(0, 0, 0, nth(-1, "NM"))

                def step(i, j, n):
                    if not (isinstance(i, int) and i + 2 >= B):
                        norm(i + 2, nth(i - 1, "p0"))
                    for g in range(8):
                        if g in H_AT and not (isinstance(i, int) and i + 1 >= B):
                            for h in H_AT[g]:
                                row_max(i + 1, h)
                        for x in items(i, g):
                            item(x, i, j, n)

                def tail():
                    for x in ("T1-", "OT-", "PR-"):
                        item(x, B, B // 2, 0)
                    dve.wait_ge(stats, 2 * B)

                steps(dve.Fori, prologue, step, tail)

            @block.tensor
            def _(pe):
                mm, tr = nc.tensor.matmul, nc.tensor.transpose
                pe.wait_ge(w_in, 16 * NW)
                pe.wait_ge(consts, N_CONST)
                if mha:
                    pe.wait_ge(w_scaled, 3)

                def use(w):
                    if known(w, 1):
                        pe.wait_ge(work_free, w)

                def transpose_rows(src, off=0):
                    for cc in range(DC):
                        for t in range(2):
                            i = tr(W_[:, cc * S + t * P:cc * S + (t + 1) * P], src[:, t, off + cc * P:off + (cc + 1) * P], self.IDF[:])
                    i.then_inc(work_full, 1)

                def prep(k, b, j, n, w):
                    if k == 0:
                        pe.wait_ge(xn_ready, b + 1)
                        use(w)
                        transpose_rows(XN)
                        return
                    use(w)
                    if not mha and k == 1:
                        for m in range(2):
                            for cc in range(DC):
                                i = mm(W_[:, m * S:(m + 1) * S], Wq[:, cc, m * P:(m + 1) * P], XNT[:, cc], start=cc == 0, stop=cc == DC - 1)
                    elif kind == "A":
                        pe.wait_ge(ctx_in[n], 16 * (j + 1))
                        for cc in range(DC):
                            mm(W_[:, 0:S], Wkv[:, cc, 0:P], CTX[:, n, cc], start=cc == 0, stop=cc == DC - 1)
                        for m in range(2):
                            for cc in range(DC):
                                i = mm(W_[:, S + m * DK:S + (m + 1) * DK], CTX[:, n, cc, m * P:(m + 1) * P], Wkv[:, cc, P:P + DK], start=cc == 0, stop=cc == DC - 1)
                    elif gathered and k == 2:
                        pe.wait_ge(ctx_in[n], 16 * (j + 1))
                        for t in range(2):
                            for cc in range(DC):
                                i = mm(W_[:, t * S:(t + 1) * S], QF[:, cc, t * P:(t + 1) * P], CTX[:, n, cc], start=cc == 0, stop=cc == DC - 1)
                    elif gathered and k == 3:
                        pe.wait_ge(prep_step, 3 * b + 3)
                        for m in range(2):
                            for t in range(2):
                                i = tr(WB[:, m * S + t * P:m * S + (t + 1) * P], OH[:, t, m * P:(m + 1) * P], self.IDB[:])
                    elif gathered and k == 4:
                        for m in range(2):
                            for cc in range(DC):
                                i = mm(W_[:, m * KVW:(m + 1) * KVW], CTX[:, n, cc, m * P:(m + 1) * P], Wkv[:, cc], start=cc == 0, stop=cc == DC - 1)
                    elif gathered and k == 5:
                        for m in range(2):
                            mm(W_[:, 0:S], KVP[:, m, 0:P], OHT[:, m], start=m == 0, stop=m == 1)
                        for t in range(2):
                            for m in range(2):
                                i = mm(W_[:, S + t * DK:S + (t + 1) * DK], OHT[:, m, t * P:(t + 1) * P], KVP[:, m, P:P + DK], start=m == 0, stop=m == 1)
                    elif mha and k in (1, 2):
                        for cc in range(DC):
                            i = mm(W_[:, :], XNT[:, cc, (k - 1) * P:k * P], Wq[:, cc, 0:2 * D], start=cc == 0, stop=cc == DC - 1)
                    elif mha and k == 3:
                        for t in range(2):
                            for cc in range(DC):
                                i = mm(W_[:, t * S:(t + 1) * S], XNT[:, cc, t * P:(t + 1) * P], Wq[:, cc, 2 * D:3 * D], start=cc == 0, stop=cc == DC - 1)
                    elif mha:
                        if k == 4:
                            pe.wait_ge(prep_step, 6 * b + 6)
                        transpose_rows(QK, (k - 4) * D)
                        return
                    i.then_inc(work_full, 1)

                def scores(b, j, n, h):
                    if h == 0:
                        pe.wait_ge(stack_in[n], 16 * NSI * (j + 1))
                    if isinstance(b, int) and b == 0:
                        if h >= 2:
                            pe.wait_ge(scores_used, h - 1)
                    else:
                        pe.wait_ge(scores_used, H * b + h - 1)
                    if mha:
                        mm(sc_slot[h % 2], self.IDB[:], MASKQ[:].rearrange("p t k -> p (t k)"), start=True, stop=True, skip_group_check=True)
                    for t in range(2):
                        i = mm(sc_slot[h % 2][:, t * S:(t + 1) * S], QS[0:KR, n, h, t * P:(t + 1) * P], KS[0:KR, n, h if mha else 0, :],
                               start=not mha, stop=True, skip_group_check=mha)
                    i.then_inc(scores_ready, 1)

                def scores_t(b, j, n, g):
                    if g == 0:
                        pe.wait_ge(nm_in[n], 16 * (j + 1))
                    if not (isinstance(b, int) and b == 0 and g < 2):
                        pe.wait_ge(exp_ready, 8 * b + g - 1)
                    slot = st_slot[g % 2]
                    if not mha:
                        for k in range(2):
                            i = mm(slot[:, k, :], KS[:, n, 0, k * P:(k + 1) * P], QS[:, n, 2 * g:2 * g + 2, :], start=True, stop=True)
                    else:
                        mm(slot[:, 0, :], self.IDB[:], MASKK[:, 0].rearrange("p h q -> p (h q)"), start=True, stop=True, skip_group_check=True)
                        for h in range(2):
                            mm(slot[:, 0, h * S:(h + 1) * S], KS[:, n, 2 * g + h, 0:P], QS[:, n, 2 * g + h, :], start=False, stop=True, skip_group_check=True)
                        mm(slot[:, 1, 0:S].rearrange("p (h q) -> p h q", h=2), self.IDB[:], MASKK[:, 1, :, 0:P], start=True, stop=True, skip_group_check=True)
                        for h in range(2):
                            i = mm(slot[:, 1, h * P:(h + 1) * P], KS[:, n, 2 * g + h, P:S], QS[:, n, 2 * g + h, P:S], start=False, stop=True, skip_group_check=True)
                    i.then_inc(st_ready, 1)

                def values(b, n, half):
                    pe.wait_ge(exp_ready, 8 * b + 4 * half + 4)
                    if half == 0:
                        pe.wait_ge(v_ready, b + 1)
                    if known(b, 1) or half:
                        pe.wait_ge(ov_ready, 2 * b + half)
                    tiles = [PVB[VW * j:VW * (j + 1), :] for j in range(4)]
                    if not mha:
                        for k in range(2):
                            for j in range(4):
                                i = mm(tiles[j], VP[:, n, k, 0, :], EX[:, 4 * half + j, k, :], start=k == 0, stop=k == 1)
                    else:
                        for h in range(2):
                            for j in range(4):
                                i = mm(tiles[j][:, h * S:(h + 1) * S], VP[:, n, 0, 2 * (4 * half + j) + h, :],
                                       EX[:, 4 * half + j, 0, h * S:(h + 1) * S], start=h == 0, stop=True, skip_group_check=True)
                        for h in range(2):
                            for j in range(4):
                                i = mm(tiles[j][:, h * S + P:(h + 1) * S], VP[:, n, 1, 2 * (4 * half + j) + h, :],
                                       EX[:, 4 * half + j, 1, h * P:(h + 1) * P], start=False, stop=True, skip_group_check=True)
                    i.then_inc(pv_done, 1)

                def item(x, i, j, n):
                    w = nth(i, x)
                    if x[0] == "p":
                        prep(int(x[1]), *at(i, 2, j, n), w)
                    elif x in ("T0", "T1-"):
                        k = int(x[1])
                        b = i - 1 if x == "T1-" else i
                        pe.wait_ge(ov_ready, 2 * b + k + 1)
                        use(w)
                        for u in range(4):
                            t_ = tr(W_[:, u * P:(u + 1) * P], OV[:, k, u * P:(u + 1) * P], self.IDF[:])
                        t_.then_inc(work_full, 1)
                    elif x == "OT-":
                        use(w)
                        transpose_rows(O)
                    elif x == "PR-":
                        use(w)
                        for t in range(2):
                            for cc in range(DC):
                                t_ = mm(W_[:, t * OW:(t + 1) * OW], OT[:, cc, t * P:(t + 1) * P], Wo[:, cc], start=cc == 0, stop=cc == DC - 1)
                        t_.then_inc(work_full, 1)
                    elif x == "NM":
                        pe.wait_ge(nms_ready, i + 2)
                        use(w)
                        tr(WB[0:3 * 2 * H, 0:P], NMS[:].rearrange("p t u -> p (t u)"), self.IDB[:]).then_inc(work_full, 1)

                def prologue():
                    for b in range(2):
                        for k in range(NPREP):
                            prep(k, b, 0, b, nth(b - 2, f"p{k}"))
                    for h in range(H):
                        scores(0, 0, 0, h)
                    item("NM", -1, -1, 1)

                def step(i, j, n):
                    for g in range(8):
                        scores_t(i, j, n, g)
                        if g in H_AT and not (isinstance(i, int) and i + 1 >= B):
                            for h in H_AT[g]:
                                scores(*at(i, 1, j, n), h)
                        if g == 4:
                            values(i, n, 0)
                        for x in items(i, g):
                            item(x, i, j, n)
                    values(i, n, 1)

                def tail():
                    for x in ("T1-", "OT-", "PR-"):
                        item(x, B, B // 2, 0)

                steps(pe.Fori, prologue, step, tail)

    def bit_ffn(self):
        nc, a = self.nc, self.a
        KH1, KH2 = DC, HID1 // P
        with ExitStack() as c:
            def sb(name, shape, dt=F32):
                return c.enter_context(nc.sbuf_tensor(f"b_{name}", shape, dt))

            def sem(name):
                return c.enter_context(nc.semaphore(f"b_{name}"))
            WF = sb("w_float", [P, 2, KH1 * HID1])
            W1 = sb("w1", [P, KH1, HID1], BF16)
            W2 = sb("w2", [P, KH2, D], BF16)
            N1 = sb("n1", [P, D])
            N2 = sb("n2", [P, HID1])
            AB = sb("act_scale_bias", [P, 2])
            ONES = sb("ones", [P, P])
            WS = sb("w_sum", [P, 1])
            WM = sb("w_mean", [P, 2])
            WI = sb("w_scale", [P, 2])
            WG = sb("w2_mean_gate", [P, 1])
            XB = sb("xb", [P, D])
            QA = sb("qa", [P, D])
            QB = sb("qb", [P, D], BF16)
            QT = sb("qt", [P, KH1, P], BF16)
            S1 = sb("s1", [P, 4])
            C1 = sb("c1", [P, 2])
            R = sb("r", [P, 2, HID1])
            G = sb("g", [P, HID1])
            SQ = sb("sq", [P, HID1])
            S2 = sb("s2", [P, 12])
            MSQ = sb("msq", [P, 1])
            Y2 = sb("y2", [P, HID1])
            Q2 = sb("q2", [P, HID1])
            Q2B = sb("q2b", [P, HID1], BF16)
            Q2T = sb("q2t", [P, KH2, P], BF16)
            C2 = sb("c2", [P, 1])
            PS = self.PS
            TB = PS[:, 0, 0:P].bitcast(BF16)
            HB = [PS[:, 1 + 2 * n:3 + 2 * n, :] for n in range(2)]
            T2B = PS[:, 5, :].bitcast(BF16)
            YB = PS[:, 6, 0:D]
            SB = PS[:, 7, 0:1]
            W2_COLS = PS[:, 1:5, :].rearrange("p k f -> p (k f)")

            w_in, ones, sums, w_sum, w_ready = sem("w_in"), sem("ones"), sem("sums"), sem("w_sum"), sem("w_ready")
            q_ready, qt_ready, qt_evac = sem("q_ready"), sem("qt_psum"), sem("qt_sbuf")
            h_ready, r_ready, g_ready, sq_ready = sem("h_ready"), sem("relu_ready"), sem("g_ready"), sem("sum_sq_ready")
            ms_ready, root_ready = sem("ms_ready"), sem("root_ready")
            q2_ready, q2t_ready, q2t_evac, y_ready, y_used = sem("q2_ready"), sem("q2t_psum"), sem("q2t_sbuf"), sem("y_ready"), sem("y_used")
            c1_ready, r_used, setup, front_step, back_step, stats = sem("c1_ready"), sem("relu_used"), sem("setup"), sem("front_step"), sem("back_step"), sem("stats")
            block = c.enter_context(nc.Block())

            def steps(loop, prologue, step):
                prologue()
                with loop(0, NT // 2 - 1) as j:
                    for n in range(2):
                        step(2 * j + n, n, True)
                step(NT - 2, 0, True)
                step(NT - 1, 1, False)

            @block.sync
            def _(sp):
                sp.dma_start(WF[:, 0, :].rearrange("p (c h) -> p c h", c=KH1), a["B_w1"].rearrange("(c p) h -> p c h", p=P)).then_inc(w_in, 16)
                sp.dma_start(WF[:, 1, :].rearrange("p (c h) -> p c h", c=KH2), a["B_w2"].rearrange("(c p) h -> p c h", p=P)).then_inc(w_in, 16)
                sp.dma_start(N1[:], a["L0_ffn_norm1_w"][None, :].broadcast_to((P, D))).then_inc(w_in, 16)
                sp.dma_start(N2[:], a["L0_ffn_norm2_w"][None, :].broadcast_to((P, HID1))).then_inc(w_in, 16)
                sp.dma_start(AB[:, 0:1], a["L0_ffn_act_scale"][None, :].broadcast_to((P, 1))).then_inc(w_in, 16)
                sp.dma_start(AB[:, 1:2], a["L0_ffn_act_bias"][None, :].broadcast_to((P, 1))).then_inc(w_in, 16)

            @block.gpsimd
            def _(pool):
                nc.gpsimd.memset(ONES[:], 1.0).then_inc(ones, 1)

            @block.scalar
            def _(act):
                s_ = nc.scalar
                act.wait_ge(w_in, 16 * 6)
                s_.activation(R[:].rearrange("p n h -> p (n h)"), WF[:, 1, :], ACT.Abs).then_inc(sums, 1)

                def front(t, n):
                    act.wait_ge(qt_ready, t + 1)
                    s_.activation(QT[:], TB.rearrange("p (c q) -> p c q", c=KH1), ACT.Copy).then_inc(qt_evac, 1)
                    act.wait_ge(c1_ready, t + 1)
                    act.wait_ge(h_ready, t + 1)
                    if not (isinstance(t, int) and t < 2):
                        act.wait_ge(g_ready, t - 1)
                    s_.activation(R[:, n].rearrange("p (k f) -> p k f", k=2), HB[n], ACT.Relu, scale=C1[:, n:n + 1]).then_inc(r_ready, 1)

                def back(t, n):
                    act.wait_ge(g_ready, t + 1)
                    s_.activation(SQ[:], G[:], ACT.Square, bias=AB[:, 1:2], accum_out=MSQ[:]).then_inc(sq_ready, 1)
                    act.wait_ge(ms_ready, t + 1)
                    s_.activation(S2[:, 1:2], S2[:, 0:1], ACT.Sqrt).then_inc(root_ready, 1)
                    act.wait_ge(q2t_ready, t + 1)
                    s_.activation(Q2T[:], T2B.rearrange("p (c q) -> p c q", c=KH2), ACT.Copy).then_inc(q2t_evac, 1)

                def step(t, n, more):
                    if more:
                        front(t + 1, 1 - n)
                    back(t, n)

                steps(act.Fori, lambda: front(0, 0), step)

            @block.vector
            def _(dve):
                v = nc.vector
                k0 = [0]

                def setup_link(ins):
                    k0[0] += 1
                    ins.then_inc(setup, 1)
                    dve.wait_ge(setup, k0[0])

                dve.wait_ge(w_in, 16 * 6)
                v.tensor_reduce(WS[:], WF[:, 0, :], AX.X, ALU.add, apply_absolute_value=True).then_inc(sums, 1)
                dve.wait_ge(w_sum, 1)
                setup_link(v.tensor_reduce(WM[:, 1:2], W2_COLS, AX.X, ALU.add))
                setup_link(v.tensor_copy(WM[:, 0:1], SB))
                setup_link(v.tensor_scalar(WM[:], WM[:], 1.0 / (D * HID1), EPS_Q, ALU.mult, ALU.max))
                setup_link(v.reciprocal(WI[:], WM[:]))
                setup_link(v.tensor_scalar(WG[:], WM[:, 1:2], self.TG[:, 2:3], None, ALU.mult))
                for w, wq in ((0, W1), (1, W2)):
                    setup_link(v.tensor_scalar(WF[:, w, :], WF[:, w, :], WI[:, w:w + 1], RND, ALU.mult, ALU.add))
                    setup_link(v.tensor_scalar(WF[:, w, :], WF[:, w, :], RND, 1.0, ALU.subtract, ALU.min))
                    v.tensor_scalar(wq[:].rearrange("p c h -> p (c h)"), WF[:, w, :], -1.0, None, ALU.max).then_inc(w_ready, 1)

                NF, NB = 7, 9
                k = [0]

                def flink(t, ins):
                    k[0] += 1
                    ins.then_inc(front_step, 1)
                    dve.wait_ge(front_step, NF * t + k[0])

                def blink(t, ins):
                    k[0] += 1
                    ins.then_inc(back_step, 1)
                    dve.wait_ge(back_step, NB * t + k[0])

                def front(t, n):
                    k[0] = 0
                    flink(t, v.tensor_scalar(XB[:], self.X[:, sl(t, 1), :].rearrange("p o d -> p (o d)"),
                                             self.MEAN[:, sl(t, 1)], self.RRMS[:, sl(t, 1)], ALU.subtract, ALU.mult))
                    flink(t, v.tensor_tensor(XB[:], XB[:], N1[:], ALU.mult))
                    flink(t, v.tensor_reduce(S1[:, 0:1], XB[:], AX.X, ALU.max, apply_absolute_value=True))
                    flink(t, v.tensor_scalar(S1[:, 1:2], S1[:, 0:1], EPS_Q, None, ALU.max))
                    flink(t, v.reciprocal(S1[:, 3:4], S1[:, 1:2]))
                    flink(t, v.tensor_scalar(S1[:, 2:3], S1[:, 3:4], 127.0, None, ALU.mult))
                    flink(t, v.tensor_scalar(QA[:], XB[:], S1[:, 2:3], RND, ALU.mult, ALU.add))
                    if not (isinstance(t, int) and t == 0):
                        dve.wait_ge(qt_ready, t)
                    v.tensor_scalar(QB[:], QA[:], RND, None, ALU.subtract).then_inc(q_ready, 1)
                    if not (isinstance(t, int) and t < 2):
                        dve.wait_ge(r_ready, t - 1)
                    v.tensor_scalar(C1[:, n:n + 1], S1[:, 1:2], 1.0 / 127.0, WM[:, 0:1], ALU.mult, ALU.mult).then_inc(c1_ready, 1)

                def back(t, n):
                    k[0] = 0
                    dve.wait_ge(r_ready, t + 1)
                    if not (isinstance(t, int) and t == 0):
                        dve.wait_ge(sq_ready, t)
                    v.scalar_tensor_tensor(G[:], R[:, n], AB[:, 0:1], R[:, n], ALU.mult, ALU.mult).then_inc(g_ready, 1)
                    dve.wait_ge(g_ready, t + 1)
                    blink(t, v.scalar_tensor_tensor(Y2[:], G[:], AB[:, 1:2], N2[:], ALU.add, ALU.mult))
                    blink(t, v.tensor_reduce(S2[:, 2:3], Y2[:], AX.X, ALU.max, apply_absolute_value=True))
                    dve.wait_ge(sq_ready, t + 1)
                    v.tensor_scalar(S2[:, 0:1], MSQ[:], 1.0 / HID1, EPS_NORM, ALU.mult, ALU.add).then_inc(ms_ready, 1)
                    dve.wait_ge(root_ready, t + 1)
                    blink(t, v.reciprocal(S2[:, 3:4], S2[:, 1:2]))
                    blink(t, v.tensor_scalar(S2[:, 4:5], S2[:, 3:4], S2[:, 3:4], S2[:, 0:1], ALU.mult, ALU.mult))
                    blink(t, v.tensor_scalar(S2[:, 4:5], S2[:, 4:5], -0.5, 1.5, ALU.mult, ALU.add))
                    blink(t, v.tensor_scalar(S2[:, 5:6], S2[:, 4:5], S2[:, 3:4], None, ALU.mult))
                    blink(t, v.tensor_scalar(S2[:, 6:7], S2[:, 2:3], S2[:, 5:6], EPS_Q, ALU.mult, ALU.max))
                    blink(t, v.reciprocal(S2[:, 7:8], S2[:, 6:7]))
                    blink(t, v.tensor_scalar(S2[:, 8:9], S2[:, 7:8], 127.0, S2[:, 5:6], ALU.mult, ALU.mult))
                    v.tensor_scalar(Q2[:], Y2[:], S2[:, 8:9], RND, ALU.mult, ALU.add).then_inc(stats, 1)
                    dve.wait_ge(stats, 3 * t + 1)
                    if not (isinstance(t, int) and t == 0):
                        dve.wait_ge(q2t_ready, t)
                    v.tensor_scalar(Q2B[:], Q2[:], RND, None, ALU.subtract).then_inc(q2_ready, 1)
                    v.tensor_scalar(C2[:], S2[:, 6:7], 1.0 / 127.0, WG[:, 0:1], ALU.mult, ALU.mult).then_inc(stats, 1)
                    dve.wait_ge(stats, 3 * t + 2)
                    dve.wait_ge(y_ready, t + 1)
                    xs = self.X[:, sl(t, 1), :].rearrange("p o d -> p (o d)")
                    v.scalar_tensor_tensor(xs, YB, C2[:], xs, ALU.mult, ALU.add).then_inc(y_used, 1)
                    dve.wait_ge(y_used, t + 1)
                    v.bn_stats(self.ST[:, sl(t, 1), :].rearrange("p o s -> p (o s)"), xs).then_inc(stats, 1)

                def step(t, n, more):
                    if more:
                        front(t + 1, 1 - n)
                    back(t, n)

                steps(dve.Fori, lambda: front(0, 0), step)
                dve.wait_ge(stats, 3 * NT)

            @block.tensor
            def _(pe):
                mm, tr = nc.tensor.matmul, nc.tensor.transpose
                pe.wait_ge(ones, 1)
                pe.wait_ge(sums, 2)
                mm(SB, ONES[:], WS[:], start=True, stop=True)
                w2_abs = R[:].rearrange("p n (k f) -> p (n k) f", f=512)
                for k in range(4):
                    i = mm(PS[:, 1 + k, :], ONES[:], w2_abs[:, k], start=True, stop=True)
                i.then_inc(w_sum, 1)
                pe.wait_ge(w_ready, 2)

                def front(t, n):
                    pe.wait_ge(q_ready, t + 1)
                    if not (isinstance(t, int) and t == 0):
                        pe.wait_ge(qt_evac, t)
                    for cc in range(KH1):
                        i = tr(TB[:, cc * P:(cc + 1) * P], QB[:, cc * P:(cc + 1) * P], self.IDB[:])
                    i.then_inc(qt_ready, 1)
                    pe.wait_ge(qt_evac, t + 1)
                    if not (isinstance(t, int) and t < 2):
                        pe.wait_ge(r_ready, t - 1)
                    for k in range(2):
                        for cc in range(KH1):
                            i = mm(HB[n][:, k, :], QT[:, cc], W1[:, cc, k * 512:(k + 1) * 512], start=cc == 0, stop=cc == KH1 - 1)
                    i.then_inc(h_ready, 1)

                def back(t, n):
                    pe.wait_ge(q2_ready, t + 1)
                    if not (isinstance(t, int) and t == 0):
                        pe.wait_ge(q2t_evac, t)
                    for cc in range(KH2):
                        i = tr(T2B[:, cc * P:(cc + 1) * P], Q2B[:, cc * P:(cc + 1) * P], self.IDB[:])
                    i.then_inc(q2t_ready, 1)
                    pe.wait_ge(q2t_evac, t + 1)
                    if not (isinstance(t, int) and t == 0):
                        pe.wait_ge(y_used, t)
                    for cc in range(KH2):
                        i = mm(YB, Q2T[:, cc], W2[:, cc], start=cc == 0, stop=cc == KH2 - 1)
                    i.then_inc(y_ready, 1)

                def step(t, n, more):
                    if more:
                        front(t + 1, 1 - n)
                    back(t, n)

                steps(pe.Fori, lambda: front(0, 0), step)

    def router(self):
        nc, a = self.nc, self.a
        with ExitStack() as c:
            def sb(name, shape, dt=F32):
                return c.enter_context(nc.sbuf_tensor(f"r_{name}", shape, dt))

            def sem(name):
                return c.enter_context(nc.semaphore(f"r_{name}"))
            GW = sb("gate", [P, DC, E])
            N2 = sb("n2", [P, DC])
            XF = sb("xf", [P, 2, D])
            XT = sb("xt", [P, 2, DC, P])
            LG = sb("logits", [P, NT, E])
            RK = sb("rank", [P, NT, E])
            M = sb("m", [P, NT])
            w_in, gate_ready, xf_ready = sem("w_in"), sem("gate_ready"), sem("xf_ready")
            t_ready, t_evac, l_ready, l_used = sem("xt_psum"), sem("xt_sbuf"), sem("logits_psum"), sem("logits_used")
            e_in, e_out, step = sem("exp_in"), sem("exp_out"), sem("step")
            block = c.enter_context(nc.Block())
            tb = [self.PS[:, n, 0:DC * P] for n in range(2)]
            lb = [self.PS[:, 2 + n, 0:E] for n in range(2)]

            @block.sync
            def _(sp):
                sp.dma_start(GW[:], a["E_gate"].rearrange("(c p) e -> p c e", p=P)).then_inc(w_in, 16)
                sp.dma_start(N2[:], a["E_n2"]).then_inc(w_in, 16)

            @block.tensor
            def _(pe):
                pe.wait_ge(gate_ready, DC)
                with pe.Fori(0, NT // 2) as j:
                    for n in range(2):
                        t = 2 * j + n
                        pe.wait_ge(xf_ready, t + 1)
                        pe.wait_ge(t_evac, 2 * j)
                        for cc in range(DC):
                            i = nc.tensor.transpose(tb[n][:, cc * P:(cc + 1) * P], XF[:, n, cc * P:(cc + 1) * P], self.IDF[:])
                        i.then_inc(t_ready, 1)
                        pe.wait_ge(t_evac, t + 1)
                        pe.wait_ge(l_used, 2 * j)
                        for cc in range(DC):
                            i = nc.tensor.matmul(lb[n], XT[:, n, cc], GW[:, cc], start=cc == 0, stop=cc == DC - 1)
                        i.then_inc(l_ready, 1)

            @block.scalar
            def _(act):
                with act.Fori(0, NT // 2) as j:
                    for n in range(2):
                        t = 2 * j + n
                        act.wait_ge(t_ready, t + 1)
                        act.wait_ge(l_ready, 2 * j)
                        nc.scalar.activation(XT[:, n], tb[n].rearrange("p (c q) -> p c q", c=DC), ACT.Copy).then_inc(t_evac, 1)
                act.wait_ge(e_in, 1)
                nc.scalar.activation(LG[:], LG[:], ACT.Exp).then_inc(e_out, 1)

            @block.vector
            def _(dve):
                v = nc.vector
                dve.wait_ge(w_in, 32)
                for cc in range(DC):
                    v.tensor_scalar(GW[:, cc], GW[:, cc], N2[:, cc:cc + 1], None, ALU.mult).then_inc(gate_ready, 1)
                with dve.Fori(0, NT // 2) as j:
                    for n in range(2):
                        t = 2 * j + n
                        dve.wait_ge(t_ready, 2 * j)
                        v.tensor_scalar(XF[:, n, :], self.X[:, sl(t, 1), :].rearrange("p o d -> p (o d)"),
                                        self.RSTD[:, sl(t, 1)], None, ALU.mult).then_inc(xf_ready, 1)
                    for n in range(2):
                        t = 2 * j + n
                        dve.wait_ge(l_ready, t + 1)
                        v.tensor_scalar(LG[:, sl(t, 1), :].rearrange("p o e -> p (o e)"), lb[n], 1.0, None, ALU.mult).then_inc(l_used, 1)
                dve.wait_ge(l_used, NT)
                k = [0]

                def link(ins):
                    k[0] += 1
                    ins.then_inc(step, 1)
                    dve.wait_ge(step, k[0])

                def wide(col):
                    return col[:, :, None].broadcast_to((P, NT, E))
                big = 3.4028234663852886e38
                link(v.tensor_scalar(LG[:], LG[:], big, -big, ALU.min, ALU.max))
                link(v.tensor_reduce(M[:], LG[:], AX.X, ALU.max))
                v.tensor_tensor(LG[:], LG[:], wide(M), ALU.subtract).then_inc(e_in, 1)
                dve.wait_ge(e_out, 1)
                link(v.tensor_reduce(M[:], LG[:], AX.X, ALU.add))
                link(v.reciprocal(M[:], M[:]))
                link(v.tensor_tensor(LG[:], LG[:], wide(M), ALU.mult))
                link(v.memset(RK[:], 0.0))
                for lo in range(E):
                    for hi in range(lo + 1, E):
                        link(v.tensor_tensor(M[:], LG[:, :, lo], LG[:, :, hi], ALU.is_ge))
                        link(v.tensor_tensor(RK[:, :, hi], RK[:, :, hi], M[:], ALU.add))
                        link(v.tensor_scalar(M[:], M[:], -1.0, 1.0, ALU.mult, ALU.add))
                        link(v.tensor_tensor(RK[:, :, lo], RK[:, :, lo], M[:], ALU.add))
                link(v.tensor_scalar(RK[:], RK[:], 2.0, None, ALU.is_lt))
                link(v.tensor_tensor(LG[:], LG[:], RK[:], ALU.mult))
                link(v.tensor_reduce(M[:], LG[:], AX.X, ALU.add))
                link(v.tensor_scalar(M[:], M[:], 1e-8, None, ALU.add))
                link(v.reciprocal(M[:], M[:]))
                link(v.tensor_tensor(LG[:], LG[:], wide(M), ALU.mult))
                link(v.tensor_scalar(self.WTS[:], LG[:], self.TG[:, 3:4], None, ALU.mult))

    def experts(self):
        nc, a = self.nc, self.a
        NG, TG_ = NT // 4, 4
        first = {"e2_l1", "e3_down", "e0_up", "e1_w1", "e1_w2"}
        layers = [("e2_l1", None, 0), ("e3_down", None, 1), ("e2_l2", 0, 2), ("e3_up", 1, 3), ("e2_l3", 2, 0),
                  ("e0_up", None, 1), ("e1_w1", None, 2), ("e1_w2", None, 2)]
        blocks = {"e2_l1": 4, "e3_down": 2, "e2_l2": 4, "e3_up": 4, "e2_l3": 4, "e0_up": 4, "e1_w1": 4, "e1_w2": 4}
        chunks = {n: DC if n in first else 4 for n in blocks}
        chunks["e3_up"] = 2
        outs = [("e2_l4", 0, 2), ("e3_out", 3, 3), ("e0_down", 1, 0), ("e1_down", 2, 1)]
        NBLK = sum(blocks.values())
        RING = 5
        with ExitStack() as c:
            def sb(name, shape, dt=F32):
                return c.enter_context(nc.sbuf_tensor(f"e_{name}", shape, dt))

            def sem(name):
                return c.enter_context(nc.semaphore(f"e_{name}"))
            W = {n: sb(n, [P, chunks[n], blocks[n] * P]) for n in blocks}
            WO = {n: sb(n, [P, 4, MW]) for n, _, _ in outs}
            N2 = sb("n2", [P, DC])
            XF = sb("xf", [P, TG_, D])
            XT = sb("xt", [P, 2, DC, 512])
            HB = [sb(f"hidden{n}", [P, 4, 512]) for n in range(4)]
            Y = sb("y", [P, 2, TG_, D])
            w_in, w_ready, xf_ready = sem("w_in"), sem("w_ready"), sem("xf_ready")
            t_ready, t_evac = sem("xt_psum"), sem("xt_sbuf")
            blk_ready, blk_used = sem("block_psum"), sem("block_used")
            o_ready, o_used = sem("out_psum"), sem("out_used")
            y_in = [sem(f"y_in{n}") for n in range(2)]
            y_out = [sem(f"y_out{n}") for n in range(2)]
            block = c.enter_context(nc.Block())
            ring = [self.PS[:, n, :] for n in range(RING)]
            ob = [self.PS[:, RING + n, 0:MW] for n in range(2)]
            tb = self.PS[:, 7, :]
            assert NBLK % RING == 0
            N_W = len(blocks) + len(outs) + 1

            def steps(loop, step):
                with loop(0, NG // 2) as j:
                    for n in range(2):
                        step(2 * j + n, j, n)

            @block.sync
            def _(sp):
                sp.dma_start(N2[:], a["E_n2"]).then_inc(w_in, 16)
                for n in blocks:
                    sp.dma_start(W[n][:], a["E_" + n].rearrange("(c p) h -> p c h", p=P)).then_inc(w_in, 16)
                for n, _, _ in outs:
                    sp.dma_start(WO[n][:], a["E_" + n][:, M0:].rearrange("(c p) h -> p c h", p=P)).then_inc(w_in, 16)

                def load(g, j, n):
                    sp.dma_start(Y[:, n], self.out_rows[:, sl(4 * g, 4), :]).then_inc(y_in[n], 16)

                def step(g, j, n):
                    sp.wait_ge(y_out[n], 16 * j)
                    load(g, j, n)
                    sp.wait_ge(o_used, 16 * g + 16)
                    sp.dma_start(self.out_rows[:, sl(4 * g, 4), :], Y[:, n]).then_inc(y_out[n], 16)

                steps(sp.Fori, step)
                for n in range(2):
                    sp.wait_ge(y_out[n], 16 * (NG // 2))

            @block.vector
            def _(dve):
                v = nc.vector
                dve.wait_ge(w_in, 16 * N_W)
                for n in ("e2_l1", "e3_down", "e0_up", "e1_w1", "e1_w2"):
                    for cc in range(DC):
                        v.tensor_scalar(W[n][:, cc], W[n][:, cc], N2[:, cc:cc + 1], None, ALU.mult).then_inc(w_ready, 1)

                def norm(g):
                    dve.wait_ge(t_evac, DC * g)
                    for t in range(TG_):
                        i = v.tensor_scalar(XF[:, t], self.X[:, sl(4 * g + t, 1), :].rearrange("p o d -> p (o d)"),
                                            self.RSTD[:, sl(4 * g + t, 1)], None, ALU.mult)
                    i.then_inc(xf_ready, 1)

                def step(g, j, n):
                    norm(g)
                    for b in range(blocks["e1_w2"]):
                        at = NBLK - 4 + b
                        dve.wait_ge(blk_ready, NBLK * g + at + 1)
                        dve.wait_ge(blk_used, NBLK * g + NBLK - 4 + b)
                        v.tensor_tensor(HB[2][:, b], HB[2][:, b], ring[at % RING], ALU.mult).then_inc(blk_used, 1)
                    dve.wait_ge(y_in[n], 16 * (j + 1))
                    m = 0
                    for name, buf, e in outs:
                        for t in range(TG_):
                            dve.wait_ge(o_ready, 16 * g + m + 1)
                            if m >= TG_:
                                dve.wait_ge(o_used, 16 * g + m - TG_ + 1)
                            v.scalar_tensor_tensor(Y[:, n, t, M0:D], ob[m % 2], self.WTS[:, sl(4 * g + t, 1), e],
                                                   Y[:, n, t, M0:D], ALU.mult, ALU.add).then_inc(o_used, 1)
                            m += 1

                steps(dve.Fori, step)

            @block.scalar
            def _(act):
                s_ = nc.scalar

                def step(g, j, n):
                    for cc in range(DC):
                        act.wait_ge(t_ready, DC * g + cc + 1)
                        s_.activation(XT[:, n, cc], tb, ACT.Copy).then_inc(t_evac, 1)
                    at = 0
                    for name, _, buf in layers[:-1]:
                        for b in range(blocks[name]):
                            act.wait_ge(blk_ready, NBLK * g + at + 1)
                            s_.activation(HB[buf][:, b], ring[at % RING], ACT.Silu if name == "e1_w1" else ACT.Gelu).then_inc(blk_used, 1)
                            at += 1
                    act.wait_ge(blk_used, NBLK * g + NBLK)

                steps(act.Fori, step)

            @block.tensor
            def _(pe):
                mm = nc.tensor.matmul
                pe.wait_ge(w_ready, 10)

                def step(g, j, n):
                    pe.wait_ge(xf_ready, g + 1)
                    for cc in range(DC):
                        pe.wait_ge(t_evac, DC * g + cc)
                        for t in range(TG_):
                            i = nc.tensor.transpose(tb[:, t * P:(t + 1) * P], XF[:, t, cc * P:(cc + 1) * P], self.IDF[:])
                        i.then_inc(t_ready, 1)
                    pe.wait_ge(t_evac, DC * g + DC)
                    at = 0
                    done_at = {}
                    for name, src, buf in layers:
                        if src is not None:
                            pe.wait_ge(blk_used, NBLK * g + done_at[src])
                        for b in range(blocks[name]):
                            if at >= RING:
                                pe.wait_ge(blk_used, NBLK * g + at - RING + 1)
                            for cc in range(chunks[name]):
                                rhs = XT[:, n, cc] if src is None else HB[src][:, cc]
                                i = mm(ring[at % RING], W[name][:, cc, b * P:(b + 1) * P], rhs, start=cc == 0, stop=cc == chunks[name] - 1)
                            i.then_inc(blk_ready, 1)
                            at += 1
                        done_at[buf] = at
                    m = 0
                    for name, buf, e in outs:
                        pe.wait_ge(blk_used, NBLK * g + done_at[buf])
                        for t in range(TG_):
                            pe.wait_ge(o_used, 16 * g + max(m - 1, 0))
                            for cc in range(4):
                                i = mm(ob[m % 2], HB[buf][:, cc, t * P:(t + 1) * P], WO[name][:, cc], start=cc == 0, stop=cc == 3)
                            i.then_inc(o_ready, 1)
                            m += 1

                steps(pe.Fori, step)


def kernel(**inputs):
    import numpy as _np
    import concourse.bacc as _bacc
    from concourse import mybir as _mybir
    from concourse.bass_utils import run_bass_kernel_spmd as _run

    g = {k: _np.asarray(v) for k, v in inputs.items()}
    rep = P // DK

    def t(name):
        return _np.ascontiguousarray(g[name].T)

    by_half = _np.arange(D).reshape(2, 4, 2, DK).transpose(0, 2, 1, 3).reshape(-1)

    lay = {
        "x": g["x"],
        "ctx_t": _np.ascontiguousarray(g["ctx_1024"].transpose(0, 2, 1)),
        "g_xattn": g["g_xattn"], "g_ffn": g["g_ffn"],
        "L0_xattn_Wq": g["L0_xattn_Wq"], "L0_xattn_Wo": g["L0_xattn_Wo"][by_half],
        "A_wkv": _np.concatenate([_np.tile(g["L0_xattn_Wk"], (1, rep)), g["L0_xattn_Wv"]], axis=1),
        "A_part_bias": _np.stack([g["L0_xattn_bq"][:P], g["L0_xattn_bq"][P:], _np.tile(g["L0_xattn_bk"], rep)], axis=1),
        "A_free_bias": _np.concatenate([g["L0_xattn_bo"], g["L0_xattn_bv"]]),
        "B_w1": t("L0_ffn_w1"), "B_w2": t("L0_ffn_w2"),
        "L0_ffn_norm1_w": g["L0_ffn_norm1_w"], "L0_ffn_norm2_w": g["L0_ffn_norm2_w"],
        "L0_ffn_act_scale": g["L0_ffn_act_scale"], "L0_ffn_act_bias": g["L0_ffn_act_bias"],
        "C_wq": t("L1_xattn_Wq"), "C_wc": t("L1_xattn_Wc")[by_half],
        "C_wkv": _np.concatenate([_np.tile(g["L1_xattn_Wkv"][:DK].T, (1, rep)), g["L1_xattn_Wkv"][DK:].T], axis=1),
        "D_wq": t("L1_ffn_wq"), "D_wk": t("L1_ffn_wk"), "D_wv": t("L1_ffn_wv"), "D_wo": t("L1_ffn_wo")[by_half],
        "D_part_w": _np.stack([_np.tile(g["L1_ffn_qn_w"], rep), _np.tile(g["L1_ffn_kn_w"], rep)], axis=1),
        "L1_ffn_n1_w": g["L1_ffn_n1_w"],
        "E_gate": t("L1_ffn_gate_w"),
        "E_n2": _np.ascontiguousarray(g["L1_ffn_n2_w"].reshape(DC, P).T),
    }
    for n in ("e0_up", "e0_down", "e1_w1", "e1_w2", "e1_down", "e2_l1", "e2_l2", "e2_l3", "e2_l4", "e3_down", "e3_up", "e3_out"):
        lay["E_" + n] = t("L1_ffn_" + n)

    nc = _bacc.Bacc("TRN2", target_bir_lowering=False, num_devices=1)
    arrays, args = {}, {}
    for name, v in lay.items():
        v = _np.ascontiguousarray(v)
        arrays[f"in_{name}_dram"] = v
        args[name] = nc.dram_tensor(f"in_{name}_dram", v.shape, _mybir.dt.from_np(v.dtype), kind="ExternalInput").ap()
    out = nc.dram_tensor("out_0_dram", (B, S, D), _mybir.dt.float32, kind="ExternalOutput").ap()
    Kernel(nc, args, out).build()
    r = _run(nc, [arrays], core_ids=[0])
    return r.results[0]["out_0_dram"]
```

```python
import concourse.bass as bass
from concourse import mybir
from contextlib import ExitStack

F32 = mybir.dt.float32
BF16 = mybir.dt.bfloat16
U32 = mybir.dt.uint32
ALU = mybir.AluOpType
ACT = mybir.ActivationFunctionType
AX = mybir.AxisListType

P = 128
B, S, D = 32, 256, 256
NT = B * S // P
H, DK = 16, 16
DC = D // P
HID1 = 1024
M0 = 64
MW = D - M0
E = 4
LN_EPS, EPS_NORM, EPS_Q, EPS_RMS = 1e-5, 1e-8, 1e-5, 1.1920929e-07
RND = 12582912.0
NEG = -1e30
Q_PART = (0, 0, 0, 1, 1, 2)
K_PART = (0, 1, 2, 0, 1, 0)
KR = 16 * len(Q_PART)


def sl(i, n):
    return bass.ds(i, n)


ORDERS = {
    "A": "p0 s0 T1- s1 h h OT- h h p1 s2 h h PR- h h p2 hi s3 h h h s4 h mid v0 h h s5 h T0 s6 h NM s7 v1",
    "C": "s0 T1- s1 p0 p1 OT- s2 h p2 h h PR- h h s3 p4 h p3 h h p5 h h hi s4 v0 h s5 h mid h s6 h h h T0 NM s7 v1",
    "D": "p0 s0 T1- s1 p1 p2 OT- s2 PR- s3 p3 h h r0 h h s4 h v0 h h T0 h s5 r1 s6 h h p4 h h p5 h hi h h mid h NM s7 v1",
}


class Kernel:

    def __init__(self, nc, a, out):
        self.nc, self.a, self.out = nc, a, out
        self.x_rows = a["x"].rearrange("b (t p) d -> p (b t) d", p=P)
        self.out_rows = out.rearrange("b (t p) d -> p (b t) d", p=P)

    def build(self):
        nc = self.nc
        with ExitStack() as c:
            def sb(name, shape, dt=F32):
                return c.enter_context(nc.sbuf_tensor(name, shape, dt))
            self.X = sb("x_all", [P, NT, D])
            self.ST = sb("row_stats", [P, NT, 6])
            self.MEAN = sb("mean", [P, NT])
            self.RSTD = sb("rstd", [P, NT])
            self.RRMS = sb("rrms", [P, NT])
            self.WTS = sb("wts", [P, NT, E])
            self.TG = sb("tanh_gates", [P, 4])
            self.IDF = sb("ident_f", [P, P])
            self.IDB = sb("ident_b", [P, P], BF16)
            self.PS = c.enter_context(nc.psum_tensor("psum", [P, 8, 512], F32))
            self.q_dram = nc.dram_tensor("q_parts", (2, 3, DK, H, S), BF16, kind="Internal").ap()
            self.k_dram = nc.dram_tensor("k_parts", (2, 3, DK, H, S), BF16, kind="Internal").ap()
            self.k1_dram = nc.dram_tensor("k1_parts", (2, 3, DK, S), BF16, kind="Internal").ap()
            self.nm_dram = nc.dram_tensor("max_parts", (2, 3, 32, P), BF16, kind="Internal").ap()
            self.np_step, self.np_var, self.np_root = [c.enter_context(nc.semaphore(f"np_{name}"))
                                                       for name in ("step", "var_ready", "root_ready")]
            self.np_steps, self.np_roots = 0, 0
            self.load_phase()
            self.norm_params("a", LN_EPS, None)
            self.attention("A")
            self.norm_params("b", LN_EPS, EPS_NORM)
            self.bit_ffn()
            self.norm_params("c", LN_EPS, None)
            self.attention("C")
            self.norm_params("d", LN_EPS, EPS_RMS)
            self.attention("D")
            self.norm_params("e", EPS_RMS, None, raw=True)
            self.experts()

    def load_phase(self):
        nc, a = self.nc, self.a
        with ExitStack() as c:
            def sem(name):
                return c.enter_context(nc.semaphore("ld_" + name))
            x_in = [sem(f"x_in{n}") for n in range(4)]
            gates_in, ident, stats, gates = sem("gates_in"), sem("ident"), sem("stats"), sem("gates")
            G = c.enter_context(nc.sbuf_tensor("gates_raw", [P, 4], F32))
            block = c.enter_context(nc.Block())
            n4 = NT // 4

            @block.sync
            def _(sp):
                for n in range(4):
                    sp.dma_start(self.X[:, n * n4:(n + 1) * n4, :], self.x_rows[:, n * n4:(n + 1) * n4, :]).then_inc(x_in[n], 16)
                sp.dma_start(G[:, 0:2], a["g_xattn"][None, :].broadcast_to((P, 2))).then_inc(gates_in, 16)
                sp.dma_start(G[:, 2:4], a["g_ffn"][None, :].broadcast_to((P, 2))).then_inc(gates_in, 16)

            @block.gpsimd
            def _(pool):
                nc.gpsimd.memset(self.IDF[:], 0.0).then_inc(ident, 1)
                nc.gpsimd.memset(self.IDB[:], 0.0).then_inc(ident, 1)
                pool.wait_ge(ident, 2)
                for m in (self.IDF, self.IDB):
                    nc.gpsimd.affine_select(out=m[:], in_=m[:], compare_op=ALU.not_equal, fill=1.0, base=0,
                                            pattern=[[-1, P]], channel_multiplier=1).then_inc(ident, 1)
                pool.wait_ge(ident, 4)

            @block.scalar
            def _(act):
                act.wait_ge(gates_in, 32)
                nc.scalar.activation(self.TG[:], G[:], ACT.Tanh).then_inc(gates, 1)
                act.wait_ge(gates, 1)

            @block.vector
            def _(dve):
                for n in range(4):
                    dve.wait_ge(x_in[n], 16)
                    with dve.Fori(n * n4 // 4, (n + 1) * n4 // 4) as j:
                        for k in range(4):
                            nc.vector.bn_stats(self.ST[:, sl(4 * j + k, 1), :].rearrange("p o s -> p (o s)"),
                                               self.X[:, sl(4 * j + k, 1), :].rearrange("p o d -> p (o d)")).then_inc(stats, 1)
                dve.wait_ge(stats, NT)

    def norm_params(self, tag, eps, rms_eps, raw=False):
        nc = self.nc
        with ExitStack() as c:
            step, sq_in, sq_out = self.np_step, self.np_var, self.np_root
            n, roots_before = [self.np_steps], self.np_roots
            V = c.enter_context(nc.sbuf_tensor(f"np{tag}_v", [P, NT], F32))
            T = c.enter_context(nc.sbuf_tensor(f"np{tag}_t", [P, NT], F32))
            R = c.enter_context(nc.sbuf_tensor(f"np{tag}_r", [P, NT], F32))
            U = c.enter_context(nc.sbuf_tensor(f"np{tag}_u", [P, NT], F32))
            block = c.enter_context(nc.Block())
            st, n_roots = self.ST, 1 if rms_eps is None else 2
            v = nc.vector

            @block.vector
            def _(dve):
                def link(ins):
                    n[0] += 1
                    ins.then_inc(step, 1)
                    dve.wait_ge(step, n[0])

                def rsqrt(out, root, k):
                    v.tensor_scalar(U[:], R[:], 0.0, None, ALU.add).then_inc(sq_in, 1)
                    dve.wait_ge(sq_out, roots_before + k)
                    link(v.reciprocal(out[:], root[:]))
                    link(v.tensor_tensor(U[:], out[:], out[:], ALU.mult))
                    link(v.tensor_tensor(U[:], U[:], R[:], ALU.mult))
                    link(v.tensor_scalar(U[:], U[:], -0.5, 1.5, ALU.mult, ALU.add))
                    link(v.tensor_tensor(out[:], out[:], U[:], ALU.mult))

                link(v.tensor_tensor(self.MEAN[:], st[:, :, 1], st[:, :, 4], ALU.add))
                link(v.tensor_scalar(self.MEAN[:], self.MEAN[:], 0.5, None, ALU.mult))
                link(v.tensor_tensor(T[:], st[:, :, 1], st[:, :, 4], ALU.subtract))
                link(v.tensor_tensor(T[:], T[:], T[:], ALU.mult))
                link(v.tensor_tensor(V[:], st[:, :, 2], st[:, :, 5], ALU.add))
                link(v.tensor_scalar(V[:], V[:], 1.0 / D, None, ALU.mult))
                link(v.tensor_scalar(T[:], T[:], 0.25, None, ALU.mult))
                link(v.tensor_tensor(V[:], V[:], T[:], ALU.add))
                if raw:
                    link(v.tensor_tensor(T[:], self.MEAN[:], self.MEAN[:], ALU.mult))
                    link(v.tensor_tensor(V[:], V[:], T[:], ALU.add))
                link(v.tensor_scalar(R[:], V[:], eps, None, ALU.add))
                rsqrt(self.RSTD, T, 1)
                if rms_eps is not None:
                    link(v.tensor_tensor(R[:], V[:], self.RSTD[:], ALU.mult))
                    link(v.tensor_tensor(R[:], R[:], self.RSTD[:], ALU.mult))
                    link(v.tensor_scalar(R[:], R[:], rms_eps, None, ALU.add))
                    rsqrt(self.RRMS, T, 2)
                    link(v.tensor_tensor(self.RRMS[:], self.RRMS[:], self.RSTD[:], ALU.mult))

            @block.scalar
            def _(act):
                for k in range(n_roots):
                    act.wait_ge(sq_in, roots_before + k + 1)
                    nc.scalar.activation(T[:], R[:], ACT.Sqrt).then_inc(sq_out, 1)

            self.np_steps, self.np_roots = n[0], roots_before + n_roots

    def attention(self, kind):
        nc, a = self.nc, self.a
        mha, gathered = kind == "D", kind == "C"
        L = kind.lower()
        with ExitStack() as c:
            def sb(name, shape, dt=F32):
                return c.enter_context(nc.sbuf_tensor(f"{L}_{name}", shape, dt))

            def sem(name):
                return c.enter_context(nc.semaphore(f"{L}_{name}"))

            OW = MW if mha else D
            QW = 3 * D if mha else D
            Wq = sb("wq", [P, DC, QW])
            Wo = sb("wo", [P, DC, OW])
            KVW = P + DK
            Wkv = None if mha else sb("wkv", [P, DC, KVW])
            CTX = None if mha else sb("ctx", [P, 2, DC, S])
            PB = sb("part_bias", [P, 3])
            FB = sb("free_bias", [P, D + DK])
            XN = sb("xn", [P, 2, D])
            XNT = sb("xnt", [P, DC, S])
            nk = 4 if mha else 3
            QF = sb("qf", [P, nk, S])
            QR = sb("q_rest", [P, nk, S])
            QP = sb("q_parts", [P, 2, 3, nk, S], BF16)
            QS = sb("q_stack", [KR + 3, 2, H, S], BF16)
            KS = sb("k_stack", [KR + 3, 2, H if mha else 1, S], BF16)
            VH = H if mha else 1
            VW = 32
            VS = sb("v_staged", [P, 2, VH, DK])
            VP = sb("v_ones", [P, 2, 2, VH, VW])
            NM = sb("neg_max", [P, 2 * H])
            NMR = sb("neg_max_rest", [P, 2 * H])
            NMS = sb("neg_max_parts", [P, 3, 2 * H], BF16)
            NMT = sb("neg_max_t", [3 * 2 * H, 2, P], BF16)
            EX = sb("exps", [P, 8, 2, 512])
            OV = sb("o_raw", [P, 2, 512])
            REC = sb("rec", [P, 16])
            HOLD = sb("hold", [P, 1])
            POOL_HOLD = sb("pool_hold", [P, 1])
            O = sb("o", [P, 2, D])
            OT = sb("o_t", [P, DC, S])
            if gathered:
                MX = sb("mx8", [P, 2, 8])
                IX = sb("ix8", [P, 2, 8], U32)
                IXF = sb("ixf", [P, 2])
                IOTA = sb("iota", [P, S])
                OH = sb("onehot", [P, 2, S], BF16)
                OHT = sb("onehot_t", [P, 2, S])
                KVP = sb("kvp", [P, 2, KVW])
            if mha:
                QK = sb("qk", [P, 2, 2 * D])
                SQ = sb("qk_sq", [P, 2 * D])
                MS = sb("qk_ms", [P, 2, 32])
                RT = sb("qk_root", [P, 2, 32])
                HALF = sb("minus_half", [P, 32])
                MASKQ = sb("mask_q", [P, 2, S], BF16)
                MASKK = sb("mask_k", [P, 2, 2, S], BF16)
                XR = sb("x1", [P, 2, D])
                YB = sb("y", [P, 2, D])

            W_, PVB = self.PS[:, 0, :], self.PS[:, 1, :]
            WB = self.PS[:, 0, :].bitcast(BF16)
            W2 = W_.rearrange("p (m s) -> p m s", m=2)
            sc_slot = [self.PS[:, 2 + n, :] for n in range(2)]
            st_slot = [self.PS[:, 4 + 2 * n:6 + 2 * n, :] for n in range(2)]

            w_in, consts = sem("weights_in"), sem("consts")
            ctx_in = [] if mha else [sem(f"ctx_in{n}") for n in range(2)]
            xn_ready = sem("xn_ready")
            work_full, work_free = sem("work_full"), sem("work_free")
            rounded, rest_ready, parts_ready = sem("parts_rounded"), sem("rest_ready"), sem("parts_ready")
            v_ready, stack_used = sem("v_ready"), sem("stack_used")
            parts_out = [sem(f"parts_out{n}") for n in range(2)]
            stack_in = [sem(f"stack_in{n}") for n in range(2)]
            scores_ready, scores_used = sem("scores_ready"), sem("scores_used")
            nm_step = sem("neg_max_step")
            nm_out = [sem(f"neg_max_out{n}") for n in range(2)]
            nm_in = [sem(f"neg_max_in{n}") for n in range(2)]
            st_ready, exp_ready, pv_done, ov_ready = sem("scores_t_ready"), sem("exp_ready"), sem("pv_done"), sem("o_raw_ready")
            rec_ready, stats = sem("rec_ready"), sem("stats")
            if not mha:
                kf_ready = sem("kf_ready")
            if kind != "A":
                prep_step = sem("prep_step")
            if kind == "A":
                x_biased = sem("x_plus_bias")
            if mha:
                w_scaled, y_ready, y_out = sem("w_scaled"), sem("y_ready"), sem("y_out")
                ms_ready, xr_ready, rt_ready = sem("ms_ready"), sem("xr_ready"), sem("rt_ready")

            NPREP = 3 if kind == "A" else 6
            ORDER = ORDERS[kind].split()
            ITEMS = [x for x in ORDER if x[0] in "TOPpN"]
            V_ITEM = {"A": "p2", "C": "p5", "D": "p3"}[kind]
            assert ORDER.count("h") == H
            FIRST, LAST = 2, B - 2

            def there(i, x):
                if not isinstance(i, int):
                    return True
                if x[0] in "sv" or x == "T0":
                    return True
                if x[-1] == "-":
                    return i >= 1
                return i + 1 < B if x in ("h", "NM") else i + 2 < B

            number = {}
            for b in range(2):
                for k in range(NPREP):
                    number[b - 2, f"p{k}"] = len(number)
            number[-1, "NM"] = len(number)
            for i in range(B):
                for x in ITEMS:
                    if there(i, x):
                        number[i, x] = len(number)
            for x in ("T1-", "OT-", "PR-"):
                number[B, x] = len(number)
            NBODY = len(ITEMS)
            for x in ITEMS:
                assert number[LAST - 1, x] == number[FIRST, x] + (LAST - 1 - FIRST) * NBODY

            def nth(i, x):
                return number[i, x] if isinstance(i, int) else number[FIRST, x] + (i - FIRST) * NBODY

            N_CONST = {"A": 5, "C": 6, "D": 10}[kind]
            NPO = 12 if mha else 7
            NSI = 6
            NW = {"A": 5, "C": 3, "D": 7}[kind]
            block = c.enter_context(nc.Block())

            def at(i, d, j, n):
                m = n + d
                return i + d, j + m // 2, m % 2

            def steps(loop, prologue, step, tail):
                prologue()
                for i in range(FIRST):
                    step(i, i // 2, i % 2)
                with loop(FIRST // 2, LAST // 2) as j:
                    for n in range(2):
                        step(2 * j + n, j, n)
                for i in range(LAST, B):
                    step(i, i // 2, i % 2)
                tail()

            def known(b, least):
                return not (isinstance(b, int) and b < least)

            @block.sync
            def _(sp):
                if kind == "A":
                    sp.dma_start(Wq[:], a["L0_xattn_Wq"].rearrange("(c p) e -> p c e", p=P)).then_inc(w_in, 16)
                    sp.dma_start(Wo[:], a["L0_xattn_Wo"].rearrange("(c p) e -> p c e", p=P)).then_inc(w_in, 16)
                    sp.dma_start(Wkv[:], a["A_wkv"].rearrange("(c p) e -> p c e", p=P)).then_inc(w_in, 16)
                    sp.dma_start(PB[:], a["A_part_bias"]).then_inc(w_in, 16)
                    sp.dma_start(FB[:], a["A_free_bias"][None, :].broadcast_to((P, D + DK))).then_inc(w_in, 16)
                elif kind == "C":
                    sp.dma_start(Wq[:], a["C_wq"].rearrange("(c p) e -> p c e", p=P)).then_inc(w_in, 16)
                    sp.dma_start(Wo[:], a["C_wc"].rearrange("(c p) e -> p c e", p=P)).then_inc(w_in, 16)
                    sp.dma_start(Wkv[:], a["C_wkv"].rearrange("(c p) e -> p c e", p=P)).then_inc(w_in, 16)
                else:
                    for n in range(3):
                        sp.dma_start(Wq[:, :, n * D:(n + 1) * D],
                                     a[f"D_w{'qkv'[n]}"].rearrange("(c p) e -> p c e", p=P)).then_inc(w_in, 16)
                    sp.dma_start(Wo[:], a["D_wo"][:, M0:].rearrange("(c p) e -> p c e", p=P)).then_inc(w_in, 16)
                    sp.dma_start(PB[:, 0:2], a["D_part_w"]).then_inc(w_in, 16)
                    sp.dma_start(PB[:, 2:3], a["L1_ffn_n1_w"][0:P][:, None]).then_inc(w_in, 16)
                    sp.dma_start(FB[:, 0:1], a["L1_ffn_n1_w"][P:D][:, None]).then_inc(w_in, 16)

                def ctx(b, j, n):
                    if mha:
                        return
                    if known(b, 2):
                        sp.wait_ge(parts_ready, b - 1)
                    sp.dma_start(CTX[:, n, :, :], a["ctx_t"][sl(b, 1)].rearrange("o (c p) s -> p (o c) s", p=P)).then_inc(ctx_in[n], 16)

                def parts(b, j, n, halves=(0, 1)):
                    if 0 in halves:
                        sp.wait_ge(parts_ready, b + 1)
                    for m in halves:
                        heads = slice(m * H // 2, (m + 1) * H // 2)
                        for t in range(3):
                            sp.dma_start(self.q_dram[n, t, :, heads].rearrange("d h s -> h d s"), QP[:, n, t, m, :]).then_inc(parts_out[n], 16)
                            if mha:
                                if m == 1 and t == 2 and known(b, 2):
                                    sp.wait_ge(stack_used, b - 1)
                                sp.dma_start(self.k_dram[n, t, :, heads].rearrange("d h s -> h d s"), QP[:, n, t, 2 + m, :]).then_inc(parts_out[n], 16)
                    if not mha and 1 in halves:
                        sp.dma_start(self.k1_dram[n].rearrange("t d s -> d t s"), QP[0:DK, n, :, 2, :]).then_inc(parts_out[n], 16)

                def stack(b, j, n, pieces):
                    if 0 in pieces:
                        sp.wait_ge(parts_out[n], 16 * NPO * (j + 1))
                        if not mha and known(b, 2):
                            sp.wait_ge(stack_used, b - 1)
                    qd = self.q_dram[n].rearrange("t d h s -> t d (h s)")
                    qs = QS[:, n, :, :].rearrange("r h s -> r (h s)")
                    for k in pieces:
                        copies, row = (3, 2, 1)[k], (0, 48, 80)[k]
                        sp.dma_start(qs[row:row + 16 * copies, :], qd[k][None].broadcast_to((copies, DK, H * S))).then_inc(stack_in[n], 16)
                        if mha:
                            kd = self.k_dram[n].rearrange("t d h s -> (t d) (h s)")
                            sp.dma_start(KS[row:row + 16 * copies, n, :, :].rearrange("r h s -> r (h s)"), kd[0:16 * copies]).then_inc(stack_in[n], 16)
                        else:
                            kd = self.k1_dram[n].rearrange("t d s -> (t d) s")
                            sp.dma_start(KS[row:row + 16 * copies, n, 0, :], kd[0:16 * copies]).then_inc(stack_in[n], 16)

                def neg_max_out(b, j, n, w):
                    sp.wait_ge(work_free, w + 1)
                    sp.dma_start(self.nm_dram[n].rearrange("t u q -> (t u) q"), NMT[:, n, :]).then_inc(nm_out[n], 16)

                def neg_max_in(b, j, n):
                    sp.wait_ge(nm_out[n], 16 * (j + 1))
                    sp.dma_start(QS[KR:KR + 3, n, :, :].rearrange("t h s -> t (h s)"),
                                 self.nm_dram[n].rearrange("t u q -> t (u q)")).then_inc(nm_in[n], 16)

                def y_store(b):
                    sp.wait_ge(y_ready, b + 1)
                    sp.dma_start(self.out_rows[:, sl(2 * b, 2), :], YB[:]).then_inc(y_out, 16)

                def prologue():
                    ctx(0, 0, 0)
                    ctx(1, 0, 1)
                    for b in range(2):
                        parts(b, 0, b)
                        stack(b, 0, b, (0, 1, 2))
                    neg_max_out(0, 0, 0, nth(-1, "NM"))
                    neg_max_in(0, 0, 0)

                def step(i, j, n):
                    prep, maxes = known(i, 0) and not (isinstance(i, int) and i + 2 >= B), not (isinstance(i, int) and i + 1 >= B)
                    nxt, nxt2 = at(i, 1, j, n), at(i, 2, j, n)
                    if prep:
                        ctx(*nxt2)
                    if mha and known(i, 1):
                        y_store(i - 1)
                    if prep and kind == "A":
                        parts(*nxt2)
                    if maxes:
                        neg_max_out(*nxt, nth(i, "NM"))
                    if prep and kind == "C":
                        parts(*nxt2, (0,))
                    if maxes:
                        neg_max_in(*nxt)
                    if prep and kind != "A":
                        parts(*nxt2, (1,) if kind == "C" else (0, 1))
                    if prep:
                        stack(*nxt2, (0, 1, 2))

                def tail():
                    if mha:
                        y_store(B - 1)
                        sp.wait_ge(y_out, 16 * B)

                steps(sp.Fori, prologue, step, tail)

            @block.gpsimd
            def _(pool):
                cn = [0]

                def const(ins):
                    cn[0] += 1
                    ins.then_inc(consts, 1)
                    pool.wait_ge(consts, cn[0])

                const(nc.gpsimd.memset(VP[:], 0.0))
                const(nc.gpsimd.memset(VP[:, :, :, :, DK:DK + 1], 1.0))
                const(nc.gpsimd.memset(POOL_HOLD[:], 0.0))
                const(nc.gpsimd.memset(QR[:], 0.0))
                const(nc.gpsimd.memset(KS[KR:KR + 3, :, :, :], 1.0))
                if gathered:
                    const(nc.gpsimd.iota(IOTA[:], [[1, S]], base=0, channel_multiplier=0, allow_small_or_imprecise_dtypes=True))
                if mha:
                    const(nc.gpsimd.memset(HALF[:], -0.5))
                    const(nc.gpsimd.memset(MASKQ[:], 0.0))
                    const(nc.gpsimd.memset(MASKK[:], 0.0))
                    const(nc.gpsimd.affine_select(out=MASKQ[:], in_=MASKQ[:], compare_op=ALU.is_ge, fill=NEG, base=0,
                                                  pattern=[[P, 2], [-1, S]], channel_multiplier=1))
                    const(nc.gpsimd.affine_select(out=MASKK[:].rearrange("p c h q -> p (c h) q"),
                                                  in_=MASKK[:].rearrange("p c h q -> p (c h) q"),
                                                  compare_op=ALU.is_ge, fill=NEG, base=0,
                                                  pattern=[[0, 4], [1, S]], channel_multiplier=-1))
                if kind == "A":
                    pool.wait_ge(w_in, 16 * NW)
                    const(nc.gpsimd.tensor_scalar(FB[:, 0:D], FB[:, 0:D], self.TG[:, 0:1], None, ALU.mult))
                g = nc.gpsimd

                def prep(b, j, n, w):
                    if mha:
                        for t in range(2):
                            pool.wait_ge(ms_ready, 2 * b + t + 1)
                            g.tensor_tensor(RT[:, t], MS[:, t], HALF[:], ALU.pow).then_inc(rt_ready, 1)
                    if kind == "A":
                        pool.wait_ge(xn_ready, b + 1)
                        g.tensor_tensor(self.X[:, sl(2 * b, 2), :], self.X[:, sl(2 * b, 2), :],
                                        FB[:, None, 0:D].broadcast_to((P, 2, D)), ALU.add).then_inc(x_biased, 1)
                    pool.wait_ge(rounded, 2 * b + 1)
                    g.tensor_tensor(QR[:], QF[:], QP[:, n, 0], ALU.subtract).then_inc(rest_ready, 1)
                    pool.wait_ge(rounded, 2 * b + 2)
                    g.tensor_tensor(QP[:, n, 2], QR[:], QP[:, n, 1], ALU.subtract).then_inc(parts_ready, 1)
                    pool.wait_ge(work_free, w + 1)
                    if known(b, 2):
                        pool.wait_ge(pv_done, 2 * (b - 1))
                    g.tensor_tensor(POOL_HOLD[:], POOL_HOLD[:], POOL_HOLD[:], ALU.add)
                    g.tensor_copy(VP[:, n, :, :, 0:DK], VS[:]).then_inc(v_ready, 1)

                def prologue():
                    for b in range(2):
                        prep(b, 0, b, nth(b - 2, V_ITEM))

                def step(i, j, n):
                    if not (isinstance(i, int) and i + 2 >= B):
                        prep(*at(i, 2, j, n), nth(i, V_ITEM))

                steps(pool.Fori, prologue, step, lambda: None)

            @block.scalar
            def _(act):
                s_ = nc.scalar
                s_.preload_act_table(ACT.Exp)
                act.wait_ge(w_in, 16 * NW)
                if mha:
                    act.wait_ge(w_scaled, 3)

                def evac(w, out, in_):
                    act.wait_ge(work_full, w + 1)
                    s_.activation(out, in_, ACT.Copy).then_inc(work_free, 1)

                def prep(k, b, w):
                    if k == 0:
                        evac(w, XNT[:], W2)
                    elif not mha and k == 1:
                        act.wait_ge(work_full, w + 1)
                        if known(b, 1):
                            act.wait_ge(parts_ready, b)
                        if kind == "A":
                            s_.activation(QF[:, 0], W2[:, 0], ACT.Identity, bias=PB[:, 0:1])
                            s_.activation(QF[:, 1], W2[:, 1], ACT.Identity, bias=PB[:, 1:2]).then_inc(work_free, 1)
                        else:
                            s_.activation(QF[:, 0:2], W2, ACT.Copy, scale=DK ** -0.5).then_inc(work_free, 1)
                    elif kind == "A":
                        act.wait_ge(work_full, w + 1)
                        s_.activation(QF[:, 2], W_[:, 0:S], ACT.Identity, bias=PB[:, 2:3]).then_inc(kf_ready, 1)
                    elif gathered and k == 3:
                        evac(w, OHT[:], WB[:, 0:2 * S].rearrange("p (m s) -> p m s", m=2))
                    elif gathered and k == 4:
                        evac(w, KVP[:], W_[:, 0:2 * KVW].rearrange("p (m s) -> p m s", m=2))
                    elif gathered and k == 5:
                        act.wait_ge(work_full, w + 1)
                        s_.activation(QF[:, 2], W_[:, 0:S], ACT.Copy).then_inc(kf_ready, 1)
                    elif mha and k in (1, 2):
                        evac(w, QK[:, k - 1], W_)
                    elif mha and k == 3:
                        act.wait_ge(work_full, w + 1)
                        if known(b, 1):
                            act.wait_ge(v_ready, b)
                        s_.activation(VS[:], W_.rearrange("p (c h d) -> p c h d", c=2, h=H), ACT.Copy).then_inc(work_free, 1)
                    elif mha and k in (4, 5):
                        act.wait_ge(work_full, w + 1)
                        if known(b, 1):
                            act.wait_ge(parts_ready, b)
                        s_.activation(QF[:, 2 * (k - 4):2 * (k - 4) + 2], W2, ACT.Copy, scale=PB[:, k - 4:k - 3]).then_inc(work_free, 1)

                def split_high(b, j, n, w):
                    if mha:
                        act.wait_ge(work_free, w + 1)
                    else:
                        act.wait_ge(kf_ready, b + 1)
                    if known(b, 2):
                        act.wait_ge(parts_out[n], 16 * NPO * j)
                    s_.activation(QP[:, n, 0], QF[:], ACT.Copy).then_inc(rounded, 1)

                def split_mid(b, n):
                    act.wait_ge(rest_ready, b + 1)
                    s_.activation(QP[:, n, 1], QR[:], ACT.Copy).then_inc(rounded, 1)

                def exps(b, g):
                    act.wait_ge(st_ready, 8 * b + g + 1)
                    if g % 4 == 0 and known(b, 1):
                        act.wait_ge(pv_done, 2 * b - 1 + g // 4)
                    if mha:
                        s_.activation(EX[:, g].rearrange("p c f -> p (c f)")[:, 0:768],
                                      st_slot[g % 2].rearrange("p c f -> p (c f)")[:, 0:768], ACT.Exp).then_inc(exp_ready, 1)
                    else:
                        s_.activation(EX[:, g], st_slot[g % 2], ACT.Exp).then_inc(exp_ready, 1)

                def raw_half(b, k):
                    act.wait_ge(pv_done, 2 * b + k + 1)
                    s_.activation(OV[:, k], PVB, ACT.Copy).then_inc(ov_ready, 1)

                def item(x, i):
                    if x[0] == "p":
                        prep(int(x[1]), i + 2, nth(i, x))
                    elif x == "OT-":
                        evac(nth(i, x), OT[:], W2)

                def prologue():
                    for b in range(2):
                        for k in range(NPREP):
                            prep(k, b, nth(b - 2, f"p{k}"))
                        split_high(b, 0, b, nth(b - 2, f"p{NPREP - 1}"))
                        split_mid(b, b)

                def step(i, j, n):
                    b, jj, nn = at(i, 2, j, n)
                    for x in ORDER:
                        if not there(i, x):
                            continue
                        if x[0] == "s":
                            exps(i, int(x[1]))
                        elif x[0] == "v":
                            raw_half(i, int(x[1]))
                        elif x == "hi":
                            split_high(b, jj, nn, nth(i, f"p{NPREP - 1}"))
                        elif x == "mid":
                            split_mid(b, nn)
                        else:
                            item(x, i)

                steps(act.Fori, prologue, step, lambda: item("OT-", B))

            @block.vector
            def _(dve):
                v = nc.vector
                dve.wait_ge(w_in, 16 * NW)
                if gathered:
                    dve.wait_ge(consts, N_CONST)
                if mha:
                    v.tensor_scalar(Wq[:, 0], Wq[:, 0], PB[:, 2:3], None, ALU.mult).then_inc(w_scaled, 1)
                    v.tensor_scalar(Wq[:, 1], Wq[:, 1], FB[:, 0:1], None, ALU.mult).then_inc(w_scaled, 1)
                    v.tensor_scalar(PB[:, 0:1], PB[:, 0:1], DK ** -0.5, None, ALU.mult).then_inc(w_scaled, 1)
                    dve.wait_ge(w_scaled, 3)
                v_part = W_[:, S:S + 2 * DK].rearrange("p (c d) -> p c d", c=2)

                def norm(b, w_before):
                    if w_before is not None:
                        dve.wait_ge(work_free, w_before + 1)
                    r = self.RRMS if mha else self.RSTD
                    for t in range(2):
                        i = v.tensor_scalar(XN[:, t, :], self.X[:, sl(2 * b + t, 1), :].rearrange("p o d -> p (o d)"),
                                            self.MEAN[:, sl(2 * b + t, 1)], r[:, sl(2 * b + t, 1)], ALU.subtract, ALU.mult)
                    i.then_inc(xn_ready, 1)

                def prep(k, b, w):
                    if kind == "A" and k == 2 or gathered and k == 5:
                        dve.wait_ge(kf_ready, b + 1)
                        if known(b, 1):
                            dve.wait_ge(v_ready, b)
                        if kind == "A":
                            v.tensor_tensor(VS[:, :, 0, :], v_part, FB[:, None, D:D + DK].broadcast_to((P, 2, DK)), ALU.add).then_inc(work_free, 1)
                        else:
                            v.tensor_copy(VS[:, :, 0, :], v_part).then_inc(work_free, 1)
                    if gathered and k == 2:
                        dve.wait_ge(work_full, w + 1)
                        v.tensor_copy(HOLD[:], W_[:, 0:1])
                        for t in range(2):
                            i = v.max(MX[:, t], W_[:, t * S:(t + 1) * S])
                        i.then_inc(prep_step, 1)
                        dve.wait_ge(prep_step, 3 * b + 1)
                        v.tensor_copy(HOLD[:], MX[:, 0, 0:1])
                        for t in range(2):
                            i = v.max_index(IX[:, t], MX[:, t], W_[:, t * S:(t + 1) * S])
                        i.then_inc(work_free, 1)
                        dve.wait_ge(work_free, w + 1)
                        v.tensor_copy(IXF[:], IX[:, :, 0]).then_inc(prep_step, 1)
                        dve.wait_ge(prep_step, 3 * b + 2)
                        for t in range(2):
                            i = v.tensor_scalar(OH[:, t], IOTA[:], IXF[:, t:t + 1], None, ALU.is_equal)
                        i.then_inc(prep_step, 1)
                    if mha and k in (1, 2):
                        t = k - 1
                        dve.wait_ge(work_free, w + 1)
                        v.tensor_tensor(SQ[:], QK[:, t], QK[:, t], ALU.mult).then_inc(prep_step, 1)
                        dve.wait_ge(prep_step, 6 * b + 2 * t + 1)
                        v.tensor_reduce(MS[:, t], SQ[:].rearrange("p (h d) -> p h d", d=DK), AX.X, ALU.add).then_inc(prep_step, 1)
                        dve.wait_ge(prep_step, 6 * b + 2 * t + 2)
                        v.tensor_scalar(MS[:, t], MS[:, t], 1.0 / DK, EPS_RMS, ALU.mult, ALU.add).then_inc(ms_ready, 1)

                def over_rms(b, t):
                    dve.wait_ge(rt_ready, 2 * b + t + 1)
                    v.tensor_tensor(QK[:, t].rearrange("p (h d) -> p h d", d=DK),
                                    QK[:, t].rearrange("p (h d) -> p h d", d=DK),
                                    RT[:, t, :, None].broadcast_to((P, 32, DK)), ALU.mult).then_inc(prep_step, 1)

                def row_max(b, h):
                    dve.wait_ge(scores_ready, H * b + h + 1)
                    v.tensor_reduce(NM[:, 2 * h:2 * h + 2], sc_slot[h % 2].rearrange("p (t k) -> p t k", t=2),
                                    AX.X, ALU.max, negate=True).then_inc(scores_used, 1)

                def neg_max(b, j, n, w):
                    dve.wait_ge(scores_used, H * (b + 1))
                    v.tensor_copy(NMS[:, 0], NM[:]).then_inc(nm_step, 1)
                    dve.wait_ge(nm_step, 4 * b + 1)
                    v.tensor_tensor(NMR[:], NM[:], NMS[:, 0], ALU.subtract).then_inc(nm_step, 1)
                    dve.wait_ge(nm_step, 4 * b + 2)
                    v.tensor_copy(NMS[:, 1], NMR[:]).then_inc(nm_step, 1)
                    dve.wait_ge(nm_step, 4 * b + 3)
                    v.tensor_tensor(NMS[:, 2], NMR[:], NMS[:, 1], ALU.subtract).then_inc(nm_step, 1)
                    dve.wait_ge(work_full, w + 1)
                    if known(b, 2):
                        dve.wait_ge(nm_out[n], 16 * j)
                    v.tensor_copy(NMT[:, n, :], WB[0:3 * 2 * H, 0:P]).then_inc(work_free, 1)

                def half(b, k, w):
                    dve.wait_ge(work_full, w + 1)
                    pv = W_.rearrange("p (h t j e) -> p h t j e", h=2, t=2, j=4)
                    rec = REC[:].rearrange("p (h t j) -> p h t j", h=2, t=2)
                    v.reciprocal(rec.rearrange("p h t j -> p (h t) j"), pv.rearrange("p h t j e -> p (h t) j e")[:, :, :, DK]).then_inc(rec_ready, 1)
                    dve.wait_ge(rec_ready, 2 * b + k + 1)
                    for t in range(2):
                        i = v.tensor_tensor(O[:, t, k * P:(k + 1) * P].rearrange("p (h j d) -> p h j d", h=2, j=4), pv[:, :, t, :, 0:DK],
                                            rec[:, :, t, :, None].broadcast_to((P, 2, 4, DK)), ALU.mult)
                    i.then_inc(work_free, 1)

                def post(b, w):
                    xs = self.X[:, sl(2 * b, 2), :]
                    if not mha:
                        dve.wait_ge(work_full, w + 1)
                        if kind == "A":
                            dve.wait_ge(x_biased, b + 1)
                        gate = self.TG[:, 0:1] if kind == "A" else self.TG[:, 1:2]
                        v.scalar_tensor_tensor(xs, W2, gate, xs, ALU.mult, ALU.add).then_inc(work_free, 1)
                        dve.wait_ge(work_free, w + 1)
                        src = [self.X[:, sl(2 * b + t, 1), :].rearrange("p o d -> p (o d)") for t in range(2)]
                    else:
                        for t in range(2):
                            i = v.tensor_scalar(XR[:, t, :], self.X[:, sl(2 * b + t, 1), :].rearrange("p o d -> p (o d)"),
                                                self.MEAN[:, sl(2 * b + t, 1)], self.RSTD[:, sl(2 * b + t, 1)], ALU.subtract, ALU.mult)
                        i.then_inc(xr_ready, 1)
                        dve.wait_ge(xr_ready, b + 1)
                        dve.wait_ge(work_full, w + 1)
                        v.tensor_tensor(XR[:, :, M0:D], XR[:, :, M0:D], W_[:, 0:2 * MW].rearrange("p (t d) -> p t d", t=2), ALU.add).then_inc(work_free, 1)
                        dve.wait_ge(work_free, w + 1)
                        if known(b, 1):
                            dve.wait_ge(y_out, 16 * b)
                        v.scalar_tensor_tensor(YB[:], XR[:], self.TG[:, 3:4], xs, ALU.mult, ALU.add).then_inc(y_ready, 1)
                        dve.wait_ge(y_ready, b + 1)
                        v.tensor_scalar(xs, XR[:], 1.0, None, ALU.mult)
                        src = [XR[:, t, :] for t in range(2)]
                    for t in range(2):
                        v.bn_stats(self.ST[:, sl(2 * b + t, 1), :].rearrange("p o s -> p (o s)"), src[t]).then_inc(stats, 1)

                def item(x, i, j, n):
                    w = nth(i, x)
                    if x[0] == "p":
                        prep(int(x[1]), i + 2, w)
                    elif x in ("T0", "T1-"):
                        half(i - 1 if x == "T1-" else i, int(x[1]), w)
                    elif x == "NM":
                        neg_max(*at(i, 1, j, n), w)
                    elif x == "PR-":
                        post(i - 1, w)

                def prologue():
                    for b in range(2):
                        norm(b, None if b == 0 else nth(-2, "p0"))
                        for k in range(NPREP):
                            prep(k, b, nth(b - 2, f"p{k}"))
                            if mha and k in (2, 3):
                                over_rms(b, k - 2)
                    for h in range(H):
                        row_max(0, h)
                    neg_max(0, 0, 0, nth(-1, "NM"))

                def step(i, j, n):
                    if not (isinstance(i, int) and i + 2 >= B):
                        norm(i + 2, nth(i - 1, "p0"))
                    h = 0
                    for x in ORDER:
                        if not there(i, x):
                            continue
                        if x == "h":
                            row_max(i + 1, h)
                            h += 1
                        elif x[0] == "r":
                            over_rms(i + 2, int(x[1]))
                        elif x in ITEMS:
                            item(x, i, j, n)

                def tail():
                    for x in ("T1-", "OT-", "PR-"):
                        item(x, B, B // 2, 0)
                    dve.wait_ge(stats, 2 * B)

                steps(dve.Fori, prologue, step, tail)

            @block.tensor
            def _(pe):
                mm, tr = nc.tensor.matmul, nc.tensor.transpose
                pe.wait_ge(w_in, 16 * NW)
                if mha:
                    pe.wait_ge(w_scaled, 3)

                def use(w):
                    if known(w, 1):
                        pe.wait_ge(work_free, w)

                def transpose_rows(src, off=0):
                    for cc in range(DC):
                        for t in range(2):
                            i = tr(W_[:, cc * S + t * P:cc * S + (t + 1) * P], src[:, t, off + cc * P:off + (cc + 1) * P], self.IDF[:])
                    i.then_inc(work_full, 1)

                def prep(k, b, j, n, w):
                    if k == 0:
                        pe.wait_ge(xn_ready, b + 1)
                        use(w)
                        transpose_rows(XN)
                        return
                    use(w)
                    if not mha and k == 1:
                        for m in range(2):
                            for cc in range(DC):
                                i = mm(W_[:, m * S:(m + 1) * S], Wq[:, cc, m * P:(m + 1) * P], XNT[:, cc], start=cc == 0, stop=cc == DC - 1)
                    elif kind == "A":
                        pe.wait_ge(ctx_in[n], 16 * (j + 1))
                        for cc in range(DC):
                            mm(W_[:, 0:S], Wkv[:, cc, 0:P], CTX[:, n, cc], start=cc == 0, stop=cc == DC - 1)
                        for m in range(2):
                            for cc in range(DC):
                                i = mm(W_[:, S + m * DK:S + (m + 1) * DK], CTX[:, n, cc, m * P:(m + 1) * P], Wkv[:, cc, P:P + DK], start=cc == 0, stop=cc == DC - 1)
                    elif gathered and k == 2:
                        pe.wait_ge(ctx_in[n], 16 * (j + 1))
                        for t in range(2):
                            for cc in range(DC):
                                i = mm(W_[:, t * S:(t + 1) * S], QF[:, cc, t * P:(t + 1) * P], CTX[:, n, cc], start=cc == 0, stop=cc == DC - 1)
                    elif gathered and k == 3:
                        pe.wait_ge(prep_step, 3 * b + 3)
                        for m in range(2):
                            for t in range(2):
                                i = tr(WB[:, m * S + t * P:m * S + (t + 1) * P], OH[:, t, m * P:(m + 1) * P], self.IDB[:])
                    elif gathered and k == 4:
                        for m in range(2):
                            for cc in range(DC):
                                i = mm(W_[:, m * KVW:(m + 1) * KVW], CTX[:, n, cc, m * P:(m + 1) * P], Wkv[:, cc], start=cc == 0, stop=cc == DC - 1)
                    elif gathered and k == 5:
                        for m in range(2):
                            mm(W_[:, 0:S], KVP[:, m, 0:P], OHT[:, m], start=m == 0, stop=m == 1)
                        for t in range(2):
                            for m in range(2):
                                i = mm(W_[:, S + t * DK:S + (t + 1) * DK], OHT[:, m, t * P:(t + 1) * P], KVP[:, m, P:P + DK], start=m == 0, stop=m == 1)
                    elif mha and k in (1, 2):
                        for cc in range(DC):
                            i = mm(W_[:, :], XNT[:, cc, (k - 1) * P:k * P], Wq[:, cc, 0:2 * D], start=cc == 0, stop=cc == DC - 1)
                    elif mha and k == 3:
                        for t in range(2):
                            for cc in range(DC):
                                i = mm(W_[:, t * S:(t + 1) * S], XNT[:, cc, t * P:(t + 1) * P], Wq[:, cc, 2 * D:3 * D], start=cc == 0, stop=cc == DC - 1)
                    elif mha:
                        if k == 4:
                            pe.wait_ge(prep_step, 6 * b + 6)
                        transpose_rows(QK, (k - 4) * D)
                        return
                    i.then_inc(work_full, 1)

                def scores(b, j, n, h):
                    if h == 0:
                        pe.wait_ge(stack_in[n], 16 * NSI * (j + 1))
                    if isinstance(b, int) and b == 0:
                        if h >= 2:
                            pe.wait_ge(scores_used, h - 1)
                    else:
                        pe.wait_ge(scores_used, H * b + h - 1)
                    if mha:
                        mm(sc_slot[h % 2], self.IDB[:], MASKQ[:].rearrange("p t k -> p (t k)"), start=True, stop=True, skip_group_check=True)
                    for t in range(2):
                        i = mm(sc_slot[h % 2][:, t * S:(t + 1) * S], QS[0:KR, n, h, t * P:(t + 1) * P], KS[0:KR, n, h if mha else 0, :],
                               start=not mha, stop=True, skip_group_check=mha)
                    i.then_inc(scores_ready, 1)

                def scores_t(b, j, n, g):
                    if g == 0:
                        pe.wait_ge(nm_in[n], 16 * (j + 1))
                    if not (isinstance(b, int) and b == 0 and g < 2):
                        pe.wait_ge(exp_ready, 8 * b + g - 1)
                    slot = st_slot[g % 2]
                    if not mha:
                        for k in range(2):
                            i = mm(slot[:, k, :], KS[:, n, 0, k * P:(k + 1) * P], QS[:, n, 2 * g:2 * g + 2, :], start=True, stop=True)
                    else:
                        mm(slot[:, 0, :], self.IDB[:], MASKK[:, 0].rearrange("p h q -> p (h q)"), start=True, stop=True, skip_group_check=True)
                        for h in range(2):
                            mm(slot[:, 0, h * S:(h + 1) * S], KS[:, n, 2 * g + h, 0:P], QS[:, n, 2 * g + h, :], start=False, stop=True, skip_group_check=True)
                        mm(slot[:, 1, 0:S].rearrange("p (h q) -> p h q", h=2), self.IDB[:], MASKK[:, 1, :, 0:P], start=True, stop=True, skip_group_check=True)
                        for h in range(2):
                            i = mm(slot[:, 1, h * P:(h + 1) * P], KS[:, n, 2 * g + h, P:S], QS[:, n, 2 * g + h, P:S], start=False, stop=True, skip_group_check=True)
                    i.then_inc(st_ready, 1)

                def values(b, n, half):
                    pe.wait_ge(exp_ready, 8 * b + 4 * half + 4)
                    if half == 0:
                        pe.wait_ge(v_ready, b + 1)
                    if known(b, 1) or half:
                        pe.wait_ge(ov_ready, 2 * b + half)
                    tiles = [PVB[VW * j:VW * (j + 1), :] for j in range(4)]
                    if not mha:
                        for k in range(2):
                            for j in range(4):
                                i = mm(tiles[j], VP[:, n, k, 0, :], EX[:, 4 * half + j, k, :], start=k == 0, stop=k == 1)
                                if half and k == j == 0:
                                    i.then_inc(stack_used, 1)
                    else:
                        for h in range(2):
                            for j in range(4):
                                i = mm(tiles[j][:, h * S:(h + 1) * S], VP[:, n, 0, 2 * (4 * half + j) + h, :],
                                       EX[:, 4 * half + j, 0, h * S:(h + 1) * S], start=h == 0, stop=True, skip_group_check=True)
                                if half and h == j == 0:
                                    i.then_inc(stack_used, 1)
                        for h in range(2):
                            for j in range(4):
                                i = mm(tiles[j][:, h * S + P:(h + 1) * S], VP[:, n, 1, 2 * (4 * half + j) + h, :],
                                       EX[:, 4 * half + j, 1, h * P:(h + 1) * P], start=False, stop=True, skip_group_check=True)
                    i.then_inc(pv_done, 1)

                def item(x, i, j, n):
                    w = nth(i, x)
                    if x[0] == "p":
                        prep(int(x[1]), *at(i, 2, j, n), w)
                    elif x in ("T0", "T1-"):
                        k = int(x[1])
                        b = i - 1 if x == "T1-" else i
                        pe.wait_ge(ov_ready, 2 * b + k + 1)
                        use(w)
                        for u in range(4):
                            t_ = tr(W_[:, u * P:(u + 1) * P], OV[:, k, u * P:(u + 1) * P], self.IDF[:])
                        t_.then_inc(work_full, 1)
                    elif x == "OT-":
                        use(w)
                        transpose_rows(O)
                    elif x == "PR-":
                        use(w)
                        for t in range(2):
                            for cc in range(DC):
                                t_ = mm(W_[:, t * OW:(t + 1) * OW], OT[:, cc, t * P:(t + 1) * P], Wo[:, cc], start=cc == 0, stop=cc == DC - 1)
                        t_.then_inc(work_full, 1)
                    elif x == "NM":
                        pe.wait_ge(nm_step, 4 * (i + 2))
                        use(w)
                        tr(WB[0:3 * 2 * H, 0:P], NMS[:].rearrange("p t u -> p (t u)"), self.IDB[:]).then_inc(work_full, 1)

                def prologue():
                    for b in range(2):
                        for k in range(NPREP):
                            prep(k, b, 0, b, nth(b - 2, f"p{k}"))
                    pe.wait_ge(consts, N_CONST)
                    for h in range(H):
                        scores(0, 0, 0, h)
                    item("NM", -1, -1, 1)

                def step(i, j, n):
                    h = 0
                    for x in ORDER:
                        if not there(i, x):
                            continue
                        if x[0] == "s":
                            scores_t(i, j, n, int(x[1]))
                        elif x == "h":
                            scores(*at(i, 1, j, n), h)
                            h += 1
                        elif x[0] == "v":
                            values(i, n, int(x[1]))
                        elif x in ITEMS:
                            item(x, i, j, n)

                def tail():
                    for x in ("T1-", "OT-", "PR-"):
                        item(x, B, B // 2, 0)

                steps(pe.Fori, prologue, step, tail)

    def bit_ffn(self):
        nc, a = self.nc, self.a
        KH1, KH2 = DC, HID1 // P
        with ExitStack() as c:
            def sb(name, shape, dt=F32):
                return c.enter_context(nc.sbuf_tensor(f"b_{name}", shape, dt))

            def sem(name):
                return c.enter_context(nc.semaphore(f"b_{name}"))
            WF = sb("w_float", [P, 2, KH1 * HID1])
            W1 = sb("w1", [P, KH1, HID1], BF16)
            W2 = sb("w2", [P, KH2, D], BF16)
            N1 = sb("n1", [P, D])
            N2 = sb("n2", [P, HID1])
            AB = sb("act_scale_bias", [P, 2])
            ONES = sb("ones", [P, P])
            WS = sb("w_sum", [P, 1])
            WM = sb("w_mean", [P, 2])
            WI = sb("w_scale", [P, 2])
            WG = sb("w2_mean_gate", [P, 1])
            XB = sb("xb", [P, D])
            QA = sb("qa", [P, D])
            QB = sb("qb", [P, D], BF16)
            QT = sb("qt", [P, KH1, P], BF16)
            S1 = sb("s1", [P, 4])
            C1 = sb("c1", [P, 2])
            R = sb("r", [P, 2, HID1])
            G = sb("g", [P, 2, HID1])
            RS = sb("r_scaled", [P, HID1])
            MINUS_RND = sb("minus_rnd", [P, 1])
            SQ = sb("sq", [P, HID1])
            S2 = sb("s2", [P, 12])
            MSQ = sb("msq", [P, 1])
            Y2 = sb("y2", [P, HID1])
            Q2 = sb("q2", [P, HID1])
            Q2B = sb("q2b", [P, HID1], BF16)
            Q2T = sb("q2t", [P, KH2, P], BF16)
            C2 = sb("c2", [P, 2])
            PS = self.PS
            TB = PS[:, 0, 0:P].bitcast(BF16)
            HB = [PS[:, 1 + 2 * n:3 + 2 * n, :] for n in range(2)]
            T2B = PS[:, 5, :].bitcast(BF16)
            YB = PS[:, 6, 0:D]
            SB = PS[:, 7, 0:1]
            W2_COLS = PS[:, 1:5, :].rearrange("p k f -> p (k f)")

            w_in, ones, sums, w_sum, w_ready = sem("w_in"), sem("ones"), sem("sums"), sem("w_sum"), sem("w_ready")
            q_ready, qt_ready, qt_evac = sem("q_ready"), sem("qt_psum"), sem("qt_sbuf")
            h_ready, r_ready, g_ready, sq_ready = sem("h_ready"), sem("relu_ready"), sem("g_ready"), sem("sum_sq_ready")
            rs_ready = sem("relu_scaled")
            ms_ready, root_ready, q2f_ready, y2_ready = sem("ms_ready"), sem("root_ready"), sem("q2_float_ready"), sem("y2_ready")
            q2_ready, q2t_ready, q2t_evac, y_ready, y_used = sem("q2_ready"), sem("q2t_psum"), sem("q2t_sbuf"), sem("y_ready"), sem("y_used")
            c1_ready, front_step, back_step, stats = sem("c1_ready"), sem("front_step"), sem("back_step"), sem("stats")
            block = c.enter_context(nc.Block())

            def steps(loop, step):
                for t in range(-2, 2):
                    step(t, t % 2)
                with loop(1, NT // 2 - 1) as j:
                    for n in range(2):
                        step(2 * j + n, n)
                for t in range(NT - 2, NT + 2):
                    step(t, t % 2)

            def there(t, d):
                return not isinstance(t, int) or 0 <= t + d < NT

            def known(t, least):
                return not (isinstance(t, int) and t < least)

            @block.sync
            def _(sp):
                sp.dma_start(WF[:, 0, :].rearrange("p (c h) -> p c h", c=KH1), a["B_w1"].rearrange("(c p) h -> p c h", p=P)).then_inc(w_in, 16)
                sp.dma_start(WF[:, 1, :].rearrange("p (c h) -> p c h", c=KH2), a["B_w2"].rearrange("(c p) h -> p c h", p=P)).then_inc(w_in, 16)
                sp.dma_start(N1[:], a["L0_ffn_norm1_w"][None, :].broadcast_to((P, D))).then_inc(w_in, 16)
                sp.dma_start(N2[:], a["L0_ffn_norm2_w"][None, :].broadcast_to((P, HID1))).then_inc(w_in, 16)
                sp.dma_start(AB[:, 0:1], a["L0_ffn_act_scale"][None, :].broadcast_to((P, 1))).then_inc(w_in, 16)
                sp.dma_start(AB[:, 1:2], a["L0_ffn_act_bias"][None, :].broadcast_to((P, 1))).then_inc(w_in, 16)

            @block.gpsimd
            def _(pool):
                g = nc.gpsimd
                g.memset(ONES[:], 1.0).then_inc(ones, 1)
                g.memset(MINUS_RND[:], -RND).then_inc(ones, 1)
                pool.wait_ge(ones, 2)

                def step(t, n):
                    if there(t, 1):
                        pool.wait_ge(rs_ready, t + 2)
                        if known(t, 1):
                            pool.wait_ge(y2_ready, t)
                        g.tensor_tensor(G[:, 1 - n], RS[:], R[:, 1 - n], ALU.mult).then_inc(g_ready, 1)

                steps(pool.Fori, step)

            @block.scalar
            def _(act):
                s_ = nc.scalar
                act.wait_ge(ones, 2)
                act.wait_ge(w_in, 16 * 6)
                s_.activation(R[:].rearrange("p n h -> p (n h)"), WF[:, 1, :], ACT.Abs).then_inc(sums, 1)

                def root(t):
                    act.wait_ge(ms_ready, t + 1)
                    s_.activation(S2[:, 1:2], S2[:, 0:1], ACT.Sqrt).then_inc(root_ready, 1)

                def last(t):
                    act.wait_ge(q2t_ready, t + 1)
                    s_.activation(Q2T[:], T2B.rearrange("p (c q) -> p c q", c=KH2), ACT.Copy).then_inc(q2t_evac, 1)

                def relu(t, n):
                    act.wait_ge(c1_ready, t + 1)
                    act.wait_ge(h_ready, t + 1)
                    if known(t, 2):
                        act.wait_ge(g_ready, t - 1)
                    s_.activation(R[:, n].rearrange("p (k f) -> p k f", k=2), HB[n], ACT.Relu, scale=C1[:, n:n + 1]).then_inc(r_ready, 1)

                def relu_scaled(t, n):
                    act.wait_ge(r_ready, t + 1)
                    if known(t, 1):
                        act.wait_ge(g_ready, t)
                    s_.activation(RS[:], R[:, n], ACT.Copy, scale=AB[:, 0:1]).then_inc(rs_ready, 1)

                def squares(t, n):
                    act.wait_ge(g_ready, t + 1)
                    s_.activation(SQ[:], G[:, n], ACT.Square, bias=AB[:, 1:2], accum_out=MSQ[:]).then_inc(sq_ready, 1)

                def front(t):
                    act.wait_ge(qt_ready, t + 1)
                    s_.activation(QT[:], TB.rearrange("p (c q) -> p c q", c=KH1), ACT.Copy).then_inc(qt_evac, 1)

                def middle(t):
                    act.wait_ge(q2f_ready, t + 1)
                    if known(t, 1):
                        act.wait_ge(q2t_ready, t)
                    s_.activation(Q2B[:], Q2[:], ACT.Identity, bias=MINUS_RND[:]).then_inc(q2_ready, 1)

                def step(t, n):
                    if there(t, 1):
                        relu(t + 1, 1 - n)
                    if there(t, 0):
                        root(t)
                    if there(t, 1):
                        relu_scaled(t + 1, 1 - n)
                    if there(t, -1):
                        last(t - 1)
                    if there(t, 2):
                        front(t + 2)
                    if there(t, 0):
                        middle(t)
                    if there(t, 1):
                        squares(t + 1, 1 - n)

                steps(act.Fori, step)

            @block.vector
            def _(dve):
                v = nc.vector

                def setup_link(ins):
                    self.np_steps += 1
                    ins.then_inc(self.np_step, 1)
                    dve.wait_ge(self.np_step, self.np_steps)

                dve.wait_ge(w_in, 16 * 6)
                v.tensor_reduce(WS[:], WF[:, 0, :], AX.X, ALU.add, apply_absolute_value=True).then_inc(sums, 1)
                dve.wait_ge(w_sum, 1)
                setup_link(v.tensor_reduce(WM[:, 1:2], W2_COLS, AX.X, ALU.add))
                setup_link(v.tensor_copy(WM[:, 0:1], SB))
                setup_link(v.tensor_scalar(WM[:], WM[:], 1.0 / (D * HID1), EPS_Q, ALU.mult, ALU.max))
                setup_link(v.reciprocal(WI[:], WM[:]))
                setup_link(v.tensor_scalar(WG[:], WM[:, 1:2], self.TG[:, 2:3], None, ALU.mult))
                for w, wq in ((0, W1), (1, W2)):
                    setup_link(v.tensor_scalar(WF[:, w, :], WF[:, w, :], WI[:, w:w + 1], RND, ALU.mult, ALU.add))
                    setup_link(v.tensor_scalar(WF[:, w, :], WF[:, w, :], RND, 1.0, ALU.subtract, ALU.min))
                    v.tensor_scalar(wq[:].rearrange("p c h -> p (c h)"), WF[:, w, :], -1.0, None, ALU.max).then_inc(w_ready, 1)

                NF, NB = 7, 9

                def y_update(t, n):
                    dve.wait_ge(y_ready, t + 1)
                    dve.wait_ge(back_step, NB * (t + 1))
                    xs = self.X[:, sl(t, 1), :].rearrange("p o d -> p (o d)")
                    v.scalar_tensor_tensor(xs, YB, C2[:, n:n + 1], xs, ALU.mult, ALU.add).then_inc(y_used, 1)

                def y_stats(t):
                    dve.wait_ge(y_used, t + 1)
                    v.bn_stats(self.ST[:, sl(t, 1), :].rearrange("p o s -> p (o s)"),
                               self.X[:, sl(t, 1), :].rearrange("p o d -> p (o d)")).then_inc(stats, 1)

                def step(t, n):
                    mid, fr, up, u = there(t, 0), there(t, 2), there(t, -2), t + 2

                    def f(k, ins):
                        ins.then_inc(front_step, 1)

                    def f_after(k):
                        dve.wait_ge(front_step, NF * u + k)

                    def m(k, ins):
                        ins.then_inc(back_step, 1)

                    def m_after(k):
                        dve.wait_ge(back_step, NB * t + k)

                    if mid:
                        dve.wait_ge(g_ready, t + 1)
                        if known(t, 1):
                            dve.wait_ge(q2f_ready, t)
                        v.scalar_tensor_tensor(Y2[:], G[:, n], AB[:, 1:2], N2[:], ALU.add, ALU.mult).then_inc(y2_ready, 1)
                    if fr:
                        if known(u, 1):
                            dve.wait_ge(front_step, NF * u)
                        f(1, v.tensor_scalar(XB[:], self.X[:, sl(u, 1), :].rearrange("p o d -> p (o d)"),
                                             self.MEAN[:, sl(u, 1)], self.RRMS[:, sl(u, 1)], ALU.subtract, ALU.mult))
                    if mid:
                        dve.wait_ge(y2_ready, t + 1)
                        if known(t, 1):
                            dve.wait_ge(back_step, NB * t)
                        m(1, v.tensor_reduce(S2[:, 2:3], Y2[:], AX.X, ALU.max, apply_absolute_value=True))
                    if up:
                        y_update(t - 2, n)
                    if mid:
                        dve.wait_ge(sq_ready, t + 1)
                        v.tensor_scalar(S2[:, 0:1], MSQ[:], 1.0 / HID1, EPS_NORM, ALU.mult, ALU.add).then_inc(ms_ready, 1)
                    if fr:
                        f_after(1)
                        f(2, v.tensor_tensor(XB[:], XB[:], N1[:], ALU.mult))
                    if fr:
                        f_after(2)
                        f(3, v.tensor_reduce(S1[:, 0:1], XB[:], AX.X, ALU.max, apply_absolute_value=True))
                        f_after(3)
                        if known(u, 1):
                            dve.wait_ge(c1_ready, u)
                        f(4, v.tensor_scalar(S1[:, 1:2], S1[:, 0:1], EPS_Q, None, ALU.max))
                    if mid:
                        dve.wait_ge(root_ready, t + 1)
                        m(2, v.reciprocal(S2[:, 3:4], S2[:, 1:2]))
                    if fr:
                        f_after(4)
                        f(5, v.reciprocal(S1[:, 3:4], S1[:, 1:2]))
                    if mid:
                        m_after(2)
                        m(3, v.tensor_scalar(S2[:, 4:5], S2[:, 3:4], S2[:, 3:4], S2[:, 0:1], ALU.mult, ALU.mult))
                    if fr:
                        f_after(5)
                        f(6, v.tensor_scalar(S1[:, 2:3], S1[:, 3:4], 127.0, None, ALU.mult))
                    if mid:
                        m_after(3)
                        m(4, v.tensor_scalar(S2[:, 4:5], S2[:, 4:5], -0.5, 1.5, ALU.mult, ALU.add))
                    if up:
                        y_stats(t - 2)
                    if fr:
                        f_after(6)
                        if known(u, 1):
                            dve.wait_ge(q_ready, u)
                        f(7, v.tensor_scalar(QA[:], XB[:], S1[:, 2:3], RND, ALU.mult, ALU.add))
                    if mid:
                        m_after(4)
                        m(5, v.tensor_scalar(S2[:, 5:6], S2[:, 4:5], S2[:, 3:4], None, ALU.mult))
                    if fr:
                        f_after(7)
                        if known(u, 1):
                            dve.wait_ge(qt_ready, u)
                        v.tensor_scalar(QB[:], QA[:], RND, None, ALU.subtract).then_inc(q_ready, 1)
                    if mid:
                        m_after(5)
                        m(6, v.tensor_scalar(S2[:, 6:7], S2[:, 2:3], S2[:, 5:6], EPS_Q, ALU.mult, ALU.max))
                    if mid:
                        m_after(6)
                        m(7, v.reciprocal(S2[:, 7:8], S2[:, 6:7]))
                    if mid:
                        m_after(7)
                        m(8, v.tensor_scalar(S2[:, 8:9], S2[:, 7:8], 127.0, S2[:, 5:6], ALU.mult, ALU.mult))
                    if fr:
                        if known(u, 2):
                            dve.wait_ge(r_ready, u - 1)
                        v.tensor_scalar(C1[:, n:n + 1], S1[:, 1:2], 1.0 / 127.0, WM[:, 0:1], ALU.mult, ALU.mult).then_inc(c1_ready, 1)
                    if mid:
                        m_after(8)
                        if known(t, 1):
                            dve.wait_ge(q2_ready, t)
                        v.tensor_scalar(Q2[:], Y2[:], S2[:, 8:9], RND, ALU.mult, ALU.add).then_inc(q2f_ready, 1)
                    if mid:
                        m(9, v.tensor_scalar(C2[:, n:n + 1], S2[:, 6:7], 1.0 / 127.0, WG[:, 0:1], ALU.mult, ALU.mult))

                steps(dve.Fori, step)
                dve.wait_ge(stats, NT)

            @block.tensor
            def _(pe):
                mm, tr = nc.tensor.matmul, nc.tensor.transpose
                pe.wait_ge(ones, 1)
                pe.wait_ge(sums, 2)
                mm(SB, ONES[:], WS[:], start=True, stop=True)
                w2_abs = R[:].rearrange("p n (k f) -> p (n k) f", f=512)
                for k in range(4):
                    i = mm(PS[:, 1 + k, :], ONES[:], w2_abs[:, k], start=True, stop=True)
                i.then_inc(w_sum, 1)
                pe.wait_ge(w_ready, 2)

                def front(t, n):
                    pe.wait_ge(q_ready, t + 1)
                    if known(t, 1):
                        pe.wait_ge(qt_evac, t)
                    for cc in range(KH1):
                        i = tr(TB[:, cc * P:(cc + 1) * P], QB[:, cc * P:(cc + 1) * P], self.IDB[:])
                    i.then_inc(qt_ready, 1)

                def front_product(t, n):
                    pe.wait_ge(qt_evac, t + 1)
                    if known(t, 2):
                        pe.wait_ge(r_ready, t - 1)
                    for k in range(2):
                        for cc in range(KH1):
                            i = mm(HB[n][:, k, :], QT[:, cc], W1[:, cc, k * 512:(k + 1) * 512], start=cc == 0, stop=cc == KH1 - 1)
                    i.then_inc(h_ready, 1)

                def last(t):
                    pe.wait_ge(q2_ready, t + 1)
                    if known(t, 1):
                        pe.wait_ge(q2t_evac, t)
                    for cc in range(KH2):
                        i = tr(T2B[:, cc * P:(cc + 1) * P], Q2B[:, cc * P:(cc + 1) * P], self.IDB[:])
                    i.then_inc(q2t_ready, 1)

                def last_product(t):
                    pe.wait_ge(q2t_evac, t + 1)
                    if known(t, 1):
                        pe.wait_ge(y_used, t)
                    for cc in range(KH2):
                        i = mm(YB, Q2T[:, cc], W2[:, cc], start=cc == 0, stop=cc == KH2 - 1)
                    i.then_inc(y_ready, 1)

                def step(t, n):
                    if there(t, -1):
                        last(t - 1)
                    if there(t, 2):
                        front(t + 2, n)
                    if there(t, -1):
                        last_product(t - 1)
                    if there(t, 2):
                        front_product(t + 2, n)

                steps(pe.Fori, step)

    def experts(self):
        nc, a = self.nc, self.a
        NG, TG_ = NT // 4, 4
        first = ("e2_l1", "e3_down", "e0_up", "e1_w1", "e1_w2")
        layers = [("e2_l1", None, 0), ("e3_down", None, 1), ("e2_l2", 0, 2), ("e3_up", 1, 3), ("e2_l3", 2, 0),
                  ("e0_up", None, 1), ("e1_w1", None, 2), ("e1_w2", None, 2)]
        blocks = {"e2_l1": 4, "e3_down": 2, "e2_l2": 4, "e3_up": 4, "e2_l3": 4, "e0_up": 4, "e1_w1": 4, "e1_w2": 4}
        chunks = {n: DC if n in first else 4 for n in blocks}
        chunks["e3_up"] = 2
        outs = [("e2_l4", 0, 2), ("e3_out", 3, 3), ("e0_down", 1, 0), ("e1_down", 2, 1)]
        NBLK = sum(blocks.values())
        RING = 5

        def known(g, least):
            return not (isinstance(g, int) and g < least)

        def steps(loop, step, extra=0):
            for g in range(2):
                step(g, 0, g)
            with loop(1, NG // 2 - 1) as j:
                for n in range(2):
                    step(2 * j + n, j, n)
            for g in range(NG - 2, NG + extra):
                step(g, g // 2, g % 2)

        with ExitStack() as c:
            def sb(name, shape, dt=F32):
                return c.enter_context(nc.sbuf_tensor(f"e_{name}", shape, dt))

            def sem(name):
                return c.enter_context(nc.semaphore(f"e_{name}"))
            W = {n: sb(n, [P, chunks[n], blocks[n] * P]) for n in blocks}
            WO = {n: sb(n, [P, 4, MW]) for n, _, _ in outs}
            GW = sb("gate", [P, DC, E])
            N2 = sb("n2", [P, DC])
            LG = sb("logits", [P, NT, E])
            RK = sb("rank", [P, NT, E])
            M = sb("m", [P, NT])
            XF = sb("xf", [P, 2, TG_, D])
            XT = sb("xt", [P, 2, DC, 512])
            gate_in, w_in, w_ready = sem("gate_in"), sem("w_in"), sem("w_ready")
            N_W = len(blocks) + len(outs)

            def norm(g, n):
                for t in range(TG_):
                    i = nc.vector.tensor_scalar(XF[:, n, t], self.X[:, sl(4 * g + t, 1), :].rearrange("p o d -> p (o d)"),
                                                self.RSTD[:, sl(4 * g + t, 1)], None, ALU.mult)
                return i

            with ExitStack() as rc:
                def rsem(name):
                    return rc.enter_context(nc.semaphore(f"r_{name}"))
                gate_ready, xf_ready = rsem("gate_ready"), rsem("xf_ready")
                t_ready, t_evac, l_ready, l_used = rsem("xt_psum"), rsem("xt_sbuf"), rsem("logits_psum"), rsem("logits_used")
                block = rc.enter_context(nc.Block())
                tb = [self.PS[:, 2 * n:2 * n + 2, :] for n in range(2)]
                lb = [self.PS[:, 4 + n, 0:TG_ * E] for n in range(2)]

                @block.sync
                def _(sp):
                    sp.dma_start(GW[:], a["E_gate"].rearrange("(c p) e -> p c e", p=P)).then_inc(gate_in, 16)
                    sp.dma_start(N2[:], a["E_n2"]).then_inc(gate_in, 16)
                    for n in blocks:
                        sp.dma_start(W[n][:], a["E_" + n].rearrange("(c p) h -> p c h", p=P)).then_inc(w_in, 16)
                    for n, _, _ in outs:
                        sp.dma_start(WO[n][:], a["E_" + n][:, M0:].rearrange("(c p) h -> p c h", p=P)).then_inc(w_in, 16)

                @block.tensor
                def _(pe):
                    pe.wait_ge(gate_ready, DC)

                    def logits(g, n):
                        pe.wait_ge(t_evac, g + 1)
                        if known(g, 2):
                            pe.wait_ge(l_used, g - 1)
                        for t in range(TG_):
                            for cc in range(DC):
                                i = nc.tensor.matmul(lb[n][:, t * E:(t + 1) * E], XT[:, n, cc, t * P:(t + 1) * P], GW[:, cc],
                                                     start=cc == 0, stop=cc == DC - 1)
                        i.then_inc(l_ready, 1)

                    def step(g, j, n):
                        if not (isinstance(g, int) and g == NG):
                            pe.wait_ge(xf_ready, g + 1)
                            if known(g, 2):
                                pe.wait_ge(t_evac, g - 1)
                            for cc in range(DC):
                                for t in range(TG_):
                                    i = nc.tensor.transpose(tb[n][:, cc, t * P:(t + 1) * P], XF[:, n, t, cc * P:(cc + 1) * P], self.IDF[:])
                            i.then_inc(t_ready, 1)
                        if known(g, 1):
                            logits(g - 1, 1 - n)

                    steps(pe.Fori, step, 1)

                @block.scalar
                def _(act):
                    def step(g, j, n):
                        act.wait_ge(t_ready, g + 1)
                        if known(g, 2):
                            act.wait_ge(l_ready, g - 1)
                        nc.scalar.activation(XT[:, n], tb[n], ACT.Copy).then_inc(t_evac, 1)

                    steps(act.Fori, step)

                @block.vector
                def _(dve):
                    v = nc.vector
                    dve.wait_ge(gate_in, 32)
                    for cc in range(DC):
                        v.tensor_scalar(GW[:, cc], GW[:, cc], N2[:, cc:cc + 1], None, ALU.mult).then_inc(gate_ready, 1)

                    def step(g, j, n):
                        if not (isinstance(g, int) and g == NG):
                            if known(g, 2):
                                dve.wait_ge(t_ready, g - 1)
                            norm(g, n).then_inc(xf_ready, 1)
                        if known(g, 1):
                            dve.wait_ge(l_ready, g)
                            v.tensor_scalar(LG[:, sl(4 * (g - 1), 4), :], lb[1 - n].rearrange("p (t e) -> p t e", e=E),
                                            1.0, None, ALU.mult).then_inc(l_used, 1)

                    steps(dve.Fori, step, 1)
                    dve.wait_ge(w_in, 16 * N_W)
                    for n in first:
                        for cc in range(DC):
                            v.tensor_scalar(W[n][:, cc], W[n][:, cc], N2[:, cc:cc + 1], None, ALU.mult).then_inc(w_ready, 1)
                    dve.wait_ge(l_used, NG)

            HB = [sb(f"hidden{n}", [P, 4, 512]) for n in range(4)]
            Y = sb("y", [P, 2, TG_, D])
            xf_ready = sem("xf_ready")
            e_in, e_out = sem("exp_in"), sem("exp_out")
            t_ready, t_evac = sem("xt_psum"), sem("xt_sbuf")
            blk_ready, blk_used = sem("block_psum"), sem("block_used")
            o_ready, o_used = sem("out_psum"), sem("out_used")
            y_in = [sem(f"y_in{n}") for n in range(2)]
            y_out = [sem(f"y_out{n}") for n in range(2)]
            block = c.enter_context(nc.Block())
            ring = [self.PS[:, n, :] for n in range(RING)]
            ob = [self.PS[:, RING + n, 0:MW] for n in range(2)]
            tb = self.PS[:, 7, :]
            assert NBLK % RING == 0

            def more(g):
                return not (isinstance(g, int) and g == NG - 1)

            @block.sync
            def _(sp):
                def load(g, j, n):
                    if known(g, 2):
                        sp.wait_ge(y_out[n], 16 * j)
                    sp.dma_start(Y[:, n], self.out_rows[:, sl(4 * g, 4), :]).then_inc(y_in[n], 16)

                def step(g, j, n):
                    load(g, j, n)
                    sp.wait_ge(o_used, 16 * g + 16)
                    sp.dma_start(self.out_rows[:, sl(4 * g, 4), :], Y[:, n]).then_inc(y_out[n], 16)

                steps(sp.Fori, step)
                for n in range(2):
                    sp.wait_ge(y_out[n], 16 * (NG // 2))

            @block.vector
            def _(dve):
                v = nc.vector

                def link(ins):
                    self.np_steps += 1
                    ins.then_inc(self.np_step, 1)
                    dve.wait_ge(self.np_step, self.np_steps)

                def wide(col):
                    return col[:, :, None].broadcast_to((P, NT, E))

                def row_weights():
                    big = 3.4028234663852886e38
                    link(v.tensor_scalar(LG[:], LG[:], big, -big, ALU.min, ALU.max))
                    link(v.tensor_reduce(M[:], LG[:], AX.X, ALU.max))
                    v.tensor_tensor(LG[:], LG[:], wide(M), ALU.subtract).then_inc(e_in, 1)
                    dve.wait_ge(e_out, 1)
                    link(v.tensor_reduce(M[:], LG[:], AX.X, ALU.add))
                    link(v.reciprocal(M[:], M[:]))
                    link(v.tensor_tensor(LG[:], LG[:], wide(M), ALU.mult))
                    link(v.memset(RK[:], 0.0))
                    for lo in range(E):
                        for hi in range(lo + 1, E):
                            link(v.tensor_tensor(M[:], LG[:, :, lo], LG[:, :, hi], ALU.is_ge))
                            link(v.tensor_tensor(RK[:, :, hi], RK[:, :, hi], M[:], ALU.add))
                            link(v.tensor_scalar(M[:], M[:], -1.0, 1.0, ALU.mult, ALU.add))
                            link(v.tensor_tensor(RK[:, :, lo], RK[:, :, lo], M[:], ALU.add))
                    link(v.tensor_scalar(RK[:], RK[:], 2.0, None, ALU.is_lt))
                    link(v.tensor_tensor(LG[:], LG[:], RK[:], ALU.mult))
                    link(v.tensor_reduce(M[:], LG[:], AX.X, ALU.add))
                    link(v.tensor_scalar(M[:], M[:], 1e-8, None, ALU.add))
                    link(v.reciprocal(M[:], M[:]))
                    link(v.tensor_tensor(LG[:], LG[:], wide(M), ALU.mult))
                    link(v.tensor_scalar(self.WTS[:], LG[:], self.TG[:, 3:4], None, ALU.mult))

                norm(0, 0).then_inc(xf_ready, 1)
                row_weights()

                def step(g, j, n):
                    if more(g):
                        if known(g, 1):
                            dve.wait_ge(t_ready, DC * g)
                        norm(g + 1, 1 - n).then_inc(xf_ready, 1)
                    for b in range(blocks["e1_w2"]):
                        at = NBLK - 4 + b
                        dve.wait_ge(blk_ready, NBLK * g + at + 1)
                        dve.wait_ge(blk_used, NBLK * g + NBLK - 4 + b)
                        v.tensor_tensor(HB[2][:, b], HB[2][:, b], ring[at % RING], ALU.mult).then_inc(blk_used, 1)
                    dve.wait_ge(y_in[n], 16 * (j + 1))
                    m = 0
                    for name, buf, e in outs:
                        for t in range(TG_):
                            dve.wait_ge(o_ready, 16 * g + m + 1)
                            if m >= TG_:
                                dve.wait_ge(o_used, 16 * g + m - TG_ + 1)
                            v.scalar_tensor_tensor(Y[:, n, t, M0:D], ob[m % 2], self.WTS[:, sl(4 * g + t, 1), e],
                                                   Y[:, n, t, M0:D], ALU.mult, ALU.add).then_inc(o_used, 1)
                            m += 1

                steps(dve.Fori, step)

            @block.scalar
            def _(act):
                s_ = nc.scalar

                def rows_t(g, n):
                    for cc in range(DC):
                        act.wait_ge(t_ready, DC * g + cc + 1)
                        s_.activation(XT[:, n, cc], tb, ACT.Copy).then_inc(t_evac, 1)

                rows_t(0, 0)
                act.wait_ge(e_in, 1)
                s_.activation(LG[:], LG[:], ACT.Exp).then_inc(e_out, 1)

                def step(g, j, n):
                    at = 0
                    for name, _, buf in layers[:-1]:
                        for b in range(blocks[name]):
                            act.wait_ge(blk_ready, NBLK * g + at + 1)
                            s_.activation(HB[buf][:, b], ring[at % RING], ACT.Silu if name == "e1_w1" else ACT.Gelu).then_inc(blk_used, 1)
                            at += 1
                    act.wait_ge(blk_used, NBLK * g + NBLK)
                    if more(g):
                        rows_t(g + 1, 1 - n)

                steps(act.Fori, step)

            @block.tensor
            def _(pe):
                mm = nc.tensor.matmul

                def rows_t(g, n):
                    pe.wait_ge(xf_ready, g + 1)
                    for cc in range(DC):
                        if known(g, 1) or cc:
                            pe.wait_ge(t_evac, DC * g + cc)
                        for t in range(TG_):
                            i = nc.tensor.transpose(tb[:, t * P:(t + 1) * P], XF[:, n, t, cc * P:(cc + 1) * P], self.IDF[:])
                        i.then_inc(t_ready, 1)

                rows_t(0, 0)

                def step(g, j, n):
                    pe.wait_ge(t_evac, DC * g + DC)
                    at = 0
                    done_at = {}
                    for name, src, buf in layers:
                        if src is not None:
                            pe.wait_ge(blk_used, NBLK * g + done_at[src])
                        for b in range(blocks[name]):
                            if at >= RING:
                                pe.wait_ge(blk_used, NBLK * g + at - RING + 1)
                            for cc in range(chunks[name]):
                                rhs = XT[:, n, cc] if src is None else HB[src][:, cc]
                                i = mm(ring[at % RING], W[name][:, cc, b * P:(b + 1) * P], rhs, start=cc == 0, stop=cc == chunks[name] - 1)
                            i.then_inc(blk_ready, 1)
                            at += 1
                        done_at[buf] = at
                    if more(g):
                        rows_t(g + 1, 1 - n)
                    m = 0
                    for name, buf, e in outs:
                        pe.wait_ge(blk_used, NBLK * g + done_at[buf])
                        for t in range(TG_):
                            if known(g, 1) or m > 1:
                                pe.wait_ge(o_used, 16 * g + max(m - 1, 0))
                            for cc in range(4):
                                i = mm(ob[m % 2], HB[buf][:, cc, t * P:(t + 1) * P], WO[name][:, cc], start=cc == 0, stop=cc == 3)
                            i.then_inc(o_ready, 1)
                            m += 1

                steps(pe.Fori, step)


def kernel(**inputs):
    import numpy as _np
    import concourse.bacc as _bacc
    from concourse import mybir as _mybir
    from concourse.bass_utils import run_bass_kernel_spmd as _run

    g = {k: _np.asarray(v) for k, v in inputs.items()}
    rep = P // DK

    def t(name):
        return _np.ascontiguousarray(g[name].T)

    by_half = _np.arange(D).reshape(2, 4, 2, DK).transpose(0, 2, 1, 3).reshape(-1)

    lay = {
        "x": g["x"],
        "ctx_t": _np.ascontiguousarray(g["ctx_1024"].transpose(0, 2, 1)),
        "g_xattn": g["g_xattn"], "g_ffn": g["g_ffn"],
        "L0_xattn_Wq": g["L0_xattn_Wq"], "L0_xattn_Wo": g["L0_xattn_Wo"][by_half],
        "A_wkv": _np.concatenate([_np.tile(g["L0_xattn_Wk"], (1, rep)), g["L0_xattn_Wv"]], axis=1),
        "A_part_bias": _np.stack([g["L0_xattn_bq"][:P], g["L0_xattn_bq"][P:], _np.tile(g["L0_xattn_bk"], rep)], axis=1),
        "A_free_bias": _np.concatenate([g["L0_xattn_bo"], g["L0_xattn_bv"]]),
        "B_w1": t("L0_ffn_w1"), "B_w2": t("L0_ffn_w2"),
        "L0_ffn_norm1_w": g["L0_ffn_norm1_w"], "L0_ffn_norm2_w": g["L0_ffn_norm2_w"],
        "L0_ffn_act_scale": g["L0_ffn_act_scale"], "L0_ffn_act_bias": g["L0_ffn_act_bias"],
        "C_wq": t("L1_xattn_Wq"), "C_wc": t("L1_xattn_Wc")[by_half],
        "C_wkv": _np.concatenate([_np.tile(g["L1_xattn_Wkv"][:DK].T, (1, rep)), g["L1_xattn_Wkv"][DK:].T], axis=1),
        "D_wq": t("L1_ffn_wq"), "D_wk": t("L1_ffn_wk"), "D_wv": t("L1_ffn_wv"), "D_wo": t("L1_ffn_wo")[by_half],
        "D_part_w": _np.stack([_np.tile(g["L1_ffn_qn_w"], rep), _np.tile(g["L1_ffn_kn_w"], rep)], axis=1),
        "L1_ffn_n1_w": g["L1_ffn_n1_w"],
        "E_gate": t("L1_ffn_gate_w"),
        "E_n2": _np.ascontiguousarray(g["L1_ffn_n2_w"].reshape(DC, P).T),
    }
    for n in ("e0_up", "e0_down", "e1_w1", "e1_w2", "e1_down", "e2_l1", "e2_l2", "e2_l3", "e2_l4", "e3_down", "e3_up", "e3_out"):
        lay["E_" + n] = t("L1_ffn_" + n)

    nc = _bacc.Bacc("TRN2", target_bir_lowering=False, num_devices=1)
    arrays, args = {}, {}
    for name, v in lay.items():
        v = _np.ascontiguousarray(v)
        arrays[f"in_{name}_dram"] = v
        args[name] = nc.dram_tensor(f"in_{name}_dram", v.shape, _mybir.dt.from_np(v.dtype), kind="ExternalInput").ap()
    out = nc.dram_tensor("out_0_dram", (B, S, D), _mybir.dt.float32, kind="ExternalOutput").ap()
    Kernel(nc, args, out).build()
    r = _run(nc, [arrays], core_ids=[0])
    return r.results[0]["out_0_dram"]
```
